# Optimizing a Trainium2 kernel written in Bass

```python
import numpy as np
import jax
import jax.numpy as jnp

def _softmax(x, axis=-1):
    return jax.nn.softmax(x, axis=axis)

def _gelu(x):
    return jax.nn.gelu(x, approximate=True)

def _silu(x):
    return jax.nn.silu(x)

def _sigmoid(x):
    return jax.nn.sigmoid(x)

def _layernorm(x, axis=-1, eps=1e-05):
    m = jnp.mean(x, axis=axis, keepdims=True)
    v = jnp.var(x, axis=axis, keepdims=True)
    return (x - m) / jnp.sqrt(v + eps)

def _scatter_add(tgt, idx, src, axis=0):
    return tgt.at[idx].add(src)

def _segment_sum(src, seg, n):
    return jax.ops.segment_sum(src, seg, n)
kernel_name = 'mk_seq_postln_d4_jaxref_r8_7db9e2'

def setup_inputs(seed: int=0):
    np.random.seed(seed)
    _w = jnp.asarray

    def _L0_attn_setup():
        import jax, jax.numpy as jnp
        import numpy as np
        ROPE_BASE = 1250
        B, L, D, NH = (2, 256, 128, 16)
        HD = D // NH

        def apply_rope(inputs, positions, base_frequency):
            head_dim = inputs.shape[-1]
            fraction = 2 * jnp.arange(0, head_dim // 2) / head_dim
            timescale = base_frequency ** fraction
            sinusoid = positions[..., None] / timescale[None, None, :]
            sinusoid = sinusoid[..., None, :]
            sin, cos = (jnp.sin(sinusoid), jnp.cos(sinusoid))
            first, second = jnp.split(inputs, 2, axis=-1)
            out = jnp.concatenate([first * cos - second * sin, second * cos + first * sin], axis=-1)
            return out.astype(inputs.dtype)
        key = jax.random.key(seed)
        ks = jax.random.split(key, 5)
        s = 0.02
        return {'x': jax.random.normal(ks[0], (B, L, D), jnp.float32), 'wq_w': jax.random.normal(ks[1], (D, D), jnp.float32) * s, 'wq_b': jnp.zeros((D,), jnp.float32), 'wk_w': jax.random.normal(ks[2], (D, D), jnp.float32) * s, 'wk_b': jnp.zeros((D,), jnp.float32), 'wv_w': jax.random.normal(ks[3], (D, D), jnp.float32) * s, 'wv_b': jnp.zeros((D,), jnp.float32), 'wo_w': jax.random.normal(ks[4], (D, D), jnp.float32) * s, 'wo_b': jnp.zeros((D,), jnp.float32)}
    _L0_attn_in = _L0_attn_setup()

    def _L0_ffn_setup():
        import jax, jax.numpy as jnp
        import numpy as np
        B, S, D, E, K = (4, 256, 128, 8, 2)
        H = 4 * D
        key = jax.random.key(seed)
        ks = jax.random.split(key, 4)
        sc = lambda n: 1.0 / np.sqrt(n)
        return {'x': jax.random.normal(ks[0], (B, S, D), jnp.float32), 'gate_w': jax.random.normal(ks[1], (D, E), jnp.float32) * sc(D), 'gate_b': jnp.zeros((E,), jnp.float32), 'w1': jax.random.normal(ks[2], (E, D, H), jnp.float32) * sc(D), 'b1': jnp.zeros((E, H), jnp.float32), 'w2': jax.random.normal(ks[3], (E, H, D), jnp.float32) * sc(H), 'b2': jnp.zeros((E, D), jnp.float32)}
    _L0_ffn_in = _L0_ffn_setup()

    def _L1_attn_setup():
        import jax, jax.numpy as jnp
        import numpy as np
        D_MODEL = 128
        N_HEADS = 16
        HEAD_DIM = D_MODEL // N_HEADS
        KV_LATENT = 32
        LN_EPS = 1e-05

        def apply_rope(x):
            b, h, t, d = x.shape
            half = d // 2
            pos = jnp.arange(t, dtype=x.dtype)[:, None]
            inv_freq = 1.0 / 10000.0 ** (jnp.arange(half, dtype=x.dtype) / half)
            angles = pos * inv_freq[None, :]
            sin = jnp.sin(angles)[None, None]
            cos = jnp.cos(angles)[None, None]
            x1, x2 = (x[..., :half], x[..., half:])
            return jnp.concatenate([x1 * cos - x2 * sin, x1 * sin + x2 * cos], axis=-1)
        key = jax.random.key(seed)
        ks = jax.random.split(key, 6)
        d, L = (D_MODEL, KV_LATENT)
        s = 1.0 / np.sqrt(d)
        sl = 1.0 / np.sqrt(L)
        return {'x': jax.random.normal(ks[0], (2, 256, d), dtype=jnp.float32), 'W_q': jax.random.uniform(ks[1], (d, d), jnp.float32, -s, s), 'W_dkv': jax.random.uniform(ks[2], (d, L), jnp.float32, -s, s), 'W_uk': jax.random.uniform(ks[3], (L, d), jnp.float32, -sl, sl), 'W_uv': jax.random.uniform(ks[4], (L, d), jnp.float32, -sl, sl), 'W_o': jax.random.uniform(ks[5], (d, d), jnp.float32, -s, s), 'ln_gamma': jnp.ones((L,), jnp.float32), 'ln_beta': jnp.zeros((L,), jnp.float32)}
    _L1_attn_in = _L1_attn_setup()

    def _L1_ffn_setup():
        import jax, jax.numpy as jnp
        import numpy as np
        DIM = 128

        def _reference_tuple_inner(x, W_r, W_k, W_v, mu_r, mu_k):
            B, T, C = x.shape
            x_prev = jnp.concatenate([jnp.zeros((B, 1, C), x.dtype), x[:, :-1, :]], axis=1)
            xr = mu_r * x + (1.0 - mu_r) * x_prev
            xk = mu_k * x + (1.0 - mu_k) * x_prev
            r = jax.nn.sigmoid(jnp.einsum('btc,dc->btd', xr, W_r))
            k = jnp.einsum('btc,dc->btd', xk, W_k)
            k_act = jnp.square(jax.nn.relu(k))
            out = r * jnp.einsum('btc,dc->btd', k_act, W_v)
            new_state = x[:, -1, :]
            return (out, new_state)
        key = jax.random.key(seed)
        ks = jax.random.split(key, 6)
        B, T, C = (8, 256, DIM)
        x = jax.random.normal(ks[0], (B, T, C), dtype=jnp.float32)
        s = 1.0 / np.sqrt(C)
        W_r = jax.random.uniform(ks[1], (C, C), jnp.float32, -s, s)
        W_k = jax.random.uniform(ks[2], (C, C), jnp.float32, -s, s)
        W_v = jax.random.uniform(ks[3], (C, C), jnp.float32, -s, s)
        mu_r = jax.random.uniform(ks[4], (C,), jnp.float32)
        mu_k = jax.random.uniform(ks[5], (C,), jnp.float32)
        return {'x': x, 'W_r': W_r, 'W_k': W_k, 'W_v': W_v, 'mu_r': mu_r, 'mu_k': mu_k}
    _L1_ffn_in = _L1_ffn_setup()

    def _L2_attn_setup():
        import jax, jax.numpy as jnp
        import numpy as np
        DIM = 128
        N_HEADS = 16
        HEAD_DIM = DIM // N_HEADS
        SCALE = HEAD_DIM ** (-0.5)
        key = jax.random.key(seed)
        kx, kq, kk, kv = jax.random.split(key, 4)
        x = jax.random.normal(kx, (2, 256, DIM), dtype=jnp.float32)
        bv_q = jax.random.normal(kq, (N_HEADS, HEAD_DIM), dtype=jnp.float32) * 0.02
        bv_k = jax.random.normal(kk, (N_HEADS, HEAD_DIM), dtype=jnp.float32) * 0.02
        bv_v = jax.random.normal(kv, (N_HEADS, HEAD_DIM), dtype=jnp.float32) * 0.02
        return {'x': x, 'bv_q': bv_q, 'bv_k': bv_k, 'bv_v': bv_v}
    _L2_attn_in = _L2_attn_setup()

    def _L2_ffn_setup():
        import jax, jax.numpy as jnp
        import numpy as np
        E = 8
        D = 128
        H = 256
        TOP_K = 2
        key = jax.random.key(seed)
        k_x, k_g, k_w1, k_w2 = jax.random.split(key, 4)
        B, S = (4, 256)
        inp = {'input': jax.random.normal(k_x, (B, S, D), dtype=jnp.float32), 'Wg': jax.random.normal(k_g, (D, E), dtype=jnp.float32) * 0.02, 'W1': jax.random.normal(k_w1, (E, D, H), dtype=jnp.float32) * 0.02, 'b1': jnp.zeros((E, H), dtype=jnp.float32), 'W2': jax.random.normal(k_w2, (E, H, D), dtype=jnp.float32) * 0.02, 'b2': jnp.zeros((E, D), dtype=jnp.float32)}
        return inp
    _L2_ffn_in = _L2_ffn_setup()

    def _L3_attn_setup():
        import jax, jax.numpy as jnp
        import numpy as np
        B, N, D, H = (2, 256, 128, 8)
        DH = D // H
        key = jax.random.key(seed)
        k0, k1, k2 = jax.random.split(key, 3)
        s = 1.0 / np.sqrt(D).astype(np.float32)
        return {'x': jax.random.normal(k0, (B, N, D), dtype=jnp.float32), 'w_qkv': jax.random.normal(k1, (3 * D, D), dtype=jnp.float32) * s, 'b_qkv': jnp.zeros((3 * D,), dtype=jnp.float32), 'w_o': jax.random.normal(k2, (D, D), dtype=jnp.float32) * s, 'b_o': jnp.zeros((D,), dtype=jnp.float32)}
    _L3_attn_in = _L3_attn_setup()

    def _L3_ffn_setup():
        import jax, jax.numpy as jnp
        import numpy as np
        HIDDEN = 128
        INTER = 512
        key = jax.random.key(seed)
        k1, k2, k3, k4, k5 = jax.random.split(key, 5)
        hidden_states = jax.random.normal(k1, (4, 256, HIDDEN), dtype=jnp.float32)
        W1 = jax.random.normal(k2, (HIDDEN, INTER), dtype=jnp.float32) * (1.0 / np.sqrt(HIDDEN))
        b1 = jax.random.normal(k3, (INTER,), dtype=jnp.float32) * 0.02
        W2 = jax.random.normal(k4, (INTER, HIDDEN), dtype=jnp.float32) * (1.0 / np.sqrt(INTER))
        b2 = jax.random.normal(k5, (HIDDEN,), dtype=jnp.float32) * 0.02
        return {'hidden_states': hidden_states, 'W1': W1, 'b1': b1, 'W2': W2, 'b2': b2}
    _L3_ffn_in = _L3_ffn_setup()
    _d = {'L0_attn_x': _L0_attn_in['x'], 'L0_attn_wq_w': _L0_attn_in['wq_w'], 'L0_attn_wq_b': _L0_attn_in['wq_b'], 'L0_attn_wk_w': _L0_attn_in['wk_w'], 'L0_attn_wk_b': _L0_attn_in['wk_b'], 'L0_attn_wv_w': _L0_attn_in['wv_w'], 'L0_attn_wv_b': _L0_attn_in['wv_b'], 'L0_attn_wo_w': _L0_attn_in['wo_w'], 'L0_attn_wo_b': _L0_attn_in['wo_b'], 'L0_ffn_gate_w': _L0_ffn_in['gate_w'], 'L0_ffn_gate_b': _L0_ffn_in['gate_b'], 'L0_ffn_w1': _L0_ffn_in['w1'], 'L0_ffn_b1': _L0_ffn_in['b1'], 'L0_ffn_w2': _L0_ffn_in['w2'], 'L0_ffn_b2': _L0_ffn_in['b2'], 'L1_attn_W_q': _L1_attn_in['W_q'], 'L1_attn_W_dkv': _L1_attn_in['W_dkv'], 'L1_attn_W_uk': _L1_attn_in['W_uk'], 'L1_attn_W_uv': _L1_attn_in['W_uv'], 'L1_attn_W_o': _L1_attn_in['W_o'], 'L1_attn_ln_gamma': _L1_attn_in['ln_gamma'], 'L1_attn_ln_beta': _L1_attn_in['ln_beta'], 'L1_ffn_W_r': _L1_ffn_in['W_r'], 'L1_ffn_W_k': _L1_ffn_in['W_k'], 'L1_ffn_W_v': _L1_ffn_in['W_v'], 'L1_ffn_mu_r': _L1_ffn_in['mu_r'], 'L1_ffn_mu_k': _L1_ffn_in['mu_k'], 'L2_attn_bv_q': _L2_attn_in['bv_q'], 'L2_attn_bv_k': _L2_attn_in['bv_k'], 'L2_attn_bv_v': _L2_attn_in['bv_v'], 'L2_ffn_Wg': _L2_ffn_in['Wg'], 'L2_ffn_W1': _L2_ffn_in['W1'], 'L2_ffn_b1': _L2_ffn_in['b1'], 'L2_ffn_W2': _L2_ffn_in['W2'], 'L2_ffn_b2': _L2_ffn_in['b2'], 'L3_attn_w_qkv': _L3_attn_in['w_qkv'], 'L3_attn_b_qkv': _L3_attn_in['b_qkv'], 'L3_attn_w_o': _L3_attn_in['w_o'], 'L3_attn_b_o': _L3_attn_in['b_o'], 'L3_ffn_W1': _L3_ffn_in['W1'], 'L3_ffn_b1': _L3_ffn_in['b1'], 'L3_ffn_W2': _L3_ffn_in['W2'], 'L3_ffn_b2': _L3_ffn_in['b2']}
    _x0 = _d['L0_attn_x']
    _d['L0_attn_x'] = jax.random.normal(jax.random.fold_in(jax.random.key(seed), 1), (16, 256, 128), dtype=_x0.dtype)
    del _x0
    return _d

def reference(L0_attn_x, L0_attn_wq_w, L0_attn_wq_b, L0_attn_wk_w, L0_attn_wk_b, L0_attn_wv_w, L0_attn_wv_b, L0_attn_wo_w, L0_attn_wo_b, L0_ffn_gate_w, L0_ffn_gate_b, L0_ffn_w1, L0_ffn_b1, L0_ffn_w2, L0_ffn_b2, L1_attn_W_q, L1_attn_W_dkv, L1_attn_W_uk, L1_attn_W_uv, L1_attn_W_o, L1_attn_ln_gamma, L1_attn_ln_beta, L1_ffn_W_r, L1_ffn_W_k, L1_ffn_W_v, L1_ffn_mu_r, L1_ffn_mu_k, L2_attn_bv_q, L2_attn_bv_k, L2_attn_bv_v, L2_ffn_Wg, L2_ffn_W1, L2_ffn_b1, L2_ffn_W2, L2_ffn_b2, L3_attn_w_qkv, L3_attn_b_qkv, L3_attn_w_o, L3_attn_b_o, L3_ffn_W1, L3_ffn_b1, L3_ffn_W2, L3_ffn_b2):

    def _L0_attn_ref(x, wq_w, wq_b, wk_w, wk_b, wv_w, wv_b, wo_w, wo_b):
        import jax, jax.numpy as jnp
        import numpy as np
        ROPE_BASE = 1250
        B, L, D, NH = (2, 256, 128, 16)
        HD = D // NH

        def apply_rope(inputs, positions, base_frequency):
            head_dim = inputs.shape[-1]
            fraction = 2 * jnp.arange(0, head_dim // 2) / head_dim
            timescale = base_frequency ** fraction
            sinusoid = positions[..., None] / timescale[None, None, :]
            sinusoid = sinusoid[..., None, :]
            sin, cos = (jnp.sin(sinusoid), jnp.cos(sinusoid))
            first, second = jnp.split(inputs, 2, axis=-1)
            out = jnp.concatenate([first * cos - second * sin, second * cos + first * sin], axis=-1)
            return out.astype(inputs.dtype)
        b, l, _ = x.shape
        q = (x @ wq_w + wq_b).reshape(b, l, NH, HD)
        k = (x @ wk_w + wk_b).reshape(b, l, NH, HD)
        v = (x @ wv_w + wv_b).reshape(b, l, NH, HD)
        pos = jnp.arange(l)
        q = apply_rope(q, pos, ROPE_BASE)
        k = apply_rope(k, pos, ROPE_BASE)
        q = q.transpose(0, 2, 1, 3)
        k = k.transpose(0, 2, 1, 3)
        v = v.transpose(0, 2, 1, 3)
        scale = jnp.sqrt(jnp.asarray(HD, q.dtype))
        scores = jnp.einsum('bnqh,bnkh->bnqk', q, k) / scale
        causal = jnp.tril(jnp.ones((l, l), bool))
        scores = jnp.where(causal, scores, jnp.finfo(scores.dtype).min)
        attn = jax.nn.softmax(scores, axis=-1)
        ctx = jnp.einsum('bnqk,bnkh->bnqh', attn, v)
        ctx = ctx.transpose(0, 2, 1, 3).reshape(b, l, D)
        return ctx @ wo_w + wo_b

    def _L0_ffn_ref(x, gate_w, gate_b, w1, b1, w2, b2):
        import jax, jax.numpy as jnp
        import numpy as np
        B, S, D, E, K = (4, 256, 128, 8, 2)
        H = 4 * D
        Bx, Sx, Dx = x.shape
        n_exp = w1.shape[0]
        logits = jnp.einsum('bsd,de->bse', x, gate_w) + gate_b
        scores = jax.nn.softmax(logits, axis=-1)
        topk_s, topk_i = jax.lax.top_k(scores, K)
        onehot = jax.nn.one_hot(topk_i, n_exp, dtype=scores.dtype)
        dispatch = jnp.einsum('bske,bsk->bse', onehot, topk_s)
        xf = x.reshape(-1, Dx)
        wf = dispatch.reshape(-1, n_exp)
        out = jnp.zeros_like(xf)
        for i in range(n_exp):
            wi = wf[:, i:i + 1]
            h = jax.nn.relu(xf * wi @ w1[i] + b1[i])
            y = h @ w2[i] + b2[i]
            out = jnp.where(wi > 0, y, out)
        return out.reshape(Bx, Sx, Dx)

    def _L1_attn_ref(x, W_q, W_dkv, W_uk, W_uv, W_o, ln_gamma, ln_beta):
        import jax, jax.numpy as jnp
        import numpy as np
        D_MODEL = 128
        N_HEADS = 16
        HEAD_DIM = D_MODEL // N_HEADS
        KV_LATENT = 32
        LN_EPS = 1e-05

        def apply_rope(x):
            b, h, t, d = x.shape
            half = d // 2
            pos = jnp.arange(t, dtype=x.dtype)[:, None]
            inv_freq = 1.0 / 10000.0 ** (jnp.arange(half, dtype=x.dtype) / half)
            angles = pos * inv_freq[None, :]
            sin = jnp.sin(angles)[None, None]
            cos = jnp.cos(angles)[None, None]
            x1, x2 = (x[..., :half], x[..., half:])
            return jnp.concatenate([x1 * cos - x2 * sin, x1 * sin + x2 * cos], axis=-1)
        b, t, _ = x.shape
        q = (x @ W_q).reshape(b, t, N_HEADS, HEAD_DIM).transpose(0, 2, 1, 3)
        lat = x @ W_dkv
        mu = jnp.mean(lat, axis=-1, keepdims=True)
        var = jnp.mean(jnp.square(lat - mu), axis=-1, keepdims=True)
        lat = (lat - mu) * jax.lax.rsqrt(var + LN_EPS) * ln_gamma + ln_beta
        k = (lat @ W_uk).reshape(b, t, N_HEADS, HEAD_DIM).transpose(0, 2, 1, 3)
        v = (lat @ W_uv).reshape(b, t, N_HEADS, HEAD_DIM).transpose(0, 2, 1, 3)
        q = apply_rope(q)
        k = apply_rope(k)
        scores = jnp.einsum('bhqd,bhkd->bhqk', q, k) / jnp.sqrt(jnp.float32(HEAD_DIM))
        causal = jnp.tril(jnp.ones((t, t), dtype=bool))
        scores = jnp.where(causal[None, None], scores, -jnp.inf)
        attn = jax.nn.softmax(scores, axis=-1)
        out = jnp.einsum('bhqk,bhkd->bhqd', attn, v)
        out = out.transpose(0, 2, 1, 3).reshape(b, t, D_MODEL)
        return out @ W_o

    def _L1_ffn_ref(x, W_r, W_k, W_v, mu_r, mu_k):
        import jax, jax.numpy as jnp
        import numpy as np
        DIM = 128

        def _reference_tuple_inner(x, W_r, W_k, W_v, mu_r, mu_k):
            B, T, C = x.shape
            x_prev = jnp.concatenate([jnp.zeros((B, 1, C), x.dtype), x[:, :-1, :]], axis=1)
            xr = mu_r * x + (1.0 - mu_r) * x_prev
            xk = mu_k * x + (1.0 - mu_k) * x_prev
            r = jax.nn.sigmoid(jnp.einsum('btc,dc->btd', xr, W_r))
            k = jnp.einsum('btc,dc->btd', xk, W_k)
            k_act = jnp.square(jax.nn.relu(k))
            out = r * jnp.einsum('btc,dc->btd', k_act, W_v)
            new_state = x[:, -1, :]
            return (out, new_state)
        return _reference_tuple_inner(x, W_r, W_k, W_v, mu_r, mu_k)[0]

    def _L2_attn_ref(x, bv_q, bv_k, bv_v):
        import jax, jax.numpy as jnp
        import numpy as np
        DIM = 128
        N_HEADS = 16
        HEAD_DIM = DIM // N_HEADS
        SCALE = HEAD_DIM ** (-0.5)
        B, T, D = x.shape
        H, HD = (N_HEADS, HEAD_DIM)
        x_h = x.reshape(B, T, H, HD)
        Q = x_h * jnp.sign(bv_q)
        K = x_h * jnp.sign(bv_k)
        V = x_h * jnp.sign(bv_v)
        scores = jnp.einsum('bqhd,bkhd->bhqk', Q, K) * SCALE
        causal = jnp.tril(jnp.ones((T, T), dtype=bool))
        attn = jnp.where(causal, jax.nn.sigmoid(scores * 4.0), 0.0)
        out = jnp.einsum('bhqk,bkhd->bqhd', attn, V)
        return out.reshape(B, T, D)

    def _L2_ffn_ref(input, Wg, W1, b1, W2, b2):
        import jax, jax.numpy as jnp
        import numpy as np
        E = 8
        D = 128
        H = 256
        TOP_K = 2
        logits = jnp.einsum('bsd,de->bse', input, Wg)
        probs = jax.nn.softmax(logits, axis=-1)
        top_vals, top_idx = jax.lax.top_k(probs, TOP_K)
        top_vals = top_vals / jnp.sum(top_vals, axis=-1, keepdims=True)
        onehot = jax.nn.one_hot(top_idx, E, dtype=input.dtype)
        mask = jnp.sum(onehot, axis=2)
        scores = jnp.sum(onehot * top_vals[..., None], axis=2)
        xm = input[None] * jnp.moveaxis(mask, -1, 0)[..., None]
        h = jnp.einsum('ebsd,edh->ebsh', xm, W1) + b1[:, None, None, :]
        h = jax.nn.relu(h)
        y = jnp.einsum('ebsh,ehd->ebsd', h, W2) + b2[:, None, None, :]
        out = jnp.sum(y * jnp.moveaxis(scores, -1, 0)[..., None], axis=0)
        return out

    def _L3_attn_ref(x, w_qkv, b_qkv, w_o, b_o):
        import jax, jax.numpy as jnp
        import numpy as np
        B, N, D, H = (2, 256, 128, 8)
        DH = D // H
        b, n, d = x.shape
        h = H
        dh = d // h
        qkv = x @ w_qkv.T + b_qkv
        qkv = qkv.reshape(b, n, 3, dh, h)
        qkv = jnp.transpose(qkv, (2, 0, 4, 1, 3))
        q, k, v = (qkv[0], qkv[1], qkv[2])
        attn = jnp.einsum('bhik,bhjk->bhij', q, k)
        out = jnp.einsum('bhik,bhkj->bhij', attn, v)
        out = jnp.transpose(out, (0, 2, 1, 3)).reshape(b, n, d)
        return out @ w_o.T + b_o

    def _L3_ffn_ref(hidden_states, W1, b1, W2, b2):
        import jax, jax.numpy as jnp
        import numpy as np
        HIDDEN = 128
        INTER = 512
        h = jax.nn.relu(jnp.einsum('bsh,hi->bsi', hidden_states, W1) + b1)
        return jnp.einsum('bsi,ih->bsh', h, W2) + b2
    x = L0_attn_x
    x = _layernorm(x + _L0_attn_ref(x, L0_attn_wq_w, L0_attn_wq_b, L0_attn_wk_w, L0_attn_wk_b, L0_attn_wv_w, L0_attn_wv_b, L0_attn_wo_w, L0_attn_wo_b), axis=-1)
    x = _layernorm(x + _L0_ffn_ref(x, L0_ffn_gate_w, L0_ffn_gate_b, L0_ffn_w1, L0_ffn_b1, L0_ffn_w2, L0_ffn_b2), axis=-1)
    x = _layernorm(x + _L1_attn_ref(x, L1_attn_W_q, L1_attn_W_dkv, L1_attn_W_uk, L1_attn_W_uv, L1_attn_W_o, L1_attn_ln_gamma, L1_attn_ln_beta), axis=-1)
    x = _layernorm(x + _L1_ffn_ref(x, L1_ffn_W_r, L1_ffn_W_k, L1_ffn_W_v, L1_ffn_mu_r, L1_ffn_mu_k), axis=-1)
    x = _layernorm(x + _L2_attn_ref(x, L2_attn_bv_q, L2_attn_bv_k, L2_attn_bv_v), axis=-1)
    x = _layernorm(x + _L2_ffn_ref(x, L2_ffn_Wg, L2_ffn_W1, L2_ffn_b1, L2_ffn_W2, L2_ffn_b2), axis=-1)
    x = _layernorm(x + _L3_attn_ref(x, L3_attn_w_qkv, L3_attn_b_qkv, L3_attn_w_o, L3_attn_b_o), axis=-1)
    x = _layernorm(x + _L3_ffn_ref(x, L3_ffn_W1, L3_ffn_b1, L3_ffn_W2, L3_ffn_b2), axis=-1)
    return x

_drawn_inputs = setup_inputs


def setup_inputs(seed=0):
    import zlib

    import numpy as np

    out = dict(_drawn_inputs(seed))
    spreads = {'L0_attn_wq_b': (0.0, 0.8),
     'L0_attn_wk_b': (0.0, 0.8),
     'L0_attn_wv_b': (0.0, 0.1),
     'L0_attn_wo_b': (0.0, 0.1),
     'L0_ffn_gate_b': (0.0, 0.1),
     'L0_ffn_b1': (0.0, 0.1),
     'L0_ffn_b2': (0.0, 0.1),
     'L1_attn_ln_gamma': (1.0, 0.2),
     'L1_attn_ln_beta': (0.0, 0.1),
     'L2_ffn_b1': (0.0, 0.297),
     'L2_ffn_b2': (0.0, 0.1),
     'L3_attn_b_qkv': (0.0, 0.1),
     'L3_attn_b_o': (0.0, 0.8)}
    factors = {'L0_attn_wq_w': 8.0,
     'L0_attn_wk_w': 8.0,
     'L1_ffn_mu_r': 3.921,
     'L3_ffn_b1': 4.998,
     'L3_ffn_b2': 3.364}
    for name, (base, spread) in spreads.items():
        noise = np.random.default_rng([zlib.crc32(name.encode()), seed]).standard_normal(out[name].shape)
        drawn = base * np.exp(spread * noise) if base else spread * noise
        out[name] = jnp.asarray(drawn.astype(out[name].dtype))
    for name, factor in factors.items():
        out[name] = (out[name] * factor).astype(out[name].dtype)
    return out
```

```python
from contextlib import ExitStack

import numpy as np

import concourse.bass as bass
from concourse import mybir

F32 = mybir.dt.float32
F32R = mybir.dt.float32r
BF16 = mybir.dt.bfloat16
ALU = mybir.AluOpType
ACT = mybir.ActivationFunctionType
AX = mybir.AxisListType

P = 128
B = 16
T = 2
L = T * P
NH = 16
HD = P // NH
G = 4
ROWS = P // G
MAX_HI = 3 * HD
MAX_LO = MAX_HI + 1
LAT = 32
NE = 8
EPS = 1e-5
MASKED = -1e30


class Event:

    def __init__(self, sem, per, base):
        self.sem, self.per, self.base = sem, per, base

    def at(self, seq, n=None):
        return seq * self.per + (self.base + (self.per if n is None else n))


def begun(seq):
    return not (isinstance(seq, int) and seq < 0)


def held(eng, count):
    return count if isinstance(count, int) else eng.to_reg(count)


def pipeline(eng, front, step, tail):
    front(0, 0)
    step(0, 0, None, front)
    step(1, 1, tail, front)
    step(2, 0, tail, front)
    with eng.Fori(1, (B - 2) // 2) as i:
        step(2 * i + 1, 1, tail, front)
        step(2 * i + 2, 0, tail, front)
    step(B - 1, 1, tail, None)
    tail(B - 1, 1)


class Core:

    def __init__(self, nc, ctx):
        self.nc, self.ctx = nc, ctx
        self.signals = {}
        sb = self.sb
        self.made = self.sem("constants_made")
        self.X = sb("X", [P, B, T, P])
        self.ident = sb("ident", [P, P])
        self.ident_r = sb("ident_r", [P, P], F32R)
        self.ident_b = sb("ident_b", [P, P], BF16)
        self.mask_f = sb("mask_f", [P, 2, P])
        self.mask_q = sb("mask_q", [P, P], BF16)
        self.mask_k = sb("mask_k", [P, P], BF16)
        self.ones = sb("ones", [P, P])
        self.eps = sb("eps", [P, T])
        self.minus_half = sb("minus_half", [P, T])
        self.spread = sb("spread", [P, 4, G, P], F32R)
        self.one_rows = sb("one_rows", [P, 1])
        self.A = ctx.enter_context(nc.psum_tensor("A", [P, 2, 512], F32))
        self.S = ctx.enter_context(nc.psum_tensor("S", [P, 2, 2, 512], F32))
        self.O = ctx.enter_context(nc.psum_tensor("O", [P, 2, 512], F32))
        self.xin = sb("xin", [P, 2, T, P])
        self.xT = sb("xT", [P, L])
        self.xres = sb("xres", [P, T, P])
        self.res = sb("res", [P, T, P])
        self.stats = sb("stats", [P, T, 6])
        self.mv = sb("mv", [P, T, 2])
        self.ve = sb("ve", [P, T])
        self.rstd = sb("rstd", [P, T])
        self.trig = sb("trig", [P, 2, 2, L])
        self.t12 = sb("t12", [P, 2, 2, L])
        self.rot = sb("rot", [P, 2, L])
        self.hi = sb("hi", [P, 2, L], F32R)
        self.lo = sb("lo", [P, 2, L], F32R)
        self.QS = sb("QS", [P, 2, G, L], F32R)
        self.KS = sb("KS", [P, 2, G, L], F32R)
        self.QM = sb("QM", [P, G, L], F32R)
        self.V = sb("V", [P, 2, T, NH, ROWS])
        self.nm = sb("nm", [P, T, G, G])
        self.M = sb("M", [P, T, G, P], F32R)
        self.probs = sb("probs", [P, 6, 2, G, P])
        self.OT = sb("OT", [P, G, L])
        self.rinv = sb("rinv", [P, T, G, G])
        self.ctx_sb = sb("ctx_sb", [P, T, P])
        self.ctxT = sb("ctxT", [P, L])

    def sb(self, name, shape, dt=F32):
        return self.ctx.enter_context(self.nc.sbuf_tensor(name, shape, dt))

    def sem(self, name):
        return self.ctx.enter_context(self.nc.semaphore(name))

    def events(self, **per):
        for k in per:
            if k not in self.signals:
                self.signals[k] = [self.sem(k), 0]
        out = {k: Event(*[self.signals[k][0], v, self.signals[k][1]]) for k, v in per.items()}
        for k, v in per.items():
            self.signals[k][1] += v * B
        return out



LN_EVENTS = dict(res=1, bn=2, mv=2, ve=1, rstd=1, x=2)


def norm_stats(c, e, dve, s):
    for t in range(T):
        if t == 0:
            dve.wait_ge(e["res"].sem, e["res"].at(s))
        dve.bn_stats(c.stats[:, t, :], c.res[:, t, :]).then_inc(e["bn"].sem, 1)
    for t in range(T):
        count = held(dve, e["bn"].at(s, t + 1))
        dve.wait_ge(c.made, 1)
        dve.wait_ge(e["bn"].sem, count)
        dve.bn_aggr(c.mv[:, t, :], c.stats[:, t, :]).then_inc(e["mv"].sem, 1)


def norm_rstd(c, e, pool, s):
    count = held(pool, e["mv"].at(s))
    pool.wait_ge(c.made, 1)
    pool.wait_ge(e["mv"].sem, count)
    pool.tensor_tensor(c.ve[:], c.mv[:, :, 1], c.eps[:], ALU.add).then_inc(e["ve"].sem, 1)
    count = held(pool, e["ve"].at(s))
    pool.wait_ge(c.made, 1)
    pool.wait_ge(e["ve"].sem, count)
    pool.tensor_tensor(c.rstd[:], c.ve[:], c.minus_half[:], ALU.pow).then_inc(e["rstd"].sem, 1)


def norm_write(c, e, dve, s):
    dve.wait_ge(e["rstd"].sem, e["rstd"].at(s))
    for t in range(T):
        dve.tensor_scalar(c.X[:, s, t, :], c.res[:, t, :], c.mv[:, t, 0:1], c.rstd[:, t:t + 1],
                          ALU.subtract, ALU.mult).then_inc(e["x"].sem, 1)


class Attention:

    def __init__(self, c, name, kind, layer, w):
        self.c, self.kind, self.layer, self.w = c, kind, layer, w
        ev = dict(xin=1, xt_ps=1, xt=1, v_ps=1, v=T, hi=1, lo=1, qst_ps=1, qs=1, kst_ps=1, ks=1,
                  p2=6, probs=6, pv=2, ot=2, ctx_ps=1, ctx=2, out_ps=1, xres=1, **LN_EVENTS)
        if kind == "sigmoid":
            ev.update(rot=2, add=1)
        else:
            ev.update(proj_ps=2, t12=4, rot=1, p1=6, rmax=6, mhi=1, m=1, mx_ps=2, qm=2,
                      rinv=2, ctxt_ps=1, ctxt=1)
        if kind == "latent":
            ev.update(lat_ps=1, lbn=T, lmv=T, lve=1, lrstd=1, lnorm=T, lscale=T, lat=T, latt_ps=1, latt=1)
        self.e = c.events(**ev)
        self.scale = HD ** -0.5 if kind != "sigmoid" else 2 * HD ** -0.5

    def pool(self, pool):
        c, e, w = self.c, self.e, self.w

        def front(s, par):
            if begun(s - 2):
                count = held(pool, e["xt_ps"].at(s - 2))
                pool.wait_ge(c.made, 1)
                pool.wait_ge(e["xt_ps"].sem, count)
            if self.kind == "sigmoid":
                if begun(s - 2):
                    count = held(pool, e["v"].at(s - 2))
                    pool.wait_ge(c.made, 1)
                    pool.wait_ge(e["v"].sem, count)
            pool.tensor_copy(c.xin[:, par], c.X[:, s]).then_inc(e["xin"].sem, 1)

        def tail(s, par):
            if begun(s - 1):
                count = held(pool, e["res"].at(s - 1))
                pool.wait_ge(c.made, 1)
                pool.wait_ge(e["res"].sem, count)
            if self.kind == "rope":
                pool.tensor_tensor(c.xres[:], c.X[:, s], w["bo"][:].unsqueeze(1).broadcast_to((P, T, P)), ALU.add).then_inc(e["xres"].sem, 1)
            else:
                pool.tensor_copy(c.xres[:], c.X[:, s]).then_inc(e["xres"].sem, 1)
            norm_rstd(c, e, pool, s)

        def latent(s):
            count = held(pool, e["lmv"].at(s))
            pool.wait_ge(c.made, 1)
            pool.wait_ge(e["lmv"].sem, count)
            pool.tensor_tensor(w["lve"][:], w["lmv"][:, :, 1], c.eps[:], ALU.add).then_inc(e["lve"].sem, 1)
            count = held(pool, e["lve"].at(s))
            pool.wait_ge(c.made, 1)
            pool.wait_ge(e["lve"].sem, count)
            pool.tensor_tensor(w["lrstd"][:], w["lve"][:], c.minus_half[:], ALU.pow).then_inc(e["lrstd"].sem, 1)

        def first(s, par):
            front(s, par)
            if self.kind == "latent":
                latent(s)

        def step(k, par, has_tail, has_front):
            if has_front:
                front(k + 1, 1 - par)
                if self.kind == "latent":
                    latent(k + 1)
            if has_tail:
                tail(k - 1, 1 - par)

        pipeline(pool, first, step, tail)

    def pe(self, pe):
        c, e, w, kind = self.c, self.e, self.w, self.kind
        soft = kind != "sigmoid"

        def x_transposes(s, par):
            pe.wait_ge(e["xin"].sem, e["xin"].at(s))
            if soft:
                if begun(s - 1):
                    pe.wait_ge(e["ks"].sem, e["ks"].at(s - 1))
            else:
                if begun(s - 2):
                    pe.wait_ge(e["ctx"].sem, e["ctx"].at(s - 2))
            for t in range(T):
                mm = pe.transpose(c.A[:, 0, t * P:(t + 1) * P], c.xin[:, par, t, :], c.ident[:])
            mm.then_inc(e["xt_ps"].sem, 1)

        def latent(s, par):
            pe.wait_ge(e["xt"].sem, e["xt"].at(s))
            if begun(s - 2):
                pe.wait_ge(e["ot"].sem, e["ot"].at(s - 2, 1))
            for t in range(T):
                mm = pe.matmul(c.O[:, 0, t * LAT:(t + 1) * LAT], c.xT[:, t * P:(t + 1) * P], w["dkv"][:],
                               start=True, stop=True)
            mm.then_inc(e["lat_ps"].sem, 1)

        def latent_T(s, par):
            pe.wait_ge(e["lat"].sem, e["lat"].at(s))
            for t in range(T):
                mm = pe.transpose(c.O[0:LAT, 0, t * P:(t + 1) * P], w["lat"][:, t, :], c.ident[:])
            mm.then_inc(e["latt_ps"].sem, 1)

        def values(s, par):
            pe.wait_ge(e["xt"].sem, e["xt"].at(s))
            if begun(s - 2):
                pe.wait_ge(e["ctx"].sem, e["ctx"].at(s - 2))
            if kind == "latent":
                pe.wait_ge(e["latt"].sem, e["latt"].at(s))
            source, weight = (w["latT"], w["uv"]) if kind == "latent" else (c.xT, w["wv"])
            for t in range(T):
                mm = pe.matmul(c.A[:, 1, t * P:(t + 1) * P], source[:, t * P:(t + 1) * P], weight[:],
                               start=True, stop=True)
            mm.then_inc(e["v_ps"].sem, 1)

        def projections(s, sw, sides=(0, 1)):
            if sw:
                pe.wait_ge(e["v"].sem, e["v"].at(s))
            else:
                pe.wait_ge(e["xt"].sem, e["xt"].at(s))
                if begun(s - 2):
                    pe.wait_ge(e["ctxt"].sem, e["ctxt"].at(s - 2))
            for j in sides:
                src = w["latT"] if (kind == "latent" and j == 1) else c.xT
                mm = pe.matmul(c.A[:, sw, j * L:(j + 1) * L], w["wqk"][j][:, sw, :], src[:], start=True, stop=True)
            if 1 in sides:
                mm.then_inc(e["proj_ps"].sem, 1)

        def stack(s, j):
            if j == 0:
                pe.wait_ge(e["hi"].sem, e["hi"].at(s))
                pe.wait_ge(e["lo"].sem, e["lo"].at(s))
                if soft:
                    pe.wait_ge(e["t12"].sem, e["t12"].at(s))
                else:
                    pe.wait_ge(e["xt"].sem, e["xt"].at(s))
                    if begun(s - 2):
                        pe.wait_ge(e["res"].sem, e["res"].at(s - 2))
            else:
                pe.wait_ge(e["qs"].sem, e["qs"].at(s))
            for g in range(G):
                out = c.A[:, g // 2, (g % 2) * L:(g % 2 + 1) * L]
                pe.matmul(out, c.spread[:, 2 * j, g, :], c.hi[:, j, :], start=True, stop=False)
                mm = pe.matmul(out, c.spread[:, 2 * j + 1, g, :], c.lo[:, j, :], start=False, stop=True)
            mm.then_inc((e["kst_ps"] if j else e["qst_ps"]).sem, 1)

        def score_slot(slot, lhs, rhs, pr, u, mask, diagonal):
            for b in range(2):
                out = slot[:, b].rearrange("p (g t k) -> p g t k", g=2, t=2)
                if u < 2:
                    pe.matmul(out[:, :, diagonal, :], c.ident_b[:], mask[:].unsqueeze(1).broadcast_to((P, 2, P)),
                              start=True, stop=False, skip_group_check=True)
                else:
                    pe.matmul(slot[:, b], c.ident_b[:], mask[:].unsqueeze(1).broadcast_to((P, G, P)),
                              start=True, stop=False, skip_group_check=True)
            width = L if u < 2 else P
            tile = diagonal if u < 2 else 1 - diagonal
            for n in range(512 // width):
                for b in range(2):
                    r = 2 * pr + b
                    rows = slice(r * ROWS, (r + 1) * ROWS)
                    g = 2 * u + n if u < 2 else n
                    right = rhs[rows, g, :] if u < 2 else rhs[rows, g, tile * P:(tile + 1) * P]
                    mm = pe.matmul(slot[:, b, n * width:(n + 1) * width], lhs[rows, g, tile * P:(tile + 1) * P], right,
                                   start=False, stop=True, skip_group_check=True)
            return mm

        def pass1(s, par, n):
            if n == 0:
                pe.wait_ge(e["qs"].sem, e["qs"].at(s))
                pe.wait_ge(e["ks"].sem, e["ks"].at(s))
            if n < 2:
                if begun(s - 1):
                    pe.wait_ge(e["probs"].sem, e["probs"].at(s - 1, 5 + n))
            else:
                pe.wait_ge(e["rmax"].sem, e["rmax"].at(s, n - 1))
            pr, u = n // 3, n % 3
            q, k = c.QS[:, par], c.KS[:, par]
            score_slot(c.S[:, n % 2], q, k, pr, u, c.mask_q, 1).then_inc(e["p1"].sem, 1)

        def maxima(s, has_front):
            pe.wait_ge(e["m"].sem, e["m"].at(s))
            if begun(s - 1):
                pe.wait_ge(e["ot"].sem, e["ot"].at(s - 1))
            if has_front and kind == "latent":
                pe.wait_ge(e["latt"].sem, e["latt"].at(s + 1))
            for g in range(G):
                for t in range(T):
                    mm = pe.matmul(c.O[:, g // 2, (g % 2) * L + t * P:(g % 2) * L + (t + 1) * P],
                                   c.M[:, t, g, :], c.ident_r[:], start=True, stop=True)
                if g % 2:
                    mm.then_inc(e["mx_ps"].sem, 1)

        def pass2(s, par, n):
            if soft and n < 2:
                pe.wait_ge(e["qm"].sem, e["qm"].at(s, n + 1))
            if n == 0:
                if not soft:
                    pe.wait_ge(e["qs"].sem, e["qs"].at(s))
                    pe.wait_ge(e["ks"].sem, e["ks"].at(s))
            if n >= 2:
                pe.wait_ge(e["probs"].sem, e["probs"].at(s, n - 1))
            elif soft:
                pe.wait_ge(e["rmax"].sem, e["rmax"].at(s, 5 + n))
            else:
                if begun(s - 1):
                    pe.wait_ge(e["probs"].sem, e["probs"].at(s - 1, 5 + n))
            pr, u = n // 3, n % 3
            q = c.QM if soft else c.QS[:, par]
            k = c.KS[:, par]
            score_slot(c.S[:, n % 2], k, q, pr, u, c.mask_k, 0).then_inc(e["p2"].sem, 1)

        def weighted(s, par, pr):
            pe.wait_ge(e["probs"].sem, e["probs"].at(s, 3 * pr + 3))
            if begun(s - 1):
                pe.wait_ge(e["ot"].sem, e["ot"].at(s - 1, pr + 1))
            if pr == 0:
                pe.wait_ge(e["v"].sem, e["v"].at(s))
                if soft:
                    pe.wait_ge(e["qm"].sem, e["qm"].at(s))
            elif soft:
                if begun(s - 1):
                    pe.wait_ge(e["res"].sem, e["res"].at(s - 1))
            for b in range(2):
                r = 2 * pr + b
                for g in range(G):
                    pe.matmul(c.O[g * ROWS:(g + 1) * ROWS, pr, b * L:(b + 1) * L],
                              c.V[:, par, 0, 4 * g + r, :], c.probs[:, 3 * pr + g // 2, b, 2 * (g % 2):2 * (g % 2) + 2, :],
                              start=True, stop=False, skip_group_check=True)
                for g in range(G):
                    mm = pe.matmul(c.O[g * ROWS:(g + 1) * ROWS, pr, b * L + P:(b + 1) * L],
                                   c.V[:, par, 1, 4 * g + r, :], c.probs[:, 3 * pr + 2, b, g, :],
                                   start=False, stop=True, skip_group_check=True)
            mm.then_inc(e["pv"].sem, 1)

        def out_transposes(s, has_front, last=False):
            pe.wait_ge(e["ot"].sem, e["ot"].at(s))
            if not last:
                pe.wait_ge(e["ks"].sem, e["ks"].at(s + 1))
                if soft and has_front:
                    pe.wait_ge(e["xt"].sem, e["xt"].at(s + 2))
            elif soft:
                pe.wait_ge(e["ctxt"].sem, e["ctxt"].at(s - 1))
            else:
                pe.wait_ge(e["res"].sem, e["res"].at(s - 1))
            for t in range(T):
                for r in range(G):
                    mm = pe.transpose(c.A[:, t, r * P:(r + 1) * P], c.OT[:, r, t * P:(t + 1) * P], c.ident[:])
            mm.then_inc(e["ctx_ps"].sem, 1)

        def ctx_transposes(s):
            pe.wait_ge(e["ctx"].sem, e["ctx"].at(s))
            for t in range(T):
                mm = pe.transpose(c.A[:, 0, t * P:(t + 1) * P], c.ctx_sb[:, t, :], c.ident[:])
            mm.then_inc(e["ctxt_ps"].sem, 1)

        def output(s, par, last=False):
            if soft:
                pe.wait_ge(e["ctxt"].sem, e["ctxt"].at(s))
                if last:
                    pe.wait_ge(e["ot"].sem, e["ot"].at(s))
                else:
                    pe.wait_ge(e["qm"].sem, e["qm"].at(s + 1))
                for t in range(T):
                    mm = pe.matmul(c.O[:, 1, t * P:(t + 1) * P], c.ctxT[:, t * P:(t + 1) * P], w["wo"][:],
                                   start=True, stop=True)
            else:
                pe.wait_ge(e["ctx"].sem, e["ctx"].at(s))
                V0, V1 = (c.V[:, par, t, :, 0:HD] for t in range(T))
                pe.matmul(c.A[:, 1, 0:P], c.ones[:], V0, start=True, stop=True)
                pe.matmul(c.A[:, 1, P:2 * P], c.ones[:], V0, start=True, stop=False)
                mm = pe.matmul(c.A[:, 1, P:2 * P], c.ones[:], V1, start=False, stop=True)
            mm.then_inc(e["out_ps"].sem, 1)

        def front(s, par):
            x_transposes(s, par)
            if kind == "latent":
                latent(s, par)
                latent_T(s, par)
            if soft:
                values(s, par)
                projections(s, 0)
                projections(s, 1)
            stack(s, 0)
            stack(s, 1)
            if soft:
                for n in range(2):
                    pass1(s, par, n)

        def tail(s, par):
            out_transposes(s, False, last=True)
            if soft:
                ctx_transposes(s)
            output(s, par, last=True)

        def soft_step(k, par, has_tail, has_front):
            nxt = 1 - par
            if has_front:
                x_transposes(k + 1, nxt)
            pass1(k, par, 2)
            if has_tail:
                out_transposes(k - 1, has_front)
            if has_front and kind == "latent":
                latent(k + 1, nxt)
            pass1(k, par, 3)
            if has_tail:
                ctx_transposes(k - 1)
            if has_front and kind == "rope":
                values(k + 1, nxt)
            pass1(k, par, 4)
            if has_front:
                projections(k + 1, 0, (0, 1) if kind == "rope" else (0,))
            pass1(k, par, 5)
            if has_front:
                if kind == "latent":
                    latent_T(k + 1, nxt)
                else:
                    projections(k + 1, 1)
            maxima(k, has_front)
            if has_front and kind == "latent":
                values(k + 1, nxt)
                projections(k + 1, 0, (1,))
            pass2(k, par, 0)
            if has_front and kind == "latent":
                projections(k + 1, 1)
            pass2(k, par, 1)
            if has_tail:
                output(k - 1, nxt)
            pass2(k, par, 2)
            pass2(k, par, 3)
            if has_front:
                stack(k + 1, 0)
            weighted(k, par, 0)
            pass2(k, par, 4)
            if has_front:
                stack(k + 1, 1)
            pass2(k, par, 5)
            if has_front:
                for n in range(2):
                    pass1(k + 1, nxt, n)
            weighted(k, par, 1)

        def sigmoid_step(k, par, has_tail, has_front):
            nxt = 1 - par
            pass2(k, par, 0)
            pass2(k, par, 1)
            if has_tail:
                out_transposes(k - 1, has_front)
            pass2(k, par, 2)
            if has_tail:
                output(k - 1, nxt)
            if has_front:
                x_transposes(k + 1, nxt)
            pass2(k, par, 3)
            weighted(k, par, 0)
            pass2(k, par, 4)
            if has_front:
                stack(k + 1, 0)
            pass2(k, par, 5)
            if has_front:
                stack(k + 1, 1)
            weighted(k, par, 1)

        pipeline(pe, front, soft_step if soft else sigmoid_step, tail)

    def act(self, act):
        c, e, w, kind = self.c, self.e, self.w, self.kind
        soft = kind != "sigmoid"

        def x_copy(s):
            act.wait_ge(e["xt_ps"].sem, e["xt_ps"].at(s))
            if soft:
                if begun(s - 1):
                    act.wait_ge(e["proj_ps"].sem, e["proj_ps"].at(s - 1))
            else:
                if begun(s - 1):
                    act.wait_ge(e["rot"].sem, e["rot"].at(s - 1))
            act.copy(c.xT[:], c.A[:, 0, 0:L]).then_inc(e["xt"].sem, 1)

        def latent_copy(s):
            act.wait_ge(e["latt_ps"].sem, e["latt_ps"].at(s))
            if begun(s - 1):
                act.wait_ge(e["proj_ps"].sem, e["proj_ps"].at(s - 1))
            act.copy(w["latT"][:], c.O[0:LAT, 0, 0:L]).then_inc(e["latt"].sem, 1)

        def round_hi(s):
            act.wait_ge(e["rot"].sem, e["rot"].at(s))
            if begun(s - 1):
                act.wait_ge(e["kst_ps"].sem, e["kst_ps"].at(s - 1))
            act.copy(c.hi[:], c.rot[:]).then_inc(e["hi"].sem, 1)

        def k_copy(s, par):
            act.wait_ge(e["kst_ps"].sem, e["kst_ps"].at(s))
            if begun(s - 2):
                act.wait_ge(e["p2"].sem, e["p2"].at(s - 2))
            act.activation(c.KS[:, par].rearrange("p g l -> p (g l)"), c.A[:].rearrange("p b n -> p (b n)"),
                           ACT.Identity, bias=c.one_rows[:]).then_inc(e["ks"].sem, 1)

        def weights(s, n):
            act.wait_ge(e["p2"].sem, e["p2"].at(s, n + 1))
            if begun(s - 1):
                act.wait_ge(e["pv"].sem, e["pv"].at(s - 1, n // 3 + 1))
            act.activation(c.probs[:, n].rearrange("p b g l -> p b (g l)"), c.S[:, n % 2],
                           ACT.Exp if soft else ACT.Tanh, scale=self.scale).then_inc(e["probs"].sem, 1)

        def o_copy(s, pr):
            act.wait_ge(e["pv"].sem, e["pv"].at(s, pr + 1))
            if begun(s - 1):
                act.wait_ge(e["ctx_ps"].sem, e["ctx_ps"].at(s - 1))
            act.copy(c.OT[:, 2 * pr:2 * pr + 2].rearrange("p r l -> p (r l)"), c.O[:, pr]).then_inc(e["ot"].sem, 1)

        def ctx_copy(s):
            act.wait_ge(e["ctxt_ps"].sem, e["ctxt_ps"].at(s))
            if begun(s - 1):
                act.wait_ge(e["out_ps"].sem, e["out_ps"].at(s - 1))
            act.copy(c.ctxT[:], c.A[:, 0, 0:L]).then_inc(e["ctxt"].sem, 1)

        def front(s, par):
            x_copy(s)
            if kind == "latent":
                latent_copy(s)
            round_hi(s)
            k_copy(s, par)

        def tail(s, par):
            if soft:
                ctx_copy(s)

        def soft_step(k, par, has_tail, has_front):
            if has_front:
                x_copy(k + 1)
            if has_tail:
                ctx_copy(k - 1)
            if has_front and kind == "latent":
                latent_copy(k + 1)
            weights(k, 0)
            weights(k, 1)
            if has_front:
                round_hi(k + 1)
            weights(k, 2)
            weights(k, 3)
            o_copy(k, 0)
            weights(k, 4)
            if has_front:
                k_copy(k + 1, 1 - par)
            weights(k, 5)
            o_copy(k, 1)

        def sigmoid_step(k, par, has_tail, has_front):
            weights(k, 0)
            weights(k, 1)
            weights(k, 2)
            if has_front:
                x_copy(k + 1)
            weights(k, 3)
            if has_front:
                round_hi(k + 1)
            o_copy(k, 0)
            weights(k, 4)
            weights(k, 5)
            if has_front:
                k_copy(k + 1, 1 - par)
            o_copy(k, 1)

        pipeline(act, front, soft_step if soft else sigmoid_step, tail)

    def dve(self, dve):
        c, e, w, kind = self.c, self.e, self.w, self.kind
        soft = kind != "sigmoid"

        def latent_norm(s):
            dve.wait_ge(e["lat_ps"].sem, e["lat_ps"].at(s))
            for t in range(T):
                dve.bn_stats(w["lstats"][:, t, :], c.O[:, 0, t * LAT:(t + 1) * LAT]).then_inc(e["lbn"].sem, 1)
            for t in range(T):
                count = held(dve, e["lbn"].at(s, t + 1))
                dve.wait_ge(c.made, 1)
                dve.wait_ge(e["lbn"].sem, count)
                dve.bn_aggr(w["lmv"][:, t, :], w["lstats"][:, t, :]).then_inc(e["lmv"].sem, 1)

        def latent_scale(s):
            dve.wait_ge(e["lrstd"].sem, e["lrstd"].at(s))
            if begun(s - 1):
                dve.wait_ge(e["latt_ps"].sem, e["latt_ps"].at(s - 1))
            for t in range(T):
                dve.tensor_scalar(w["lnorm"][:, t, :], c.O[:, 0, t * LAT:(t + 1) * LAT], w["lmv"][:, t, 0:1],
                                  w["lrstd"][:, t:t + 1], ALU.subtract, ALU.mult).then_inc(e["lnorm"].sem, 1)
            for t in range(T):
                dve.wait_ge(e["lnorm"].sem, e["lnorm"].at(s, t + 1))
                dve.tensor_tensor(w["lscale"][:, t, :], w["lnorm"][:, t, :], w["gamma"][:], ALU.mult).then_inc(e["lscale"].sem, 1)
            for t in range(T):
                dve.wait_ge(e["lscale"].sem, e["lscale"].at(s, t + 1))
                dve.tensor_tensor(w["lat"][:, t, :], w["lscale"][:, t, :], w["beta"][:], ALU.add).then_inc(e["lat"].sem, 1)

        def v_copy(s, par):
            if kind == "sigmoid":
                dve.wait_ge(e["xin"].sem, e["xin"].at(s))
                if begun(s - 2):
                    dve.wait_ge(e["out_ps"].sem, e["out_ps"].at(s - 2))
            else:
                dve.wait_ge(e["v_ps"].sem, e["v_ps"].at(s))
                if begun(s - 2):
                    dve.wait_ge(e["pv"].sem, e["pv"].at(s - 2))
            for t in range(T):
                out = c.V[:, par, t, :, 0:HD]
                if kind == "rope":
                    ins = dve.tensor_tensor(out, c.A[:, 1, t * P:(t + 1) * P].rearrange("p (h d) -> p h d", d=HD),
                                            w["bv"][:].rearrange("p (h d) -> p h d", d=HD), ALU.add)
                elif kind == "latent":
                    ins = dve.tensor_copy(out, c.A[:, 1, t * P:(t + 1) * P].rearrange("p (h d) -> p h d", d=HD))
                else:
                    ins = dve.tensor_tensor(out, c.xin[:, par, t, :].rearrange("p (h d) -> p h d", d=HD),
                                            w["sv"][:].rearrange("p (h d) -> p h d", d=HD), ALU.mult)
                ins.then_inc(e["v"].sem, 1)

        def rotate(s):
            if soft:
                if begun(s - 1):
                    dve.wait_ge(e["rot"].sem, e["rot"].at(s - 1))
                for sw in range(2):
                    dve.wait_ge(e["proj_ps"].sem, e["proj_ps"].at(s, sw + 1))
                    for j in range(2):
                        dve.scalar_tensor_tensor(c.t12[:, sw, j, :], c.A[:, sw, j * L:(j + 1) * L],
                                                 w["bqk"][:, sw, j:j + 1], c.trig[:, self.layer, sw, :],
                                                 ALU.add, ALU.mult).then_inc(e["t12"].sem, 1)
                dve.wait_ge(e["t12"].sem, e["t12"].at(s))
                if begun(s - 1):
                    dve.wait_ge(e["lo"].sem, e["lo"].at(s - 1))
                if begun(s - 1):
                    dve.wait_ge(e["hi"].sem, e["hi"].at(s - 1))
                dve.tensor_tensor(c.rot[:], c.t12[:, 0], c.t12[:, 1], ALU.add).then_inc(e["rot"].sem, 1)
            else:
                dve.wait_ge(e["xt"].sem, e["xt"].at(s))
                if begun(s - 1):
                    dve.wait_ge(e["lo"].sem, e["lo"].at(s - 1))
                if begun(s - 1):
                    dve.wait_ge(e["hi"].sem, e["hi"].at(s - 1))
                for j in range(2):
                    dve.tensor_scalar(c.rot[:, j, :], c.xT[:], w["sqk"][:, j:j + 1], None,
                                      ALU.mult).then_inc(e["rot"].sem, 1)

        def round_lo(s):
            dve.wait_ge(e["hi"].sem, e["hi"].at(s))
            if begun(s - 1):
                dve.wait_ge(e["kst_ps"].sem, e["kst_ps"].at(s - 1))
            if not soft:
                dve.wait_ge(e["rot"].sem, e["rot"].at(s))
            dve.tensor_tensor(c.lo[:], c.rot[:], c.hi[:].bitcast(F32), ALU.subtract).then_inc(e["lo"].sem, 1)

        def q_copy(s, par):
            dve.wait_ge(e["qst_ps"].sem, e["qst_ps"].at(s))
            if soft:
                if begun(s - 2):
                    dve.wait_ge(e["qm"].sem, e["qm"].at(s - 2))
            else:
                if begun(s - 2):
                    dve.wait_ge(e["p2"].sem, e["p2"].at(s - 2))
            dve.tensor_copy(c.QS[:, par].rearrange("p g l -> p (g l)"),
                            c.A[:].rearrange("p b n -> p (b n)")).then_inc(e["qs"].sem, 1)

        def row_max(s, n):
            dve.wait_ge(e["p1"].sem, e["p1"].at(s, n + 1))
            if n == 0:
                if begun(s - 1):
                    dve.wait_ge(e["m"].sem, e["m"].at(s - 1))
            pr, u = n // 3, n % 3
            slot = c.S[:, n % 2]
            if u < 2:
                dve.tensor_reduce(c.nm[:, 1, 2 * pr:2 * pr + 2, 2 * u:2 * u + 2], slot.rearrange("p b (g k) -> p b g k", g=2),
                                  AX.X, ALU.max, negate=True).then_inc(e["rmax"].sem, 1)
            else:
                dve.tensor_reduce(c.nm[:, 0, 2 * pr:2 * pr + 2, :], slot.rearrange("p b (g k) -> p b g k", g=G),
                                  AX.X, ALU.max, negate=True).then_inc(e["rmax"].sem, 1)

        def max_columns(s):
            dve.wait_ge(e["rmax"].sem, e["rmax"].at(s))
            if begun(s - 1):
                dve.wait_ge(e["mx_ps"].sem, e["mx_ps"].at(s - 1))
            cols = c.M[:].rearrange("p t g (r i) -> p t g r i", i=ROWS)
            nm = c.nm[:].rearrange("p t r g -> p t g r")
            dve.tensor_copy(cols[:, :, :, :, MAX_HI], nm).then_inc(e["mhi"].sem, 1)
            dve.wait_ge(e["mhi"].sem, e["mhi"].at(s))
            dve.tensor_tensor(cols[:, :, :, :, MAX_LO], nm, cols[:, :, :, :, MAX_HI].bitcast(F32),
                              ALU.subtract).then_inc(e["m"].sem, 1)

        def add_max(s, par):
            if begun(s - 1):
                dve.wait_ge(e["p2"].sem, e["p2"].at(s - 1))
            for h in range(2):
                dve.wait_ge(e["mx_ps"].sem, e["mx_ps"].at(s, h + 1))
                dve.tensor_tensor(c.QM[:, 2 * h:2 * h + 2].rearrange("p g l -> p (g l)"), c.O[:, h, :],
                                  c.QS[:, par, 2 * h:2 * h + 2].rearrange("p g l -> p (g l)").bitcast(F32),
                                  ALU.add).then_inc(e["qm"].sem, 1)

        def context(s):
            dve.wait_ge(e["ctx_ps"].sem, e["ctx_ps"].at(s))
            if soft:
                if begun(s - 1):
                    dve.wait_ge(e["ctx"].sem, e["ctx"].at(s - 1))
                if begun(s - 1):
                    dve.wait_ge(e["ctxt_ps"].sem, e["ctxt_ps"].at(s - 1))
                for t in range(T):
                    dve.reciprocal(c.rinv[:, t], c.A[:, t].rearrange("p (r g i) -> p r g i", r=G, g=G)[:, :, :, HD])\
                       .then_inc(e["rinv"].sem, 1)
            else:
                if begun(s - 1):
                    dve.wait_ge(e["add"].sem, e["add"].at(s - 1))
            for t in range(T):
                sums = c.A[:, t].rearrange("p (r g i) -> p r g i", r=G, g=G)[:, :, :, 0:HD]
                out = c.ctx_sb[:, t, :].rearrange("p (g r d) -> p r g d", g=G, r=G)
                if soft:
                    dve.wait_ge(e["rinv"].sem, e["rinv"].at(s, t + 1))
                    ins = dve.tensor_tensor(out, sums, c.rinv[:, t].unsqueeze(3).broadcast_to((P, G, G, HD)), ALU.mult)
                else:
                    ins = dve.tensor_copy(out, sums)
                ins.then_inc(e["ctx"].sem, 1)

        def residual(s):
            dve.wait_ge(e["out_ps"].sem, e["out_ps"].at(s))
            dve.wait_ge(e["xres"].sem, e["xres"].at(s))
            if begun(s - 1):
                dve.wait_ge(e["x"].sem, e["x"].at(s - 1))
            out = (c.O if soft else c.A)[:, 1, 0:L].rearrange("p (t d) -> p t d", t=T)
            if soft:
                dve.tensor_tensor(c.res[:], out, c.xres[:], ALU.add).then_inc(e["res"].sem, 1)
            else:
                dve.wait_ge(e["ctx"].sem, e["ctx"].at(s))
                dve.tensor_tensor(c.ctxT[:].rearrange("p (t d) -> p t d", t=T), out, c.ctx_sb[:], ALU.add)\
                   .then_inc(e["add"].sem, 1)
                dve.wait_ge(e["add"].sem, e["add"].at(s))
                dve.tensor_tensor(c.res[:], c.ctxT[:].rearrange("p (t d) -> p t d", t=T), c.xres[:], ALU.add)\
                   .then_inc(e["res"].sem, 1)
            norm_stats(c, e, dve, s)

        def front(s, par):
            if kind == "latent":
                latent_norm(s)
                latent_scale(s)
            v_copy(s, par)
            rotate(s)
            round_lo(s)
            q_copy(s, par)

        def tail(s, par):
            context(s)
            residual(s)
            norm_write(c, e, dve, s)

        def soft_step(k, par, has_tail, has_front):
            row_max(k, 0)
            row_max(k, 1)
            row_max(k, 2)
            if has_tail:
                context(k - 1)
            if has_front and kind == "latent":
                latent_norm(k + 1)
            row_max(k, 3)
            if has_front:
                if kind == "latent":
                    latent_scale(k + 1)
                else:
                    v_copy(k + 1, 1 - par)
            row_max(k, 4)
            row_max(k, 5)
            max_columns(k)
            add_max(k, par)
            if has_front and kind == "latent":
                v_copy(k + 1, 1 - par)
            if has_front:
                rotate(k + 1)
            if has_tail:
                residual(k - 1)
            if has_front:
                round_lo(k + 1)
                q_copy(k + 1, 1 - par)
            if has_tail:
                norm_write(c, e, dve, k - 1)

        def sigmoid_step(k, par, has_tail, has_front):
            if has_tail:
                context(k - 1)
            if has_front:
                v_copy(k + 1, 1 - par)
            if has_tail:
                residual(k - 1)
            if has_front:
                rotate(k + 1)
            if has_tail:
                norm_write(c, e, dve, k - 1)
            if has_front:
                round_lo(k + 1)
                q_copy(k + 1, 1 - par)

        pipeline(dve, front, soft_step if soft else sigmoid_step, tail)


class ChannelMix:

    def __init__(self, c, name, w):
        self.c, self.w = c, w
        self.e = c.events(zero=1, xin=1, xt_ps=1, xt=1, mixed=2, xk=1, xr=1, k_ps=1, relu=1, act=1,
                          r_ps=1, v_ps=1, gate=1, gated=1, xres=1, **LN_EVENTS)

    def banks(self, par):
        c = self.c
        return [c.S[:, 0, 0], c.S[:, 0, 1], c.S[:, 1, 0], c.S[:, 1, 1]] if par else \
               [c.A[:, 0], c.A[:, 1], c.O[:, 0], c.O[:, 1]]

    def pool(self, pool):
        c, e = self.c, self.e

        def front(s, par):
            if begun(s - 2):
                count = held(pool, e["xt_ps"].at(s - 2))
                pool.wait_ge(c.made, 1)
                pool.wait_ge(e["xt_ps"].sem, count)
            pool.tensor_copy(c.xin[:, par], c.X[:, s]).then_inc(e["xin"].sem, 1)

        def tail(s, par):
            if begun(s - 1):
                count = held(pool, e["res"].at(s - 1))
                pool.wait_ge(c.made, 1)
                pool.wait_ge(e["res"].sem, count)
            pool.tensor_copy(c.xres[:], c.X[:, s]).then_inc(e["xres"].sem, 1)
            norm_rstd(c, e, pool, s)

        def step(k, par, has_tail, has_front):
            if has_front:
                front(k + 1, 1 - par)
            if has_tail:
                tail(k - 1, 1 - par)

        pipeline(pool, front, step, tail)

    def pe(self, pe):
        c, e, w = self.c, self.e, self.w

        def front(s, par):
            pe.wait_ge(e["xin"].sem, e["xin"].at(s))
            if begun(s - 2):
                pe.wait_ge(e["xt"].sem, e["xt"].at(s - 2))
            for t in range(T):
                mm = pe.transpose(self.banks(par)[0][:, t * P:(t + 1) * P], c.xin[:, par, t, :], c.ident[:])
            mm.then_inc(e["xt_ps"].sem, 1)

        def middle(s, par):
            xT, k, r, v = self.banks(par)
            pe.wait_ge(e["xk"].sem, e["xk"].at(s))
            if begun(s - 2):
                pe.wait_ge(e["relu"].sem, e["relu"].at(s - 2))
            pe.matmul(k[:, 0:L], w["wk"][:], w["xk"][:, par], start=True, stop=True).then_inc(e["k_ps"].sem, 1)
            pe.wait_ge(e["xr"].sem, e["xr"].at(s))
            if begun(s - 2):
                pe.wait_ge(e["gate"].sem, e["gate"].at(s - 2))
            for t in range(T):
                mm = pe.matmul(r[:, t * P:(t + 1) * P], w["xr"][:, par, t * P:(t + 1) * P], w["wr"][:], start=True, stop=True)
            mm.then_inc(e["r_ps"].sem, 1)

        def tail(s, par):
            xT, k, r, v = self.banks(par)
            pe.wait_ge(e["act"].sem, e["act"].at(s))
            if begun(s - 2):
                pe.wait_ge(e["gated"].sem, e["gated"].at(s - 2))
            for t in range(T):
                mm = pe.matmul(v[:, t * P:(t + 1) * P], w["kact"][:, par, t * P:(t + 1) * P], w["wv"][:], start=True, stop=True)
            mm.then_inc(e["v_ps"].sem, 1)

        def step(k, par, has_tail, has_front):
            if has_front:
                front(k + 1, 1 - par)
            middle(k, par)
            if has_tail:
                tail(k - 1, 1 - par)

        pipeline(pe, front, step, tail)

    def act(self, act):
        c, e, w = self.c, self.e, self.w
        act.mul(w["xTs"][:, :, 0:1], c.ones[:, 0:2].unsqueeze(2), 0.0).then_inc(e["zero"].sem, 1)

        def front(s, par):
            act.wait_ge(e["xt_ps"].sem, e["xt_ps"].at(s))
            if begun(s - 2):
                act.wait_ge(e["xk"].sem, e["xk"].at(s - 2))
            if begun(s - 2):
                act.wait_ge(e["xr"].sem, e["xr"].at(s - 2))
            act.copy(w["xTs"][:, par, 1:L + 1], self.banks(par)[0][:, 0:L]).then_inc(e["xt"].sem, 1)

        def middle(s, par):
            act.wait_ge(e["k_ps"].sem, e["k_ps"].at(s))
            if begun(s - 1):
                act.wait_ge(e["act"].sem, e["act"].at(s - 1))
            act.activation(w["relu"][:], self.banks(par)[1][:, 0:L], ACT.Relu).then_inc(e["relu"].sem, 1)
            act.wait_ge(e["relu"].sem, e["relu"].at(s))
            if begun(s - 2):
                act.wait_ge(e["v_ps"].sem, e["v_ps"].at(s - 2))
            act.activation(w["kact"][:, par], w["relu"][:], ACT.Square).then_inc(e["act"].sem, 1)
            act.wait_ge(e["r_ps"].sem, e["r_ps"].at(s))
            if begun(s - 2):
                act.wait_ge(e["gated"].sem, e["gated"].at(s - 2))
            act.activation(w["tanh"][:, par], self.banks(par)[2][:, 0:L], ACT.Tanh, scale=0.5).then_inc(e["gate"].sem, 1)

        def step(k, par, has_tail, has_front):
            if has_front:
                front(k + 1, 1 - par)
            middle(k, par)

        pipeline(act, front, step, lambda s, par: None)

    def dve(self, dve):
        c, e, w = self.c, self.e, self.w
        dve.wait_ge(e["zero"].sem, e["zero"].at(0))

        def front(s, par):
            dve.wait_ge(e["xt"].sem, e["xt"].at(s))
            if begun(s - 1):
                dve.wait_ge(e["xk"].sem, e["xk"].at(s - 1))
            if begun(s - 1):
                dve.wait_ge(e["xr"].sem, e["xr"].at(s - 1))
            for j in range(2):
                dve.tensor_scalar(w["mixed"][:, j], w["xTs"][:, par, 1:L + 1], w["mu"][:, j:j + 1], None, ALU.mult)\
                   .then_inc(e["mixed"].sem, 1)
            dve.wait_ge(e["mixed"].sem, e["mixed"].at(s, 1))
            if begun(s - 2):
                dve.wait_ge(e["k_ps"].sem, e["k_ps"].at(s - 2))
            dve.scalar_tensor_tensor(w["xk"][:, par], w["xTs"][:, par, 0:L], w["nu"][:, 0:1], w["mixed"][:, 0],
                                     ALU.mult, ALU.add).then_inc(e["xk"].sem, 1)
            dve.wait_ge(e["mixed"].sem, e["mixed"].at(s, 2))
            if begun(s - 2):
                dve.wait_ge(e["r_ps"].sem, e["r_ps"].at(s - 2))
            dve.scalar_tensor_tensor(w["xr"][:, par], w["xTs"][:, par, 0:L], w["nu"][:, 1:2], w["mixed"][:, 1],
                                     ALU.mult, ALU.add).then_inc(e["xr"].sem, 1)

        def tail(s, par):
            dve.wait_ge(e["v_ps"].sem, e["v_ps"].at(s))
            dve.wait_ge(e["gate"].sem, e["gate"].at(s))
            if begun(s - 1):
                dve.wait_ge(e["res"].sem, e["res"].at(s - 1))
            dve.scalar_tensor_tensor(w["gated"][:], w["tanh"][:, par], 1.0, self.banks(par)[3][:, 0:L],
                                     ALU.add, ALU.mult).then_inc(e["gated"].sem, 1)
            dve.wait_ge(e["gated"].sem, e["gated"].at(s))
            dve.wait_ge(e["xres"].sem, e["xres"].at(s))
            if begun(s - 1):
                dve.wait_ge(e["x"].sem, e["x"].at(s - 1))
            dve.scalar_tensor_tensor(c.res[:].rearrange("p t d -> p (t d)"), w["gated"][:], 0.5,
                                     c.xres[:].rearrange("p t d -> p (t d)"), ALU.mult, ALU.add).then_inc(e["res"].sem, 1)
            norm_stats(c, e, dve, s)
            norm_write(c, e, dve, s)

        def step(k, par, has_tail, has_front):
            if has_front:
                front(k + 1, 1 - par)
            if has_tail:
                tail(k - 1, 1 - par)

        pipeline(dve, front, step, tail)


class LinearAttention:

    def __init__(self, c, name, w):
        self.c, self.w = c, w
        self.e = c.events(xin=1, xt_ps=1, xt=1, q_ps=1, q=1, kv_ps=1, kv=T, g_ps=1, g=1,
                          o_ps=1, o=1, out_ps=1, xres=1, **LN_EVENTS)

    banks = ChannelMix.banks

    def pool(self, pool):
        c, e, w = self.c, self.e, self.w

        def front(s, par):
            if begun(s - 2):
                count = held(pool, e["xt_ps"].at(s - 2))
                pool.wait_ge(c.made, 1)
                pool.wait_ge(e["xt_ps"].sem, count)
            pool.tensor_copy(c.xin[:, par], c.X[:, s]).then_inc(e["xin"].sem, 1)

        def tail(s, par):
            if begun(s - 1):
                count = held(pool, e["res"].at(s - 1))
                pool.wait_ge(c.made, 1)
                pool.wait_ge(e["res"].sem, count)
            pool.tensor_tensor(c.xres[:], c.X[:, s], w["bo"][:].unsqueeze(1).broadcast_to((P, T, P)), ALU.add).then_inc(e["xres"].sem, 1)
            norm_rstd(c, e, pool, s)

        def step(k, par, has_tail, has_front):
            if has_front:
                front(k + 1, 1 - par)
            if has_tail:
                tail(k - 1, 1 - par)

        pipeline(pool, front, step, tail)

    def pe(self, pe):
        c, e, w = self.c, self.e, self.w

        def front(s, par):
            b = self.banks(par)
            pe.wait_ge(e["xin"].sem, e["xin"].at(s))
            if begun(s - 2):
                pe.wait_ge(e["g"].sem, e["g"].at(s - 2))
            for t in range(T):
                mm = pe.transpose(b[0][:, t * P:(t + 1) * P], c.xin[:, par, t, :], c.ident[:])
            mm.then_inc(e["xt_ps"].sem, 1)

        def middle(s, par):
            b = self.banks(par)
            pe.wait_ge(e["xt"].sem, e["xt"].at(s))
            if begun(s - 2):
                pe.wait_ge(e["o"].sem, e["o"].at(s - 2))
            pe.matmul(b[1][:, 0:L], w["wq"][:], w["xT"][:, par], start=True, stop=True).then_inc(e["q_ps"].sem, 1)
            if begun(s - 2):
                pe.wait_ge(e["res"].sem, e["res"].at(s - 2))
            for t in range(T):
                mm = pe.matmul(b[2 + t][:, 0:2 * P], w["xT"][:, par, t * P:(t + 1) * P], w["wkv"][:], start=True, stop=True)
            mm.then_inc(e["kv_ps"].sem, 1)

        def tail(s, par):
            b = self.banks(par)
            pe.wait_ge(e["kv"].sem, e["kv"].at(s))
            for t in range(T):
                mm = pe.matmul(b[0][:, 0:P], w["kv"][:, par, t, 0:P], w["kv"][:, par, t, P:2 * P],
                               start=t == 0, stop=t == T - 1)
            mm.then_inc(e["g_ps"].sem, 1)
            pe.wait_ge(e["g"].sem, e["g"].at(s))
            pe.wait_ge(e["q"].sem, e["q"].at(s))
            pe.matmul(b[1][:, 0:L], w["g"][:], w["q"][:, par], start=True, stop=True).then_inc(e["o_ps"].sem, 1)
            pe.wait_ge(e["o"].sem, e["o"].at(s))
            for t in range(T):
                mm = pe.matmul(b[2][:, t * P:(t + 1) * P], w["oT"][:, t * P:(t + 1) * P], w["wo"][:], start=True, stop=True)
            mm.then_inc(e["out_ps"].sem, 1)

        def step(k, par, has_tail, has_front):
            middle(k, par)
            if has_tail:
                tail(k - 1, 1 - par)
            if has_front:
                front(k + 1, 1 - par)

        pipeline(pe, front, step, tail)

    def act(self, act):
        c, e, w = self.c, self.e, self.w

        def front(s, par):
            act.wait_ge(e["xt_ps"].sem, e["xt_ps"].at(s))
            if begun(s - 2):
                act.wait_ge(e["kv_ps"].sem, e["kv_ps"].at(s - 2))
            act.copy(w["xT"][:, par], self.banks(par)[0][:, 0:L]).then_inc(e["xt"].sem, 1)

        def middle(s, par):
            act.wait_ge(e["q_ps"].sem, e["q_ps"].at(s))
            if begun(s - 2):
                act.wait_ge(e["o_ps"].sem, e["o_ps"].at(s - 2))
            act.activation(w["q"][:, par], self.banks(par)[1][:, 0:L], ACT.Identity, bias=w["bq"][:]).then_inc(e["q"].sem, 1)

        def tail(s, par):
            act.wait_ge(e["o_ps"].sem, e["o_ps"].at(s))
            if begun(s - 1):
                act.wait_ge(e["out_ps"].sem, e["out_ps"].at(s - 1))
            act.copy(w["oT"][:], self.banks(par)[1][:, 0:L]).then_inc(e["o"].sem, 1)

        def step(k, par, has_tail, has_front):
            middle(k, par)
            if has_tail:
                tail(k - 1, 1 - par)
            if has_front:
                front(k + 1, 1 - par)

        pipeline(act, front, step, tail)

    def dve(self, dve):
        c, e, w = self.c, self.e, self.w

        def middle(s, par):
            dve.wait_ge(e["kv_ps"].sem, e["kv_ps"].at(s))
            if begun(s - 2):
                dve.wait_ge(e["g_ps"].sem, e["g_ps"].at(s - 2))
            for t in range(T):
                dve.tensor_tensor(w["kv"][:, par, t], self.banks(par)[2 + t][:, 0:2 * P], w["bkv"][:], ALU.add)\
                   .then_inc(e["kv"].sem, 1)

        def tail(s, par):
            b = self.banks(par)
            dve.wait_ge(e["g_ps"].sem, e["g_ps"].at(s))
            if begun(s - 1):
                dve.wait_ge(e["o_ps"].sem, e["o_ps"].at(s - 1))
            dve.tensor_tensor(w["g"][:], b[0][:, 0:P], w["blocks"][:], ALU.mult).then_inc(e["g"].sem, 1)
            dve.wait_ge(e["out_ps"].sem, e["out_ps"].at(s))
            dve.wait_ge(e["xres"].sem, e["xres"].at(s))
            if begun(s - 1):
                dve.wait_ge(e["x"].sem, e["x"].at(s - 1))
            dve.tensor_tensor(c.res[:].rearrange("p t d -> p (t d)"), b[2][:, 0:L],
                              c.xres[:].rearrange("p t d -> p (t d)"), ALU.add).then_inc(e["res"].sem, 1)
            norm_stats(c, e, dve, s)
            norm_write(c, e, dve, s)

        def step(k, par, has_tail, has_front):
            middle(k, par)
            if has_tail:
                tail(k - 1, 1 - par)

        pipeline(dve, lambda s, par: None, step, tail)


class Mlp:

    def __init__(self, c, name, w, out):
        self.c, self.w, self.out = c, w, out
        self.e = c.events(xin=1, xt_ps=1, xt=1, h_ps=2, ha=2, hd=2, y_ps=1, xres=1, stored=16, **LN_EVENTS)

    banks = ChannelMix.banks

    def pool(self, pool):
        c, e, w = self.c, self.e, self.w

        def front(s, par):
            if begun(s - 2):
                count = held(pool, e["xt_ps"].at(s - 2))
                pool.wait_ge(c.made, 1)
                pool.wait_ge(e["xt_ps"].sem, count)
            pool.tensor_copy(c.xin[:, par], c.X[:, s]).then_inc(e["xin"].sem, 1)

        def tail(s, par):
            if begun(s - 1):
                count = held(pool, e["res"].at(s - 1))
                pool.wait_ge(c.made, 1)
                pool.wait_ge(e["res"].sem, count)
            pool.tensor_tensor(c.xres[:], c.X[:, s], w["b2"][:].unsqueeze(1).broadcast_to((P, T, P)), ALU.add).then_inc(e["xres"].sem, 1)
            norm_rstd(c, e, pool, s)

        def step(k, par, has_tail, has_front):
            if has_front:
                front(k + 1, 1 - par)
            if has_tail:
                tail(k - 1, 1 - par)

        pipeline(pool, front, step, tail)

    def sync(self, sp):
        c, e = self.c, self.e
        with sp.Fori(0, B) as s:
            sp.wait_ge(e["x"].sem, e["x"].at(s))
            sp.dma_start(self.out[s].rearrange("(t p) d -> p t d", t=T), c.X[:, s]).then_inc(e["stored"].sem, 16)
        sp.wait_ge(e["stored"].sem, e["stored"].at(B - 1))

    def pe(self, pe):
        c, e, w = self.c, self.e, self.w

        def front(s, par):
            b = self.banks(par)
            pe.wait_ge(e["xin"].sem, e["xin"].at(s))
            if begun(s - 2):
                pe.wait_ge(e["xt"].sem, e["xt"].at(s - 2))
            for t in range(T):
                mm = pe.transpose(b[0][:, t * P:(t + 1) * P], c.xin[:, par, t, :], c.ident[:])
            mm.then_inc(e["xt_ps"].sem, 1)

        def middle(s, par):
            b = self.banks(par)
            pe.wait_ge(e["xt"].sem, e["xt"].at(s))
            if begun(s - 2):
                pe.wait_ge(e["ha"].sem, e["ha"].at(s - 2))
            if begun(s - 2):
                pe.wait_ge(e["hd"].sem, e["hd"].at(s - 2))
            for j in range(4):
                mm = pe.matmul(b[2 + j // 2][:, (j % 2) * L:(j % 2 + 1) * L], w["w1"][:, j * P:(j + 1) * P], w["xT"][:, par],
                               start=True, stop=True)
                if j % 2:
                    mm.then_inc(e["h_ps"].sem, 1)

        def tail(s, par):
            b = self.banks(par)
            pe.wait_ge(e["ha"].sem, e["ha"].at(s))
            pe.wait_ge(e["hd"].sem, e["hd"].at(s))
            if begun(s - 2):
                pe.wait_ge(e["res"].sem, e["res"].at(s - 2))
            for t in range(T):
                for j in range(4):
                    mm = pe.matmul(b[1][:, t * P:(t + 1) * P], w["h"][:, par, j, t * P:(t + 1) * P], w["w2"][:, j],
                                   start=j == 0, stop=j == 3)
            mm.then_inc(e["y_ps"].sem, 1)

        def step(k, par, has_tail, has_front):
            if has_front:
                front(k + 1, 1 - par)
            middle(k, par)
            if has_tail:
                tail(k - 1, 1 - par)

        pipeline(pe, front, step, tail)

    def act(self, act):
        c, e, w = self.c, self.e, self.w

        def front(s, par):
            act.wait_ge(e["xt_ps"].sem, e["xt_ps"].at(s))
            if begun(s - 2):
                act.wait_ge(e["h_ps"].sem, e["h_ps"].at(s - 2))
            act.copy(w["xT"][:, par], self.banks(par)[0][:, 0:L]).then_inc(e["xt"].sem, 1)

        def middle(s, par):
            act.wait_ge(e["h_ps"].sem, e["h_ps"].at(s, 1))
            if begun(s - 2):
                act.wait_ge(e["y_ps"].sem, e["y_ps"].at(s - 2))
            for j in range(2):
                act.activation(w["h"][:, par, j], self.banks(par)[2][:, j * L:(j + 1) * L], ACT.Relu,
                               bias=w["b1"][:, j:j + 1]).then_inc(e["ha"].sem, 1)

        def step(k, par, has_tail, has_front):
            if has_front:
                front(k + 1, 1 - par)
            middle(k, par)

        pipeline(act, front, step, lambda s, par: None)

    def dve(self, dve):
        c, e, w = self.c, self.e, self.w

        def middle(s, par):
            dve.wait_ge(e["h_ps"].sem, e["h_ps"].at(s, 2))
            if begun(s - 2):
                dve.wait_ge(e["y_ps"].sem, e["y_ps"].at(s - 2))
            for j in range(2, 4):
                dve.tensor_scalar(w["h"][:, par, j], self.banks(par)[3][:, (j - 2) * L:(j - 1) * L], w["b1"][:, j:j + 1],
                                  0.0, ALU.add, ALU.max).then_inc(e["hd"].sem, 1)

        def tail(s, par):
            dve.wait_ge(e["y_ps"].sem, e["y_ps"].at(s))
            dve.wait_ge(e["xres"].sem, e["xres"].at(s))
            if begun(s - 1):
                dve.wait_ge(e["x"].sem, e["x"].at(s - 1))
            dve.tensor_tensor(c.res[:].rearrange("p t d -> p (t d)"), self.banks(par)[1][:, 0:L],
                              c.xres[:].rearrange("p t d -> p (t d)"), ALU.add).then_inc(e["res"].sem, 1)
            norm_stats(c, e, dve, s)
            norm_write(c, e, dve, s)

        def step(k, par, has_tail, has_front):
            middle(k, par)
            if has_tail:
                tail(k - 1, 1 - par)

        pipeline(dve, lambda s, par: None, step, tail)


class Experts:

    def __init__(self, c, name, layer, w):
        self.c, self.layer, self.w = c, layer, w
        self.NJ = w["hidden"] // P
        self.NA = self.NJ // 2
        self.NG = 18 if layer == 0 else 17
        self.e = c.events(xin=1, xt_ps=1, xt=1, lg_ps=1, d=1, ex=1, gate=self.NG, sc=1, z=T, z_ps=1, zT=1,
                          wt_ps=1, wt=1, b_ps=1, acc0=1, h_ps=NE, ha=NE * self.NA, hd=NE * (self.NJ - self.NA),
                          y_ps=NE, acc=NE - 1, xres=1, **LN_EVENTS)

    def pool(self, pool):
        c, e = self.c, self.e

        def front(s, par):
            if begun(s - 2):
                count = held(pool, e["xt_ps"].at(s - 2))
                pool.wait_ge(c.made, 1)
                pool.wait_ge(e["xt_ps"].sem, count)
            if self.layer == 0:
                if begun(s - 2):
                    count = held(pool, e["z"].at(s - 2))
                    pool.wait_ge(c.made, 1)
                    pool.wait_ge(e["z"].sem, count)
            pool.tensor_copy(c.xin[:, par], c.X[:, s]).then_inc(e["xin"].sem, 1)
            if begun(s - 1):
                count = held(pool, e["acc0"].at(s - 1))
                pool.wait_ge(c.made, 1)
                pool.wait_ge(e["acc0"].sem, count)
            pool.tensor_copy(c.xres[:], c.X[:, s]).then_inc(e["xres"].sem, 1)

        def step(k, par, has_tail, has_front):
            if has_tail:
                norm_rstd(c, e, pool, k - 1)
            if has_front:
                front(k + 1, 1 - par)

        pipeline(pool, front, step, lambda s, par: norm_rstd(c, e, pool, s))

    def pe(self, pe):
        c, e, w, NJ = self.c, self.e, self.w, self.NJ

        def front(s, par, n):
            if n == 0:
                pe.wait_ge(e["xin"].sem, e["xin"].at(s))
                if self.layer == 0:
                    if begun(s - 1):
                        pe.wait_ge(e["zT"].sem, e["zT"].at(s - 1))
                for t in range(T):
                    mm = pe.transpose(c.A[:, 0, t * P:(t + 1) * P], c.xin[:, par, t, :], c.ident[:])
                mm.then_inc(e["xt_ps"].sem, 1)
            elif n == 1:
                pe.wait_ge(e["xt"].sem, e["xt"].at(s))
                if begun(s - 1):
                    pe.wait_ge(e["acc0"].sem, e["acc0"].at(s - 1))
                xT = c.xT if self.layer == 0 else w["zT"][:, par]
                for t in range(T):
                    mm = pe.matmul(c.A[:, 1, t * NE:(t + 1) * NE], xT[:, t * P:(t + 1) * P], w["gate"][:],
                                   start=True, stop=True)
                mm.then_inc(e["lg_ps"].sem, 1)
            elif n == 2:
                if self.layer == 0:
                    pe.wait_ge(e["z"].sem, e["z"].at(s))
                    for t in range(T):
                        mm = pe.transpose(c.A[:, 0, t * P:(t + 1) * P], w["z"][:, t, :], c.ident[:])
                    mm.then_inc(e["z_ps"].sem, 1)
                pe.wait_ge(e["sc"].sem, e["sc"].at(s))
                for t in range(T):
                    mm = pe.transpose(c.A[0:NE, 1, t * P:(t + 1) * P], w["sc"][:, par, t, :], c.ident[:])
                mm.then_inc(e["wt_ps"].sem, 1)
            else:
                pe.wait_ge(e["wt"].sem, e["wt"].at(s))
                for t in range(T):
                    mm = pe.matmul(c.A[:, 1, t * P:(t + 1) * P], w["wT"][:, t * P:(t + 1) * P], w["b2"][:], start=True, stop=True)
                mm.then_inc(e["b_ps"].sem, 1)

        def hidden(s, par, x):
            if x == 0:
                got_input = e["zT"] if self.layer == 0 else e["xt"]
                pe.wait_ge(got_input.sem, got_input.at(s))
            if x >= 2:
                pe.wait_ge(e["ha"].sem, e["ha"].at(s, (x - 1) * self.NA))
                pe.wait_ge(e["hd"].sem, e["hd"].at(s, (x - 1) * (NJ - self.NA)))
            else:
                if begun(s - 1):
                    pe.wait_ge(e["ha"].sem, e["ha"].at(s - 1, (NE + x - 1) * self.NA))
                if begun(s - 1):
                    pe.wait_ge(e["hd"].sem, e["hd"].at(s - 1, (NE + x - 1) * (NJ - self.NA)))
            for j in range(NJ):
                bank, col = self.place(j)
                mm = pe.matmul(c.S[:, x % 2, bank, col:col + L], w["w1"][:, x, j * P:(j + 1) * P], w["zT"][:, par],
                               start=True, stop=True)
            mm.then_inc(e["h_ps"].sem, 1)

        def output(s, x):
            pe.wait_ge(e["ha"].sem, e["ha"].at(s, (x + 1) * self.NA))
            pe.wait_ge(e["hd"].sem, e["hd"].at(s, (x + 1) * (NJ - self.NA)))
            if x >= 2:
                pe.wait_ge(e["acc"].sem, e["acc"].at(s, x - 1))
            else:
                added = e["acc"] if x == 0 else e["res"]
                if begun(s - 1):
                    pe.wait_ge(added.sem, added.at(s - 1))
            for t in range(T):
                for j in range(NJ):
                    mm = pe.matmul(c.O[:, x % 2, t * P:(t + 1) * P], w["h"][:, x % 2, j, t * P:(t + 1) * P],
                                   w["w2"][:, x * NJ + j], start=j == 0, stop=j == NJ - 1)
            mm.then_inc(e["y_ps"].sem, 1)

        def whole_front(s, par):
            for n in range(4):
                front(s, par, n)

        def step(k, par, has_tail, has_front):
            for x in range(NE):
                hidden(k, par, x)
                if x > 0:
                    output(k, x - 1)
                if has_front and x in (1, 2, 5, 6):
                    front(k + 1, 1 - par, (1, 2, 5, 6).index(x))
            output(k, NE - 1)

        pipeline(pe, whole_front, step, lambda s, par: None)

    def place(self, j):
        return (0, j * L) if j < self.NA else (1, (j - self.NA) * L)

    def act(self, act):
        c, e, w = self.c, self.e, self.w

        def front(s, par, n):
            if n == 0:
                act.wait_ge(e["xt_ps"].sem, e["xt_ps"].at(s))
                if self.layer == 0:
                    if begun(s - 1):
                        act.wait_ge(e["lg_ps"].sem, e["lg_ps"].at(s - 1))
                    act.copy(c.xT[:], c.A[:, 0, 0:L]).then_inc(e["xt"].sem, 1)
                else:
                    if begun(s - 2):
                        act.wait_ge(e["h_ps"].sem, e["h_ps"].at(s - 2))
                    act.copy(w["zT"][:, par], c.A[:, 0, 0:L]).then_inc(e["xt"].sem, 1)
            elif n == 1:
                act.wait_ge(e["d"].sem, e["d"].at(s))
                act.activation(w["ex"][:], w["d"][:], ACT.Exp).then_inc(e["ex"].sem, 1)
            else:
                if self.layer == 0:
                    act.wait_ge(e["z_ps"].sem, e["z_ps"].at(s))
                    if begun(s - 2):
                        act.wait_ge(e["h_ps"].sem, e["h_ps"].at(s - 2))
                    act.copy(w["zT"][:, par], c.A[:, 0, 0:L]).then_inc(e["zT"].sem, 1)
                act.wait_ge(e["wt_ps"].sem, e["wt_ps"].at(s))
                if begun(s - 1):
                    act.wait_ge(e["b_ps"].sem, e["b_ps"].at(s - 1))
                act.copy(w["wT"][:], c.A[0:NE, 1, 0:L]).then_inc(e["wt"].sem, 1)

        def relu(s, x):
            act.wait_ge(e["h_ps"].sem, e["h_ps"].at(s, x + 1))
            if x >= 2:
                act.wait_ge(e["y_ps"].sem, e["y_ps"].at(s, x - 1))
            else:
                if begun(s - 1):
                    act.wait_ge(e["y_ps"].sem, e["y_ps"].at(s - 1, NE + x - 1))
            for j in range(self.NA):
                bank, col = self.place(j)
                act.activation(w["h"][:, x % 2, j], c.S[:, x % 2, bank, col:col + L], ACT.Relu,
                               bias=w["b1"][:, x * self.NJ + j:x * self.NJ + j + 1]).then_inc(e["ha"].sem, 1)

        def whole_front(s, par):
            for n in range(3):
                front(s, par, n)

        def step(k, par, has_tail, has_front):
            for x in range(NE):
                relu(k, x)
                if has_front and x in (1, 3, 5):
                    front(k + 1, 1 - par, (1, 3, 5).index(x))

        pipeline(act, whole_front, step, lambda s, par: None)

    def dve(self, dve):
        c, e, w, NJ = self.c, self.e, self.w, self.NJ

        def bc(col):
            return col.unsqueeze(2).broadcast_to((P, T, NE))

        def gate(s, par, part):
            n = 2 * part

            def link(ins):
                nonlocal n
                n += 1
                ins.then_inc(e["gate"].sem, 1)
                count = held(dve, e["gate"].at(s, n))
                dve.wait_ge(c.made, 1)
                dve.wait_ge(e["gate"].sem, count)

            if part == 0:
                dve.wait_ge(e["lg_ps"].sem, e["lg_ps"].at(s))
                lg = c.A[:, 1, 0:T * NE].rearrange("p (t x) -> p t x", x=NE)
                if begun(s - 1):
                    dve.wait_ge(e["ex"].sem, e["ex"].at(s - 1))
                link(dve.tensor_tensor(w["lg"][:], lg, w["bg"][:].unsqueeze(1).broadcast_to((P, T, NE)), ALU.add))
                link(dve.tensor_reduce(w["top"][:], w["lg"][:], AX.X, ALU.max, negate=True))
                dve.tensor_tensor(w["d"][:], w["lg"][:], bc(w["top"][:]), ALU.add).then_inc(e["d"].sem, 1)
                return
            dve.wait_ge(e["ex"].sem, e["ex"].at(s))
            link(dve.tensor_reduce(w["total"][:], w["ex"][:], AX.X, ALU.add))
            link(dve.reciprocal(w["inv"][:], w["total"][:]))
            link(dve.tensor_tensor(w["pr"][:], w["ex"][:], bc(w["inv"][:]), ALU.mult))
            for t in range(T):
                link(dve.max(w["v8"][:, t, :], w["pr"][:, t, :]))
            for t in range(T):
                link(dve.max_index(w["i8"][:, t, :], w["v8"][:, t, :], w["pr"][:, t, :]))
            link(dve.tensor_copy(w["f8"][:], w["i8"][:]))
            v1, v2, i1, i2 = w["v8"][:, :, 0], w["v8"][:, :, 1], w["f8"][:, :, 0], w["f8"][:, :, 1]
            if begun(s - 2):
                dve.wait_ge(e["wt_ps"].sem, e["wt_ps"].at(s - 2))
            if begun(s - 2):
                dve.wait_ge(e["res"].sem, e["res"].at(s - 2))
            if self.layer == 0:
                link(dve.tensor_tensor(w["g"][:, 0], i2, i1, ALU.is_gt))
                link(dve.scalar_tensor_tensor(w["g"][:, 1], v2, 0.0, w["g"][:, 0], ALU.is_gt, ALU.mult))
                link(dve.tensor_scalar(w["g"][:, 2], w["g"][:, 1], -1.0, 1.0, ALU.mult, ALU.add))
                link(dve.tensor_tensor(w["g"][:, 3], v1, w["g"][:, 2], ALU.mult))
                link(dve.tensor_tensor(w["g"][:, 4], v2, w["g"][:, 1], ALU.mult))
                link(dve.tensor_tensor(w["g"][:, 5], w["g"][:, 3], w["g"][:, 4], ALU.add))
                link(dve.tensor_tensor(w["g"][:, 6], i2, w["g"][:, 1], ALU.mult))
                link(dve.tensor_tensor(w["g"][:, 7], w["g"][:, 6], i1, ALU.max))
                dve.tensor_tensor(w["sc"][:, par], w["iota"][:].unsqueeze(1).broadcast_to((P, T, NE)), bc(w["g"][:, 7]),
                                  ALU.is_equal).then_inc(e["sc"].sem, 1)
                if begun(s - 1):
                    dve.wait_ge(e["z_ps"].sem, e["z_ps"].at(s - 1))
                for t in range(T):
                    dve.tensor_scalar(w["z"][:, t, :], c.xin[:, par, t, :], w["g"][:, 5, t:t + 1], None, ALU.mult)\
                       .then_inc(e["z"].sem, 1)
            else:
                iota = w["iota"][:].unsqueeze(1).broadcast_to((P, T, NE))
                link(dve.tensor_tensor(w["g"][:, 0], v1, v2, ALU.add))
                link(dve.reciprocal(w["g"][:, 1], w["g"][:, 0]))
                link(dve.tensor_tensor(w["oh"][:, 0], iota, bc(i1), ALU.is_equal))
                link(dve.tensor_tensor(w["oh"][:, 1], iota, bc(i2), ALU.is_equal))
                link(dve.tensor_tensor(w["oh"][:, 2], w["oh"][:, 0], bc(v1), ALU.mult))
                link(dve.tensor_tensor(w["oh"][:, 3], w["oh"][:, 1], bc(v2), ALU.mult))
                link(dve.tensor_tensor(w["oh"][:, 4], w["oh"][:, 2], w["oh"][:, 3], ALU.add))
                dve.tensor_tensor(w["sc"][:, par], w["oh"][:, 4], bc(w["g"][:, 1]), ALU.mult).then_inc(e["sc"].sem, 1)
            assert n == self.NG, n

        def start_sum(s):
            dve.wait_ge(e["b_ps"].sem, e["b_ps"].at(s))
            dve.wait_ge(e["xres"].sem, e["xres"].at(s))
            dve.tensor_tensor(w["acc0"][:].rearrange("p t d -> p (t d)"), c.A[:, 1, 0:L],
                              c.xres[:].rearrange("p t d -> p (t d)"), ALU.add).then_inc(e["acc0"].sem, 1)

        def relu(s, x):
            dve.wait_ge(e["h_ps"].sem, e["h_ps"].at(s, x + 1))
            if x >= 2:
                dve.wait_ge(e["y_ps"].sem, e["y_ps"].at(s, x - 1))
            else:
                if begun(s - 1):
                    dve.wait_ge(e["y_ps"].sem, e["y_ps"].at(s - 1, NE + x - 1))
            for j in range(self.NA, NJ):
                bank, col = self.place(j)
                dve.tensor_scalar(w["h"][:, x % 2, j], c.S[:, x % 2, bank, col:col + L], w["b1"][:, x * NJ + j:x * NJ + j + 1],
                                  0.0, ALU.add, ALU.max).then_inc(e["hd"].sem, 1)

        def add(s, par, x):
            dve.wait_ge(e["y_ps"].sem, e["y_ps"].at(s, x + 1))
            if x == 0:
                dve.wait_ge(e["acc0"].sem, e["acc0"].at(s))
                dve.wait_ge(e["sc"].sem, e["sc"].at(s))
            else:
                dve.wait_ge(e["acc"].sem, e["acc"].at(s, x))
            if x == NE - 1:
                if begun(s - 1):
                    dve.wait_ge(e["x"].sem, e["x"].at(s - 1))
            src = w["acc0"] if x == 0 else w["acc"]
            dst = c.res if x == NE - 1 else w["acc"]
            for t in range(T):
                ins = dve.scalar_tensor_tensor(dst[:, t, :], c.O[:, x % 2, t * P:(t + 1) * P], w["sc"][:, par, t, x:x + 1],
                                               src[:, t, :], ALU.mult, ALU.add)
            ins.then_inc((e["res"] if x == NE - 1 else e["acc"]).sem, 1)

        def front(s, par):
            gate(s, par, 0)
            gate(s, par, 1)
            start_sum(s)

        def step(k, par, has_tail, has_front):
            for x in range(NE):
                relu(k, x)
                if x > 0:
                    add(k, par, x - 1)
                if has_front:
                    if x == 3:
                        gate(k + 1, 1 - par, 0)
                    if x == 4:
                        gate(k + 1, 1 - par, 1)
                if x == 1 and has_tail:
                    norm_write(c, e, dve, k - 1)
            add(k, par, NE - 1)
            norm_stats(c, e, dve, k)
            if has_front:
                start_sum(k + 1)

        pipeline(dve, front, step, lambda s, par: norm_write(c, e, dve, s))


def build(nc, x, out, d, last=8):
    with ExitStack() as ctx:
        c = Core(nc, ctx)
        sb = c.sb
        loads = {n: [] for n in ("consts", "l0", "x", "moe0", "l1", "l2", "moe2", "l3")}

        def load(group, dst, src):
            loads[group].append((dst, src))
            return dst

        def row(name):
            return d[name].rearrange("(o n) -> o n", o=1).broadcast_to((P, d[name].shape[0]))

        raw_spread = c.probs[:, 0:2].rearrange("p n b g l -> p (n b g l)")[:, 0:4 * G * P]
        load("consts", c.ident[:], d["ident"])
        load("consts", c.mask_f[:], d["masks"])
        load("consts", raw_spread, d["spread"])
        load("consts", c.one_rows[:], d["one_rows"])
        load("consts", c.trig[:], d["trig"])
        load("x", c.X[:], x.rearrange("b (t p) d -> p b t d", t=T))

        work = c.probs[:].rearrange("p n b g l -> p (n b g l)")

        def carve(shapes, at=0):
            got = {}
            for name, shape in shapes.items():
                size = int(np.prod(shape))
                axes = " ".join("abc"[:len(shape)])
                view = work[:, at:at + size]
                got[name] = view.rearrange(f"p ({axes}) -> p {axes}", **dict(zip("abc", shape)))
                at += size
            assert at <= 6 * 2 * G * P
            return got

        w0 = dict(wqk_both=sb("wqk0", [P, 2, 2, P]), wv=sb("wv0", [P, P]), wo=sb("wo0", [P, P]),
                             bqk=sb("bqk0", [P, 2, 2]), bv=sb("bv0", [P, P]), bo=sb("bo0", [P, P]))
        w0["wqk"] = [w0["wqk_both"][:, 0], w0["wqk_both"][:, 1]]
        for dst, name in ((w0["wqk_both"], "wqk0"), (w0["wv"], "wv0"), (w0["wo"], "wo0"), (w0["bqk"], "bqk0")):
            load("l0", dst[:], d[name])
        load("l0", w0["bv"][:], row("bv0"))
        load("l0", w0["bo"][:], row("bo0"))
        w1 = dict(wq=sb("wq1", [P, 2, P]), uk=sb("uk1", [LAT, 2, P]), uv=sb("uv1", [LAT, P]),
                             dkv=sb("dkv1", [P, LAT]), wo=sb("wo1", [P, P]), bqk=sb("bqk1", [P, 2, 2]),
                             gamma=sb("gamma1", [P, LAT]), beta=sb("beta1", [P, LAT]),
                             lstats=sb("lstats", [P, T, 6]), lmv=sb("lmv", [P, T, 2]), lve=sb("lve", [P, T]),
                             lrstd=sb("lrstd", [P, T]), lnorm=sb("lnorm", [P, T, LAT]),
                             lscale=sb("lscale", [P, T, LAT]), lat=sb("lat", [P, T, LAT]), latT=sb("latT", [LAT, L]))
        w1["wqk"] = [w1["wq"], w1["uk"]]
        for dst, name in ((w1["wq"], "wq1"), (w1["uk"], "uk1"), (w1["uv"], "uv1"), (w1["dkv"], "dkv1"), (w1["wo"], "wo1")):
            load("l1", dst[:], d[name])
        load("l1", w1["gamma"][:], row("gamma1"))
        load("l1", w1["beta"][:], row("beta1"))
        wm = dict(wr=sb("wr", [P, P]), wk=sb("wk", [P, P]), wv=sb("wvm", [P, P]), mu=sb("mu", [P, 2]),
                             nu=sb("nu", [P, 2]),
                             **carve(dict(xTs=(2, L + 2), mixed=(2, L), xk=(2, L), xr=(2, L), relu=(L,), kact=(2, L),
                                          tanh=(2, L), gated=(L,))))
        for dst, name in ((wm["wr"], "wrm"), (wm["wk"], "wkm"), (wm["wv"], "wvm"), (wm["mu"], "mu")):
            load("l1", dst[:], d[name])
        w2 = dict(raw_qk=sb("raw_qk", [P, 2]), raw_v=sb("raw_v", [P, P]), sqk=sb("sqk", [P, 2]),
                             sv=sb("sv", [P, P]), neg_qk=sb("neg_qk", [P, 2]), neg_v=sb("neg_v", [P, P]))
        load("l2", w2["raw_qk"][:], d["sqk"])
        load("l2", w2["raw_v"][:], row("sv"))
        moe = {}
        for layer, hidden in ((0, d["w1_0"].shape[2]), (2, d["w1_2"].shape[2])):
            nj = hidden // P
            moe[layer] = m = dict(
                hidden=hidden, w1=sb(f"ew1_{layer}", [P, NE, hidden]), w2=sb(f"ew2_{layer}", [P, NE * nj, P]),
                b1=sb(f"eb1_{layer}", [P, NE * nj]), b2=sb(f"eb2_{layer}", [NE, P]), gate=sb(f"eg_{layer}", [P, NE]),
                bg=sb(f"ebg_{layer}", [P, NE]))
            load(f"moe{layer}", m["w1"][:], d[f"w1_{layer}"])
            load(f"moe{layer}", m["w2"][:], d[f"w2_{layer}"])
            load(f"moe{layer}", m["b1"][:], d[f"b1_{layer}"])
            load(f"moe{layer}", m["b2"][:], d[f"b2_{layer}"])
            load(f"moe{layer}", m["gate"][:], d[f"gate_{layer}"])
        load("moe0", moe[0]["bg"][:], row("bg_0"))
        shared = dict(iota=sb("iota", [P, NE]),
                      **carve(dict(h=(2, 4, L), zT=(2, L), z=(T, P), acc0=(T, P), acc=(T, P))), lg=sb("lg", [P, T, NE]), d=sb("d", [P, T, NE]),
                      ex=sb("ex", [P, T, NE]), pr=sb("pr", [P, T, NE]), v8=sb("v8", [P, T, NE]), f8=sb("f8", [P, T, NE]),
                      i8=sb("i8", [P, T, NE], mybir.dt.uint32), sc=sb("sc", [P, 2, T, NE]), oh=sb("oh", [P, 5, T, NE]),
                      top=sb("top", [P, T]), total=sb("total", [P, T]), inv=sb("inv", [P, T]), g=sb("g", [P, 8, T]),
                      wT=sb("wT", [NE, L]))
        for m in moe.values():
            for k, v in shared.items():
                m[k] = v
        load("consts", shared["iota"][:], row("iota"))
        w3 = dict(wq=sb("wq3", [P, P]), wkv=sb("wkv3", [P, 2 * P]), wo=sb("wo3", [P, P]), bq=sb("bq3", [P, 1]),
                             bkv=sb("bkv3", [P, 2 * P]), bo=sb("bo3", [P, P]), blocks=sb("blocks", [P, P]),
                             **carve(dict(xT=(2, L), q=(2, L), kv=(2, T, 2 * P), g=(P,), oT=(L,)), at=8 * L))
        for dst, name in ((w3["wq"], "wq3"), (w3["wkv"], "wkv3"), (w3["wo"], "wo3"), (w3["bq"], "bq3"), (w3["blocks"], "blocks")):
            load("l3", dst[:], d[name])
        load("l3", w3["bkv"][:], row("bkv3"))
        load("l3", w3["bo"][:], row("bo3"))
        w4 = dict(w1=sb("w1_3", [P, 4 * P]), w2=sb("w2_3", [P, 4, P]), b1=sb("b1_3", [P, 4]), b2=sb("b2_3", [P, P]),
                             xT=w3["xT"], h=shared["h"])
        for dst, name in ((w4["w1"], "w1_3"), (w4["w2"], "w2_3"), (w4["b1"], "b1_3")):
            load("l3", dst[:], d[name])
        load("l3", w4["b2"][:], row("b2_3"))

        loaded = {g: c.sem(f"loaded_{g}") for g in loads}
        made = c.made
        signs = c.sem("signs")
        phases = [("l0", Attention(c, "rope0", "rope", 0, w0)), ("moe0", Experts(c, "moe0", 0, moe[0])),
                  ("l1", Attention(c, "latent1", "latent", 1, w1)), ("l1", ChannelMix(c, "mix1", wm)),
                  ("l2", Attention(c, "sigmoid2", "sigmoid", None, w2)), ("moe2", Experts(c, "moe2", 2, moe[2])),
                  ("l3", LinearAttention(c, "linear3", w3)), ("l3", Mlp(c, "mlp3", w4, out))][:last]
        N_MADE = 13

        def enter(eng, n):
            group, phase = phases[n]
            eng.wait_ge(loaded[group], 16 * len(loads[group]))
            if n == 0:
                eng.wait_ge(loaded["x"], 16 * len(loads["x"]))
                eng.wait_ge(loaded["consts"], 16 * len(loads["consts"]))
                eng.wait_ge(made, N_MADE)
            else:
                eng.wait_ge(phases[n - 1][1].e["x"].sem, phases[n - 1][1].e["x"].at(B - 1))
            return phase

        block = ctx.enter_context(nc.Block())

        @block.sync
        def _(sp):
            for group in ("consts", "l0", "x", "moe0", "l1", "l2", "moe2", "l3"):
                for dst, src in loads[group]:
                    sp.dma_start(dst, src).then_inc(loaded[group], 16)
            if last == 8:
                phases[-1][1].sync(sp)
            else:
                sp.wait_ge(phases[-1][1].e["x"].sem, phases[-1][1].e["x"].at(B - 1))
                sp.dma_start(out.rearrange("b (t p) d -> p b t d", t=T), c.X[:]).then_inc(loaded["x"], 16)
                sp.wait_ge(loaded["x"], 32)
                for group in loads:
                    sp.wait_ge(loaded[group], 16 * len(loads[group]))

        @block.gpsimd
        def _(pool):
            for n in range(len(phases)):
                enter(pool, n).pool(pool)

        @block.tensor
        def _(pe):
            for n in range(len(phases)):
                enter(pe, n).pe(pe)

        @block.scalar
        def _(act):
            for n in range(len(phases)):
                enter(act, n).act(act)

        @block.vector
        def _(dve):
            dve.memset(c.V[:], 0.0).then_inc(made, 1)
            dve.memset(c.M[:].bitcast(F32), 0.0).then_inc(made, 1)
            dve.memset(c.ones[:], 1.0).then_inc(made, 1)
            dve.memset(c.eps[:], EPS).then_inc(made, 1)
            dve.memset(c.minus_half[:], -0.5).then_inc(made, 1)
            dve.memset(w1["bqk"][:], 0.0).then_inc(made, 1)
            dve.memset(moe[2]["bg"][:], 0.0).then_inc(made, 1)
            dve.wait_ge(made, 1)
            dve.memset(c.V[:, :, :, :, HD:HD + 1].rearrange("p a t h o -> p (a t h) o"), 1.0).then_inc(made, 1)
            dve.wait_ge(loaded["consts"], 16 * len(loads["consts"]))
            dve.tensor_copy(c.ident_r[:], c.ident[:]).then_inc(made, 1)
            dve.tensor_copy(c.ident_b[:], c.ident[:]).then_inc(made, 1)
            dve.tensor_copy(c.mask_q[:], c.mask_f[:, 0]).then_inc(made, 1)
            dve.tensor_copy(c.mask_k[:], c.mask_f[:, 1]).then_inc(made, 1)
            dve.tensor_copy(c.spread[:].rearrange("p a g l -> p (a g l)"), raw_spread).then_inc(made, 1)
            for n in range(len(phases)):
                phase = enter(dve, n)
                if n == 2:
                    dve.tensor_scalar(wm["nu"][:], wm["mu"][:], -1.0, 1.0, ALU.mult, ALU.add).then_inc(signs, 1)
                    dve.wait_ge(loaded["l2"], 16 * len(loads["l2"]))
                    dve.tensor_scalar(w2["neg_qk"][:], w2["raw_qk"][:], 0.0, None, ALU.is_lt).then_inc(signs, 1)
                    dve.tensor_scalar(w2["neg_v"][:], w2["raw_v"][:], 0.0, 0.5, ALU.is_lt, ALU.mult).then_inc(signs, 1)
                    dve.tensor_scalar(w2["sv"][:], w2["raw_v"][:], 0.0, 0.5, ALU.is_gt, ALU.mult).then_inc(signs, 1)
                    dve.wait_ge(signs, 4)
                    dve.scalar_tensor_tensor(w2["sqk"][:], w2["raw_qk"][:], 0.0, w2["neg_qk"][:], ALU.is_gt, ALU.subtract)\
                       .then_inc(signs, 1)
                    dve.tensor_tensor(w2["sv"][:], w2["sv"][:], w2["neg_v"][:], ALU.subtract).then_inc(signs, 1)
                    dve.wait_ge(signs, 6)
                phase.dve(dve)



def shape_constants():
    f = np.float32
    rows = np.arange(P)
    masks = np.stack([np.where(rows[None, :] > rows[:, None], MASKED, 0.0),
                      np.where(rows[:, None] > rows[None, :], MASKED, 0.0)], 1).astype(f)
    slots = {0: (0, 1), 1: (2,), 2: (0, 2), 3: (1,)}
    spread = np.zeros((P, 4, G, P), f)
    for kind, ss in slots.items():
        for g in range(G):
            for r in range(G):
                for slot in ss:
                    for i in range(HD):
                        spread[HD * (G * g + r) + i, kind, g, ROWS * r + HD * slot + i] = 1.0
    one_rows = ((rows % ROWS == MAX_HI) | (rows % ROWS == MAX_LO)).astype(f)[:, None]
    half = HD // 2
    pos = np.arange(L).astype(f)
    scale0 = np.power(f(1250), (f(2) * np.arange(half).astype(f) / f(HD))).astype(f)
    freq1 = (f(1.0) / np.power(f(10000.0), np.arange(half).astype(f) / f(half))).astype(f)
    trig = np.zeros((P, 2, 2, L), f)
    for layer, angle in enumerate(((pos[:, None] / scale0[None, :]).astype(f), (pos[:, None] * freq1[None, :]).astype(f))):
        for p in range(P):
            i = p % HD
            a = angle[:, i % half].astype(np.float64)
            trig[p, layer, 0] = np.cos(a)
            trig[p, layer, 1] = np.sin(a) * (-1.0 if i < half else 1.0)
    blocks = (rows[:, None] % 8 == rows[None, :] % 8).astype(f)
    return dict(ident=np.eye(P, dtype=f), masks=masks, spread=spread.reshape(P, -1), one_rows=one_rows, trig=trig,
                blocks=blocks, iota=np.arange(NE).astype(f))


def layout(inputs):
    a = {k: np.asarray(v) for k, v in inputs.items()}

    def halves_swapped(m):
        return m.reshape(*m.shape[:-1], NH, 2, HD // 2)[..., ::-1, :].reshape(m.shape)

    def with_swapped(m):
        return np.stack([m, halves_swapped(m)], -2)

    out = shape_constants()
    wq, wk = with_swapped(a["L0_attn_wq_w"]), with_swapped(a["L0_attn_wk_w"])
    out["wqk0"] = np.stack([wq, wk], 1)
    out["bqk0"] = np.stack([with_swapped(a["L0_attn_wq_b"]), with_swapped(a["L0_attn_wk_b"])], 0).transpose(2, 1, 0)
    out["wv0"], out["bv0"], out["wo0"], out["bo0"] = (a["L0_attn_" + n] for n in ("wv_w", "wv_b", "wo_w", "wo_b"))
    out["wq1"], out["uk1"] = with_swapped(a["L1_attn_W_q"]), with_swapped(a["L1_attn_W_uk"])
    out["uv1"], out["dkv1"], out["wo1"] = a["L1_attn_W_uv"], a["L1_attn_W_dkv"], a["L1_attn_W_o"]
    out["gamma1"], out["beta1"] = a["L1_attn_ln_gamma"], a["L1_attn_ln_beta"]
    for n in "rkv":
        out[f"w{n}m"] = a[f"L1_ffn_W_{n}"].T
    out["mu"] = np.stack([a["L1_ffn_mu_k"], a["L1_ffn_mu_r"]], 1)
    out["sqk"] = np.stack([a["L2_attn_bv_q"].reshape(P), a["L2_attn_bv_k"].reshape(P)], 1)
    out["sv"] = a["L2_attn_bv_v"].reshape(P)
    for layer, pre, names in ((0, "L0_ffn_", ("gate_w", "w1", "b1", "w2", "b2")), (2, "L2_ffn_", ("Wg", "W1", "b1", "W2", "b2"))):
        gate, w1, b1, w2, b2 = (a[pre + n] for n in names)
        out[f"gate_{layer}"], out[f"b2_{layer}"] = gate, b2
        out[f"w1_{layer}"] = w1.transpose(1, 0, 2)
        out[f"b1_{layer}"] = b1.reshape(-1, P).T
        out[f"w2_{layer}"] = w2.reshape(-1, P, P).transpose(1, 0, 2)
    out["bg_0"] = a["L0_ffn_gate_b"]
    wqkv = a["L3_attn_w_qkv"].T
    out["wq3"], out["wkv3"] = wqkv[:, :P], wqkv[:, P:]
    out["bq3"], out["bkv3"] = a["L3_attn_b_qkv"][:P, None], a["L3_attn_b_qkv"][P:]
    out["wo3"] = a["L3_attn_w_o"].T.reshape(8, P // 8, P).transpose(1, 0, 2).reshape(P, P)
    out["bo3"] = a["L3_attn_b_o"]
    out["w1_3"], out["b1_3"] = a["L3_ffn_W1"], a["L3_ffn_b1"].reshape(-1, P).T
    out["w2_3"], out["b2_3"] = a["L3_ffn_W2"].reshape(-1, P, P).transpose(1, 0, 2), a["L3_ffn_b2"]
    return {k: np.ascontiguousarray(v) for k, v in out.items()}


def kernel(**inputs):
    import concourse.bacc as bacc
    from concourse.bass_utils import run_bass_kernel_spmd

    nc = bacc.Bacc("TRN2", target_bir_lowering=False, num_devices=1)
    arrays = {"in_x": np.ascontiguousarray(inputs["L0_attn_x"])}
    arrays.update({"in_" + k: v for k, v in layout(inputs).items()})
    dram = {k[3:]: nc.dram_tensor(k, v.shape, mybir.dt.from_np(v.dtype), kind="ExternalInput").ap()
            for k, v in arrays.items()}
    x = dram.pop("x")
    out = nc.dram_tensor("out", x.shape, F32, kind="ExternalOutput").ap()
    build(nc, x, out, dram)
    return run_bass_kernel_spmd(nc, [arrays], core_ids=[0]).results[0]["out"]
```

```python
from contextlib import ExitStack

import numpy as np

import concourse.bass as bass
from concourse import mybir

F32 = mybir.dt.float32
F32R = mybir.dt.float32r
BF16 = mybir.dt.bfloat16
ALU = mybir.AluOpType
ACT = mybir.ActivationFunctionType
AX = mybir.AxisListType

P = 128
B = 16
T = 2
L = T * P
NH = 16
HD = P // NH
G = 4
ROWS = P // G
MAX_HI = 3 * HD
MAX_LO = MAX_HI + 1
LAT = 32
NE = 8
EPS = 1e-5
MASKED = -1e30


class Event:

    def __init__(self, sem, per, base):
        self.sem, self.per, self.base = sem, per, base

    def at(self, seq, n=None):
        return seq * self.per + (self.base + (self.per if n is None else n))


def begun(seq):
    return not (isinstance(seq, int) and seq < 0)


def held(eng, count):
    return count if isinstance(count, int) else eng.to_reg(count)


def pipeline(eng, front, step, tail):
    front(0, 0)
    step(0, 0, None, front)
    step(1, 1, tail, front)
    step(2, 0, tail, front)
    with eng.Fori(1, (B - 2) // 2) as i:
        step(2 * i + 1, 1, tail, front)
        step(2 * i + 2, 0, tail, front)
    step(B - 1, 1, tail, None)
    tail(B - 1, 1)


def copy_in(c, e, act, s, par):
    if begun(s - 2):
        count = held(act, e["xt_ps"].at(s - 2))
        act.wait_ge(c.made, 1)
        act.wait_ge(e["xt_ps"].sem, count)
    act.copy(c.xin[:, par], c.X[:, s]).then_inc(e["xin"].sem, 1)


class Core:

    def __init__(self, nc, ctx):
        self.nc, self.ctx = nc, ctx
        self.signals = {}
        sb = self.sb
        self.made = self.sem("constants_made")
        self.X = sb("X", [P, B, T, P])
        self.ident = sb("ident", [P, P])
        self.ident_r = sb("ident_r", [P, P], F32R)
        self.ident_b = sb("ident_b", [P, P], BF16)
        self.mask_f = sb("mask_f", [P, 2, P])
        self.mask_q = sb("mask_q", [P, P], BF16)
        self.mask_k = sb("mask_k", [P, P], BF16)
        self.ones = sb("ones", [P, P])
        self.eps = sb("eps", [P, T])
        self.minus_half = sb("minus_half", [P, T])
        self.spread = sb("spread", [P, 4, G, P], F32R)
        self.one_rows = sb("one_rows", [P, 1])
        self.A = ctx.enter_context(nc.psum_tensor("A", [P, 2, 512], F32))
        self.S = ctx.enter_context(nc.psum_tensor("S", [P, 2, 2, 512], F32))
        self.O = ctx.enter_context(nc.psum_tensor("O", [P, 2, 512], F32))
        self.xin = sb("xin", [P, 2, T, P])
        self.xT = sb("xT", [P, L])
        self.xres = sb("xres", [P, T, P])
        self.res = sb("res", [P, T, P])
        self.stats = sb("stats", [P, T, 6])
        self.mv = sb("mv", [P, T, 2])
        self.ve = sb("ve", [P, T])
        self.rstd = sb("rstd", [P, T])
        self.trig = sb("trig", [P, 2, 2, L])
        self.t12 = sb("t12", [P, 2, 2, L])
        self.rot = sb("rot", [P, 2, L])
        self.hi = sb("hi", [P, 2, L], F32R)
        self.lo = sb("lo", [P, 2, L], F32R)
        self.QS = sb("QS", [P, 2, G, L], F32R)
        self.KS = sb("KS", [P, 2, G, L], F32R)
        self.QM = sb("QM", [P, G, L], F32R)
        self.V = sb("V", [P, 2, T, NH, ROWS])
        self.nm = sb("nm", [P, T, G, G])
        self.M = sb("M", [P, T, G, P], F32R)
        self.probs = sb("probs", [P, 6, 2, G, P])
        self.OT = sb("OT", [P, G, L])
        self.rinv = sb("rinv", [P, T, G, G])
        self.ctx_sb = sb("ctx_sb", [P, T, P])
        self.ctxT = sb("ctxT", [P, L])

    def sb(self, name, shape, dt=F32):
        return self.ctx.enter_context(self.nc.sbuf_tensor(name, shape, dt))

    def sem(self, name):
        return self.ctx.enter_context(self.nc.semaphore(name))

    def events(self, **per):
        for k in per:
            if k not in self.signals:
                self.signals[k] = [self.sem(k), 0]
        out = {k: Event(*[self.signals[k][0], v, self.signals[k][1]]) for k, v in per.items()}
        for k, v in per.items():
            self.signals[k][1] += v * B
        return out



LN_EVENTS = dict(res=1, bn=2, mv=2, ve=1, rstd=1, x=2)


def norm_stats(c, e, dve, s):
    for t in range(T):
        if t == 0:
            dve.wait_ge(e["res"].sem, e["res"].at(s))
        dve.bn_stats(c.stats[:, t, :], c.res[:, t, :]).then_inc(e["bn"].sem, 1)
    for t in range(T):
        count = held(dve, e["bn"].at(s, t + 1))
        dve.wait_ge(c.made, 1)
        dve.wait_ge(e["bn"].sem, count)
        dve.bn_aggr(c.mv[:, t, :], c.stats[:, t, :]).then_inc(e["mv"].sem, 1)


def norm_rstd(c, e, pool, s):
    count = held(pool, e["mv"].at(s))
    pool.wait_ge(c.made, 1)
    pool.wait_ge(e["mv"].sem, count)
    pool.tensor_tensor(c.ve[:], c.mv[:, :, 1], c.eps[:], ALU.add).then_inc(e["ve"].sem, 1)
    count = held(pool, e["ve"].at(s))
    pool.wait_ge(c.made, 1)
    pool.wait_ge(e["ve"].sem, count)
    pool.tensor_tensor(c.rstd[:], c.ve[:], c.minus_half[:], ALU.pow).then_inc(e["rstd"].sem, 1)


def norm_write(c, e, dve, s):
    dve.wait_ge(e["rstd"].sem, e["rstd"].at(s))
    for t in range(T):
        dve.tensor_scalar(c.X[:, s, t, :], c.res[:, t, :], c.mv[:, t, 0:1], c.rstd[:, t:t + 1],
                          ALU.subtract, ALU.mult).then_inc(e["x"].sem, 1)


class Attention:

    def __init__(self, c, name, kind, layer, w):
        self.c, self.kind, self.layer, self.w = c, kind, layer, w
        ev = dict(xin=1, xt_ps=1, xt=1, v_ps=1, v=T, hi=1, lo=1, qst_ps=1, qs=1, kst_ps=1, ks=1,
                  p2=6, probs=6, pv=2, ot=2, ctx_ps=1, ctx=2, out_ps=1, xres=1, **LN_EVENTS)
        if kind == "sigmoid":
            ev.update(rot=2, add=1)
        else:
            ev.update(proj_ps=2, t12=4, rot=1, p1=6, rmax=6, mhi=1, m=1, mx_ps=2, qm=2,
                      rinv=2, ctxt_ps=1, ctxt=1)
        if kind == "latent":
            ev.update(lat_ps=1, lbn=T, lmv=T, lve=1, lrstd=1, lnorm=T, lscale=T, lat=T, latt_ps=1, latt=1)
        self.e = c.events(**ev)
        self.rest = None
        self.v_bank = c.O[:, 0] if kind == "latent" else c.A[:, 1]
        self.scale = HD ** -0.5 if kind != "sigmoid" else 2 * HD ** -0.5

    def pool(self, pool):
        c, e, w = self.c, self.e, self.w

        def front(s, par):
            if begun(s - 2):
                count = held(pool, e["xt_ps"].at(s - 2))
                pool.wait_ge(c.made, 1)
                pool.wait_ge(e["xt_ps"].sem, count)
            if self.kind == "sigmoid":
                if begun(s - 2):
                    count = held(pool, e["v"].at(s - 2))
                    pool.wait_ge(c.made, 1)
                    pool.wait_ge(e["v"].sem, count)
            pool.tensor_copy(c.xin[:, par], c.X[:, s]).then_inc(e["xin"].sem, 1)

        def tail(s, par):
            if begun(s - 1):
                count = held(pool, e["res"].at(s - 1))
                pool.wait_ge(c.made, 1)
                pool.wait_ge(e["res"].sem, count)
            if self.kind == "rope":
                pool.tensor_tensor(c.xres[:], c.X[:, s], w["bo"][:].unsqueeze(1).broadcast_to((P, T, P)), ALU.add).then_inc(e["xres"].sem, 1)
            else:
                pool.tensor_copy(c.xres[:], c.X[:, s]).then_inc(e["xres"].sem, 1)
            norm_rstd(c, e, pool, s)

        def latent(s):
            count = held(pool, e["lmv"].at(s))
            pool.wait_ge(c.made, 1)
            pool.wait_ge(e["lmv"].sem, count)
            pool.tensor_tensor(w["lve"][:], w["lmv"][:, :, 1], c.eps[:], ALU.add).then_inc(e["lve"].sem, 1)
            count = held(pool, e["lve"].at(s))
            pool.wait_ge(c.made, 1)
            pool.wait_ge(e["lve"].sem, count)
            pool.tensor_tensor(w["lrstd"][:], w["lve"][:], c.minus_half[:], ALU.pow).then_inc(e["lrstd"].sem, 1)

        def first(s, par):
            front(s, par)
            if self.kind == "latent":
                latent(s)

        def step(k, par, has_tail, has_front):
            if self.rest and isinstance(k, int) and k == 1:
                pool.wait_ge(self.rest[0], self.rest[1])
            if has_front:
                front(k + 1, 1 - par)
                if self.kind == "latent":
                    latent(k + 1)
            if has_tail:
                tail(k - 1, 1 - par)

        pipeline(pool, first, step, tail)

    def pe(self, pe):
        c, e, w, kind = self.c, self.e, self.w, self.kind
        soft = kind != "sigmoid"

        def x_transposes(s, par):
            pe.wait_ge(e["xin"].sem, e["xin"].at(s))
            if begun(s - 1):
                pe.wait_ge(e["ks"].sem, e["ks"].at(s - 1))
            for t in range(T):
                mm = pe.transpose(c.A[:, 0, t * P:(t + 1) * P], c.xin[:, par, t, :], c.ident[:])
            mm.then_inc(e["xt_ps"].sem, 1)

        def latent(s, par):
            pe.wait_ge(e["xt"].sem, e["xt"].at(s))
            if begun(s - 2):
                pe.wait_ge(e["ot"].sem, e["ot"].at(s - 2, 1))
            for t in range(T):
                mm = pe.matmul(c.O[:, 0, t * LAT:(t + 1) * LAT], c.xT[:, t * P:(t + 1) * P], w["dkv"][:],
                               start=True, stop=True)
            mm.then_inc(e["lat_ps"].sem, 1)

        def latent_T(s, par):
            pe.wait_ge(e["lat"].sem, e["lat"].at(s))
            for t in range(T):
                mm = pe.transpose(c.O[0:LAT, 0, t * P:(t + 1) * P], w["lat"][:, t, :], c.ident[:])
            mm.then_inc(e["latt_ps"].sem, 1)

        def values(s, par):
            pe.wait_ge(e["xt"].sem, e["xt"].at(s))
            if kind == "rope":
                if begun(s - 2):
                    pe.wait_ge(e["ctx"].sem, e["ctx"].at(s - 2))
            else:
                pe.wait_ge(e["latt"].sem, e["latt"].at(s))
                if begun(s - 1):
                    pe.wait_ge(e["qm"].sem, e["qm"].at(s - 1, 1))
            source, weight = (w["latT"], w["uv"]) if kind == "latent" else (c.xT, w["wv"])
            for t in range(T):
                mm = pe.matmul(self.v_bank[:, t * P:(t + 1) * P], source[:, t * P:(t + 1) * P], weight[:],
                               start=True, stop=True)
            mm.then_inc(e["v_ps"].sem, 1)

        def projections(s, sw, sides=(0, 1)):
            if sw and kind == "latent":
                if begun(s - 2):
                    pe.wait_ge(e["ctx"].sem, e["ctx"].at(s - 2))
            elif sw:
                pe.wait_ge(e["v"].sem, e["v"].at(s))
            else:
                pe.wait_ge(e["xt"].sem, e["xt"].at(s))
                if begun(s - 2):
                    pe.wait_ge(e["ctxt"].sem, e["ctxt"].at(s - 2))
            if kind == "latent" and 1 in sides:
                pe.wait_ge(e["latt"].sem, e["latt"].at(s))
            for j in sides:
                src = w["latT"] if (kind == "latent" and j == 1) else c.xT
                mm = pe.matmul(c.A[:, sw, j * L:(j + 1) * L], w["wqk"][j][:, sw, :], src[:], start=True, stop=True)
            if 1 in sides:
                mm.then_inc(e["proj_ps"].sem, 1)

        def stack(s, j):
            if j == 0:
                pe.wait_ge(e["hi"].sem, e["hi"].at(s))
                pe.wait_ge(e["lo"].sem, e["lo"].at(s))
                if soft:
                    pe.wait_ge(e["t12"].sem, e["t12"].at(s))
                else:
                    pe.wait_ge(e["xt"].sem, e["xt"].at(s))
                    if begun(s - 2):
                        pe.wait_ge(e["ctx"].sem, e["ctx"].at(s - 2))
            else:
                pe.wait_ge(e["qs"].sem, e["qs"].at(s))
            for g in range(G):
                out = c.A[:, g // 2, (g % 2) * L:(g % 2 + 1) * L]
                pe.matmul(out, c.spread[:, 2 * j, g, :], c.hi[:, j, :], start=True, stop=False)
                mm = pe.matmul(out, c.spread[:, 2 * j + 1, g, :], c.lo[:, j, :], start=False, stop=True)
            mm.then_inc((e["kst_ps"] if j else e["qst_ps"]).sem, 1)

        def score_slot(slot, lhs, rhs, pr, u, mask, diagonal):
            for b in range(2):
                out = slot[:, b].rearrange("p (g t k) -> p g t k", g=2, t=2)
                if u < 2:
                    pe.matmul(out[:, :, diagonal, :], c.ident_b[:], mask[:].unsqueeze(1).broadcast_to((P, 2, P)),
                              start=True, stop=False, skip_group_check=True)
                else:
                    pe.matmul(slot[:, b], c.ident_b[:], mask[:].unsqueeze(1).broadcast_to((P, G, P)),
                              start=True, stop=False, skip_group_check=True)
            width = L if u < 2 else P
            tile = diagonal if u < 2 else 1 - diagonal
            for n in range(512 // width):
                for b in range(2):
                    r = 2 * pr + b
                    rows = slice(r * ROWS, (r + 1) * ROWS)
                    g = 2 * u + n if u < 2 else n
                    right = rhs[rows, g, :] if u < 2 else rhs[rows, g, tile * P:(tile + 1) * P]
                    mm = pe.matmul(slot[:, b, n * width:(n + 1) * width], lhs[rows, g, tile * P:(tile + 1) * P], right,
                                   start=False, stop=True, skip_group_check=True)
            return mm

        def pass1(s, par, n):
            if n == 0:
                pe.wait_ge(e["qs"].sem, e["qs"].at(s))
                pe.wait_ge(e["ks"].sem, e["ks"].at(s))
            if n < 2:
                if begun(s - 1):
                    pe.wait_ge(e["probs"].sem, e["probs"].at(s - 1, 5 + n))
            else:
                pe.wait_ge(e["rmax"].sem, e["rmax"].at(s, n - 1))
            pr, u = n // 3, n % 3
            q, k = c.QS[:, par], c.KS[:, par]
            score_slot(c.S[:, n % 2], q, k, pr, u, c.mask_q, 1).then_inc(e["p1"].sem, 1)

        def maxima(s, has_front):
            pe.wait_ge(e["m"].sem, e["m"].at(s))
            if begun(s - 1):
                pe.wait_ge(e["ot"].sem, e["ot"].at(s - 1))
            if has_front and kind == "latent":
                pe.wait_ge(e["latt"].sem, e["latt"].at(s + 1))
            for g in range(G):
                for t in range(T):
                    mm = pe.matmul(c.O[:, g // 2, (g % 2) * L + t * P:(g % 2) * L + (t + 1) * P],
                                   c.M[:, t, g, :], c.ident_r[:], start=True, stop=True)
                if g % 2:
                    mm.then_inc(e["mx_ps"].sem, 1)

        def pass2(s, par, n):
            if soft and n < 2:
                pe.wait_ge(e["qm"].sem, e["qm"].at(s, n + 1))
            if n == 0:
                if not soft:
                    pe.wait_ge(e["qs"].sem, e["qs"].at(s))
                    pe.wait_ge(e["ks"].sem, e["ks"].at(s))
            if n >= 2:
                pe.wait_ge(e["probs"].sem, e["probs"].at(s, n - 1))
            elif soft:
                pe.wait_ge(e["rmax"].sem, e["rmax"].at(s, 5 + n))
            else:
                if begun(s - 1):
                    pe.wait_ge(e["probs"].sem, e["probs"].at(s - 1, 5 + n))
            pr, u = n // 3, n % 3
            q = c.QM if soft else c.QS[:, par]
            k = c.KS[:, par]
            score_slot(c.S[:, n % 2], k, q, pr, u, c.mask_k, 0).then_inc(e["p2"].sem, 1)

        def weighted(s, par, pr, has_front=True):
            pe.wait_ge(e["probs"].sem, e["probs"].at(s, 3 * pr + 3))
            if begun(s - 1):
                pe.wait_ge(e["ot"].sem, e["ot"].at(s - 1, pr + 1))
            if pr == 0:
                pe.wait_ge(e["v"].sem, e["v"].at(s))
                if soft:
                    pe.wait_ge(e["qm"].sem, e["qm"].at(s))
                if kind == "latent" and has_front:
                    pe.wait_ge(e["v"].sem, e["v"].at(s + 1))
            else:
                if begun(s - 1):
                    pe.wait_ge(e["res"].sem, e["res"].at(s - 1))
            for b in range(2):
                r = 2 * pr + b
                for g in range(G):
                    pe.matmul(c.O[g * ROWS:(g + 1) * ROWS, pr, b * L:(b + 1) * L],
                              c.V[:, par, 0, 4 * g + r, :], c.probs[:, 3 * pr + g // 2, b, 2 * (g % 2):2 * (g % 2) + 2, :],
                              start=True, stop=False, skip_group_check=True)
                for g in range(G):
                    mm = pe.matmul(c.O[g * ROWS:(g + 1) * ROWS, pr, b * L + P:(b + 1) * L],
                                   c.V[:, par, 1, 4 * g + r, :], c.probs[:, 3 * pr + 2, b, g, :],
                                   start=False, stop=True, skip_group_check=True)
            mm.then_inc(e["pv"].sem, 1)

        def out_transposes(s, has_front, last=False):
            pe.wait_ge(e["ot"].sem, e["ot"].at(s))
            if not last:
                pe.wait_ge(e["ks"].sem, e["ks"].at(s + 1))
                if has_front:
                    pe.wait_ge(e["xt"].sem, e["xt"].at(s + 2))
            elif soft:
                pe.wait_ge(e["ctxt"].sem, e["ctxt"].at(s - 1))
            else:
                pe.wait_ge(e["ctx"].sem, e["ctx"].at(s - 1))
            for t in range(T):
                for r in range(G):
                    mm = pe.transpose(c.A[:, t, r * P:(r + 1) * P], c.OT[:, r, t * P:(t + 1) * P], c.ident[:])
            mm.then_inc(e["ctx_ps"].sem, 1)

        def ctx_transposes(s):
            pe.wait_ge(e["ctx"].sem, e["ctx"].at(s))
            for t in range(T):
                mm = pe.transpose(c.A[:, 0, t * P:(t + 1) * P], c.ctx_sb[:, t, :], c.ident[:])
            mm.then_inc(e["ctxt_ps"].sem, 1)

        def output(s, par, last=False):
            if soft:
                pe.wait_ge(e["ctxt"].sem, e["ctxt"].at(s))
                if last:
                    pe.wait_ge(e["ot"].sem, e["ot"].at(s))
                else:
                    pe.wait_ge(e["qm"].sem, e["qm"].at(s + 1))
                for t in range(T):
                    mm = pe.matmul(c.O[:, 1, t * P:(t + 1) * P], c.ctxT[:, t * P:(t + 1) * P], w["wo"][:],
                                   start=True, stop=True)
            else:
                pe.wait_ge(e["ctx"].sem, e["ctx"].at(s))
                pe.wait_ge(e["ot"].sem, e["ot"].at(s))
                V0, V1 = (c.V[:, par, t, :, 0:HD] for t in range(T))
                pe.matmul(c.O[:, 1, 0:P], c.ones[:], V0, start=True, stop=True)
                pe.matmul(c.O[:, 1, P:2 * P], c.ones[:], V0, start=True, stop=False)
                mm = pe.matmul(c.O[:, 1, P:2 * P], c.ones[:], V1, start=False, stop=True)
            mm.then_inc(e["out_ps"].sem, 1)

        def front(s, par):
            x_transposes(s, par)
            if kind == "latent":
                latent(s, par)
                latent_T(s, par)
            if soft:
                values(s, par)
                projections(s, 0)
                projections(s, 1)
            stack(s, 0)
            stack(s, 1)
            for n in range(2 if soft else 1):
                (pass1 if soft else pass2)(s, par, n)

        def tail(s, par):
            out_transposes(s, False, last=True)
            if soft:
                ctx_transposes(s)
            output(s, par, last=True)

        def rope_step(k, par, has_tail, has_front):
            nxt = 1 - par
            if has_front:
                x_transposes(k + 1, nxt)
            pass1(k, par, 2)
            if has_tail:
                out_transposes(k - 1, has_front)
            pass1(k, par, 3)
            pass1(k, par, 4)
            if has_tail:
                ctx_transposes(k - 1)
            if has_front:
                values(k + 1, nxt)
            pass1(k, par, 5)
            if has_front:
                projections(k + 1, 0)
            maxima(k, has_front)
            if has_front:
                projections(k + 1, 1)
            pass2(k, par, 0)
            pass2(k, par, 1)
            if has_tail:
                output(k - 1, nxt)
            pass2(k, par, 2)
            pass2(k, par, 3)
            if has_front:
                stack(k + 1, 0)
            weighted(k, par, 0, has_front)
            pass2(k, par, 4)
            if has_front:
                stack(k + 1, 1)
            pass2(k, par, 5)
            if has_front:
                pass1(k + 1, nxt, 0)
                pass1(k + 1, nxt, 1)
            weighted(k, par, 1)

        def latent_step(k, par, has_tail, has_front):
            nxt = 1 - par
            if has_front:
                x_transposes(k + 1, nxt)
            pass1(k, par, 2)
            if has_tail:
                out_transposes(k - 1, has_front)
            if has_front:
                latent(k + 1, nxt)
            pass1(k, par, 3)
            pass1(k, par, 4)
            if has_tail:
                ctx_transposes(k - 1)
            pass1(k, par, 5)
            if has_front:
                projections(k + 1, 0, (0,))
                latent_T(k + 1, nxt)
                projections(k + 1, 1, (0,))
            maxima(k, has_front)
            if has_front:
                projections(k + 1, 0, (1,))
                projections(k + 1, 1, (1,))
            pass2(k, par, 0)
            if has_front:
                values(k + 1, nxt)
            pass2(k, par, 1)
            if has_tail:
                output(k - 1, nxt)
            pass2(k, par, 2)
            pass2(k, par, 3)
            if has_front:
                stack(k + 1, 0)
            weighted(k, par, 0, has_front)
            pass2(k, par, 4)
            if has_front:
                stack(k + 1, 1)
            pass2(k, par, 5)
            if has_front:
                pass1(k + 1, nxt, 0)
                pass1(k + 1, nxt, 1)
            weighted(k, par, 1)

        def sigmoid_step(k, par, has_tail, has_front):
            nxt = 1 - par
            if has_front:
                x_transposes(k + 1, nxt)
            pass2(k, par, 1)
            if has_tail:
                out_transposes(k - 1, has_front)
            pass2(k, par, 2)
            if has_tail:
                output(k - 1, nxt)
            pass2(k, par, 3)
            if has_front:
                stack(k + 1, 0)
            weighted(k, par, 0, has_front)
            pass2(k, par, 4)
            if has_front:
                stack(k + 1, 1)
            pass2(k, par, 5)
            if has_front:
                pass2(k + 1, nxt, 0)
            weighted(k, par, 1)

        pipeline(pe, front, {"rope": rope_step, "latent": latent_step, "sigmoid": sigmoid_step}[kind], tail)

    def act(self, act):
        c, e, w, kind = self.c, self.e, self.w, self.kind
        soft = kind != "sigmoid"

        def x_copy(s):
            act.wait_ge(e["xt_ps"].sem, e["xt_ps"].at(s))
            if soft:
                if begun(s - 1):
                    act.wait_ge(e["proj_ps"].sem, e["proj_ps"].at(s - 1))
            else:
                if begun(s - 1):
                    act.wait_ge(e["rot"].sem, e["rot"].at(s - 1))
            act.copy(c.xT[:], c.A[:, 0, 0:L]).then_inc(e["xt"].sem, 1)

        def latent_copy(s):
            act.wait_ge(e["latt_ps"].sem, e["latt_ps"].at(s))
            if begun(s - 1):
                act.wait_ge(e["proj_ps"].sem, e["proj_ps"].at(s - 1))
            act.copy(w["latT"][:], c.O[0:LAT, 0, 0:L]).then_inc(e["latt"].sem, 1)

        def round_hi(s):
            act.wait_ge(e["rot"].sem, e["rot"].at(s))
            if begun(s - 1):
                act.wait_ge(e["kst_ps"].sem, e["kst_ps"].at(s - 1))
            act.copy(c.hi[:], c.rot[:]).then_inc(e["hi"].sem, 1)

        def k_copy(s, par):
            act.wait_ge(e["kst_ps"].sem, e["kst_ps"].at(s))
            if begun(s - 2):
                act.wait_ge(e["p2"].sem, e["p2"].at(s - 2))
            act.activation(c.KS[:, par].rearrange("p g l -> p (g l)"), c.A[:].rearrange("p b n -> p (b n)"),
                           ACT.Identity, bias=c.one_rows[:]).then_inc(e["ks"].sem, 1)

        def weights(s, n):
            act.wait_ge(e["p2"].sem, e["p2"].at(s, n + 1))
            if begun(s - 1):
                act.wait_ge(e["pv"].sem, e["pv"].at(s - 1, n // 3 + 1))
            act.activation(c.probs[:, n].rearrange("p b g l -> p b (g l)"), c.S[:, n % 2],
                           ACT.Exp if soft else ACT.Tanh, scale=self.scale).then_inc(e["probs"].sem, 1)

        def o_copy(s, pr):
            act.wait_ge(e["pv"].sem, e["pv"].at(s, pr + 1))
            if begun(s - 1):
                act.wait_ge(e["ctx_ps"].sem, e["ctx_ps"].at(s - 1))
            act.copy(c.OT[:, 2 * pr:2 * pr + 2].rearrange("p r l -> p (r l)"), c.O[:, pr]).then_inc(e["ot"].sem, 1)

        def ctx_copy(s):
            act.wait_ge(e["ctxt_ps"].sem, e["ctxt_ps"].at(s))
            if begun(s - 1):
                act.wait_ge(e["out_ps"].sem, e["out_ps"].at(s - 1))
            act.copy(c.ctxT[:], c.A[:, 0, 0:L]).then_inc(e["ctxt"].sem, 1)

        def front(s, par):
            x_copy(s)
            if kind == "latent":
                latent_copy(s)
            round_hi(s)
            k_copy(s, par)

        def tail(s, par):
            if soft:
                ctx_copy(s)

        def rope_step(k, par, has_tail, has_front):
            if has_front:
                x_copy(k + 1)
            if has_tail:
                ctx_copy(k - 1)
            weights(k, 0)
            weights(k, 1)
            if has_front:
                round_hi(k + 1)
            weights(k, 2)
            weights(k, 3)
            o_copy(k, 0)
            weights(k, 4)
            if has_front:
                k_copy(k + 1, 1 - par)
            weights(k, 5)
            o_copy(k, 1)

        def latent_step(k, par, has_tail, has_front):
            if has_front:
                x_copy(k + 1)
            if has_tail:
                ctx_copy(k - 1)
            if has_front:
                latent_copy(k + 1)
            weights(k, 0)
            weights(k, 1)
            if has_front:
                round_hi(k + 1)
            weights(k, 2)
            weights(k, 3)
            o_copy(k, 0)
            weights(k, 4)
            if has_front:
                k_copy(k + 1, 1 - par)
            weights(k, 5)
            o_copy(k, 1)

        def sigmoid_step(k, par, has_tail, has_front):
            if has_front:
                x_copy(k + 1)
            weights(k, 0)
            if has_front:
                round_hi(k + 1)
            weights(k, 1)
            weights(k, 2)
            weights(k, 3)
            o_copy(k, 0)
            weights(k, 4)
            if has_front:
                k_copy(k + 1, 1 - par)
            weights(k, 5)
            o_copy(k, 1)

        pipeline(act, front, {"rope": rope_step, "latent": latent_step, "sigmoid": sigmoid_step}[kind], tail)

    def dve(self, dve):
        c, e, w, kind = self.c, self.e, self.w, self.kind
        soft = kind != "sigmoid"

        def latent_norm(s):
            dve.wait_ge(e["lat_ps"].sem, e["lat_ps"].at(s))
            for t in range(T):
                dve.bn_stats(w["lstats"][:, t, :], c.O[:, 0, t * LAT:(t + 1) * LAT]).then_inc(e["lbn"].sem, 1)
            for t in range(T):
                count = held(dve, e["lbn"].at(s, t + 1))
                dve.wait_ge(c.made, 1)
                dve.wait_ge(e["lbn"].sem, count)
                dve.bn_aggr(w["lmv"][:, t, :], w["lstats"][:, t, :]).then_inc(e["lmv"].sem, 1)

        def latent_scale(s):
            dve.wait_ge(e["lrstd"].sem, e["lrstd"].at(s))
            if begun(s - 1):
                dve.wait_ge(e["latt_ps"].sem, e["latt_ps"].at(s - 1))
            for t in range(T):
                dve.tensor_scalar(w["lnorm"][:, t, :], c.O[:, 0, t * LAT:(t + 1) * LAT], w["lmv"][:, t, 0:1],
                                  w["lrstd"][:, t:t + 1], ALU.subtract, ALU.mult).then_inc(e["lnorm"].sem, 1)
            for t in range(T):
                dve.wait_ge(e["lnorm"].sem, e["lnorm"].at(s, t + 1))
                dve.tensor_tensor(w["lscale"][:, t, :], w["lnorm"][:, t, :], w["gamma"][:], ALU.mult).then_inc(e["lscale"].sem, 1)
            for t in range(T):
                dve.wait_ge(e["lscale"].sem, e["lscale"].at(s, t + 1))
                dve.tensor_tensor(w["lat"][:, t, :], w["lscale"][:, t, :], w["beta"][:], ALU.add).then_inc(e["lat"].sem, 1)

        def v_copy(s, par):
            if kind == "sigmoid":
                dve.wait_ge(e["xin"].sem, e["xin"].at(s))
                if begun(s - 2):
                    dve.wait_ge(e["out_ps"].sem, e["out_ps"].at(s - 2))
            else:
                dve.wait_ge(e["v_ps"].sem, e["v_ps"].at(s))
                if begun(s - 2):
                    dve.wait_ge(e["pv"].sem, e["pv"].at(s - 2))
            for t in range(T):
                out = c.V[:, par, t, :, 0:HD]
                if kind == "rope":
                    ins = dve.tensor_tensor(out, self.v_bank[:, t * P:(t + 1) * P].rearrange("p (h d) -> p h d", d=HD),
                                            w["bv"][:].rearrange("p (h d) -> p h d", d=HD), ALU.add)
                elif kind == "latent":
                    ins = dve.tensor_copy(out, self.v_bank[:, t * P:(t + 1) * P].rearrange("p (h d) -> p h d", d=HD))
                else:
                    ins = dve.tensor_tensor(out, c.xin[:, par, t, :].rearrange("p (h d) -> p h d", d=HD),
                                            w["sv"][:].rearrange("p (h d) -> p h d", d=HD), ALU.mult)
                ins.then_inc(e["v"].sem, 1)

        def rotate(s):
            if soft:
                if begun(s - 1):
                    dve.wait_ge(e["rot"].sem, e["rot"].at(s - 1))
                for sw in range(2):
                    dve.wait_ge(e["proj_ps"].sem, e["proj_ps"].at(s, sw + 1))
                    for j in range(2):
                        dve.scalar_tensor_tensor(c.t12[:, sw, j, :], c.A[:, sw, j * L:(j + 1) * L],
                                                 w["bqk"][:, sw, j:j + 1], c.trig[:, self.layer, sw, :],
                                                 ALU.add, ALU.mult).then_inc(e["t12"].sem, 1)
                dve.wait_ge(e["t12"].sem, e["t12"].at(s))
                if begun(s - 1):
                    dve.wait_ge(e["lo"].sem, e["lo"].at(s - 1))
                if begun(s - 1):
                    dve.wait_ge(e["hi"].sem, e["hi"].at(s - 1))
                dve.tensor_tensor(c.rot[:], c.t12[:, 0], c.t12[:, 1], ALU.add).then_inc(e["rot"].sem, 1)
            else:
                dve.wait_ge(e["xt"].sem, e["xt"].at(s))
                if begun(s - 1):
                    dve.wait_ge(e["lo"].sem, e["lo"].at(s - 1))
                if begun(s - 1):
                    dve.wait_ge(e["hi"].sem, e["hi"].at(s - 1))
                for j in range(2):
                    dve.tensor_scalar(c.rot[:, j, :], c.xT[:], w["sqk"][:, j:j + 1], None,
                                      ALU.mult).then_inc(e["rot"].sem, 1)

        def round_lo(s):
            dve.wait_ge(e["hi"].sem, e["hi"].at(s))
            if begun(s - 1):
                dve.wait_ge(e["kst_ps"].sem, e["kst_ps"].at(s - 1))
            if not soft:
                dve.wait_ge(e["rot"].sem, e["rot"].at(s))
            dve.tensor_tensor(c.lo[:], c.rot[:], c.hi[:].bitcast(F32), ALU.subtract).then_inc(e["lo"].sem, 1)

        def q_copy(s, par):
            dve.wait_ge(e["qst_ps"].sem, e["qst_ps"].at(s))
            if soft:
                if begun(s - 2):
                    dve.wait_ge(e["qm"].sem, e["qm"].at(s - 2))
            else:
                if begun(s - 2):
                    dve.wait_ge(e["p2"].sem, e["p2"].at(s - 2))
            dve.tensor_copy(c.QS[:, par].rearrange("p g l -> p (g l)"),
                            c.A[:].rearrange("p b n -> p (b n)")).then_inc(e["qs"].sem, 1)

        def row_max(s, n):
            dve.wait_ge(e["p1"].sem, e["p1"].at(s, n + 1))
            if n == 0:
                if begun(s - 1):
                    dve.wait_ge(e["m"].sem, e["m"].at(s - 1))
            pr, u = n // 3, n % 3
            slot = c.S[:, n % 2]
            if u < 2:
                dve.tensor_reduce(c.nm[:, 1, 2 * pr:2 * pr + 2, 2 * u:2 * u + 2], slot.rearrange("p b (g k) -> p b g k", g=2),
                                  AX.X, ALU.max, negate=True).then_inc(e["rmax"].sem, 1)
            else:
                dve.tensor_reduce(c.nm[:, 0, 2 * pr:2 * pr + 2, :], slot.rearrange("p b (g k) -> p b g k", g=G),
                                  AX.X, ALU.max, negate=True).then_inc(e["rmax"].sem, 1)

        def max_columns(s):
            dve.wait_ge(e["rmax"].sem, e["rmax"].at(s))
            if begun(s - 1):
                dve.wait_ge(e["mx_ps"].sem, e["mx_ps"].at(s - 1))
            cols = c.M[:].rearrange("p t g (r i) -> p t g r i", i=ROWS)
            nm = c.nm[:].rearrange("p t r g -> p t g r")
            dve.tensor_copy(cols[:, :, :, :, MAX_HI], nm).then_inc(e["mhi"].sem, 1)
            dve.wait_ge(e["mhi"].sem, e["mhi"].at(s))
            dve.tensor_tensor(cols[:, :, :, :, MAX_LO], nm, cols[:, :, :, :, MAX_HI].bitcast(F32),
                              ALU.subtract).then_inc(e["m"].sem, 1)

        def add_max(s, par):
            if begun(s - 1):
                dve.wait_ge(e["p2"].sem, e["p2"].at(s - 1))
            for h in range(2):
                dve.wait_ge(e["mx_ps"].sem, e["mx_ps"].at(s, h + 1))
                dve.tensor_tensor(c.QM[:, 2 * h:2 * h + 2].rearrange("p g l -> p (g l)"), c.O[:, h, :],
                                  c.QS[:, par, 2 * h:2 * h + 2].rearrange("p g l -> p (g l)").bitcast(F32),
                                  ALU.add).then_inc(e["qm"].sem, 1)

        def context(s):
            dve.wait_ge(e["ctx_ps"].sem, e["ctx_ps"].at(s))
            if soft:
                if begun(s - 1):
                    dve.wait_ge(e["ctx"].sem, e["ctx"].at(s - 1))
                if begun(s - 1):
                    dve.wait_ge(e["ctxt_ps"].sem, e["ctxt_ps"].at(s - 1))
                for t in range(T):
                    dve.reciprocal(c.rinv[:, t], c.A[:, t].rearrange("p (r g i) -> p r g i", r=G, g=G)[:, :, :, HD])\
                       .then_inc(e["rinv"].sem, 1)
            else:
                if begun(s - 1):
                    dve.wait_ge(e["add"].sem, e["add"].at(s - 1))
            for t in range(T):
                sums = c.A[:, t].rearrange("p (r g i) -> p r g i", r=G, g=G)[:, :, :, 0:HD]
                out = c.ctx_sb[:, t, :].rearrange("p (g r d) -> p r g d", g=G, r=G)
                if soft:
                    dve.wait_ge(e["rinv"].sem, e["rinv"].at(s, t + 1))
                    ins = dve.tensor_tensor(out, sums, c.rinv[:, t].unsqueeze(3).broadcast_to((P, G, G, HD)), ALU.mult)
                else:
                    ins = dve.tensor_copy(out, sums)
                ins.then_inc(e["ctx"].sem, 1)

        def residual(s):
            dve.wait_ge(e["out_ps"].sem, e["out_ps"].at(s))
            dve.wait_ge(e["xres"].sem, e["xres"].at(s))
            if begun(s - 1):
                dve.wait_ge(e["x"].sem, e["x"].at(s - 1))
            out = c.O[:, 1, 0:L].rearrange("p (t d) -> p t d", t=T)
            if soft:
                dve.tensor_tensor(c.res[:], out, c.xres[:], ALU.add).then_inc(e["res"].sem, 1)
            else:
                dve.wait_ge(e["ctx"].sem, e["ctx"].at(s))
                dve.tensor_tensor(c.ctxT[:].rearrange("p (t d) -> p t d", t=T), out, c.ctx_sb[:], ALU.add)\
                   .then_inc(e["add"].sem, 1)
                dve.wait_ge(e["add"].sem, e["add"].at(s))
                dve.tensor_tensor(c.res[:], c.ctxT[:].rearrange("p (t d) -> p t d", t=T), c.xres[:], ALU.add)\
                   .then_inc(e["res"].sem, 1)
            norm_stats(c, e, dve, s)

        def front(s, par):
            if kind == "latent":
                latent_norm(s)
                latent_scale(s)
            v_copy(s, par)
            rotate(s)
            round_lo(s)
            q_copy(s, par)

        def tail(s, par):
            context(s)
            residual(s)
            norm_write(c, e, dve, s)

        def rope_step(k, par, has_tail, has_front):
            row_max(k, 0)
            row_max(k, 1)
            row_max(k, 2)
            if has_tail:
                context(k - 1)
            row_max(k, 3)
            row_max(k, 4)
            if has_front:
                v_copy(k + 1, 1 - par)
            row_max(k, 5)
            max_columns(k)
            add_max(k, par)
            if has_front:
                rotate(k + 1)
                round_lo(k + 1)
                q_copy(k + 1, 1 - par)
            if has_tail:
                residual(k - 1)
                norm_write(c, e, dve, k - 1)

        def latent_step(k, par, has_tail, has_front):
            row_max(k, 0)
            row_max(k, 1)
            if has_tail:
                context(k - 1)
            row_max(k, 2)
            if has_front:
                latent_norm(k + 1)
            row_max(k, 3)
            row_max(k, 4)
            if has_front:
                latent_scale(k + 1)
            row_max(k, 5)
            max_columns(k)
            add_max(k, par)
            if has_front:
                rotate(k + 1)
                v_copy(k + 1, 1 - par)
            if has_tail:
                residual(k - 1)
            if has_front:
                round_lo(k + 1)
            if has_tail:
                norm_write(c, e, dve, k - 1)
            if has_front:
                q_copy(k + 1, 1 - par)

        def sigmoid_step(k, par, has_tail, has_front):
            if has_front:
                rotate(k + 1)
            if has_tail:
                context(k - 1)
            if has_front:
                round_lo(k + 1)
                q_copy(k + 1, 1 - par)
                v_copy(k + 1, 1 - par)
            if has_tail:
                residual(k - 1)
                norm_write(c, e, dve, k - 1)

        pipeline(dve, front, {"rope": rope_step, "latent": latent_step, "sigmoid": sigmoid_step}[kind], tail)


class ChannelMix:

    def __init__(self, c, name, w):
        self.c, self.w = c, w
        self.e = c.events(zero=1, xin=1, xt_ps=1, xt=1, mixed=2, xk=1, xr=1, k_ps=1, relu=1, act=1,
                          r_ps=1, v_ps=1, gate=1, gated=1, xres=1, **LN_EVENTS)

    def banks(self, par):
        c = self.c
        return [c.S[:, 0, 0], c.S[:, 0, 1], c.S[:, 1, 0], c.S[:, 1, 1]] if par else \
               [c.A[:, 0], c.A[:, 1], c.O[:, 0], c.O[:, 1]]

    def pool(self, pool):
        c, e = self.c, self.e

        def tail(s, par):
            if begun(s - 1):
                count = held(pool, e["res"].at(s - 1))
                pool.wait_ge(c.made, 1)
                pool.wait_ge(e["res"].sem, count)
            pool.tensor_copy(c.xres[:], c.X[:, s]).then_inc(e["xres"].sem, 1)
            norm_rstd(c, e, pool, s)

        def step(k, par, has_tail, has_front):
            if has_tail:
                tail(k - 1, 1 - par)

        pipeline(pool, lambda s, par: None, step, tail)

    def pe(self, pe):
        c, e, w = self.c, self.e, self.w

        def front(s, par):
            pe.wait_ge(e["xin"].sem, e["xin"].at(s))
            if begun(s - 2):
                pe.wait_ge(e["xt"].sem, e["xt"].at(s - 2))
            for t in range(T):
                mm = pe.transpose(self.banks(par)[0][:, t * P:(t + 1) * P], c.xin[:, par, t, :], c.ident[:])
            mm.then_inc(e["xt_ps"].sem, 1)

        def middle(s, par):
            xT, k, r, v = self.banks(par)
            pe.wait_ge(e["xk"].sem, e["xk"].at(s))
            if begun(s - 2):
                pe.wait_ge(e["relu"].sem, e["relu"].at(s - 2))
            pe.matmul(k[:, 0:L], w["wk"][:], w["xk"][:, par], start=True, stop=True).then_inc(e["k_ps"].sem, 1)
            pe.wait_ge(e["xr"].sem, e["xr"].at(s))
            if begun(s - 2):
                pe.wait_ge(e["gate"].sem, e["gate"].at(s - 2))
            for t in range(T):
                mm = pe.matmul(r[:, t * P:(t + 1) * P], w["xr"][:, par, t * P:(t + 1) * P], w["wr"][:], start=True, stop=True)
            mm.then_inc(e["r_ps"].sem, 1)

        def tail(s, par):
            xT, k, r, v = self.banks(par)
            pe.wait_ge(e["act"].sem, e["act"].at(s))
            if begun(s - 2):
                pe.wait_ge(e["gated"].sem, e["gated"].at(s - 2))
            for t in range(T):
                mm = pe.matmul(v[:, t * P:(t + 1) * P], w["kact"][:, par, t * P:(t + 1) * P], w["wv"][:], start=True, stop=True)
            mm.then_inc(e["v_ps"].sem, 1)

        def step(k, par, has_tail, has_front):
            if has_front:
                front(k + 1, 1 - par)
            middle(k, par)
            if has_tail:
                tail(k - 1, 1 - par)

        pipeline(pe, front, step, tail)

    def act(self, act):
        c, e, w = self.c, self.e, self.w
        act.mul(w["xTs"][:, :, 0:1], c.ones[:, 0:2].unsqueeze(2), 0.0).then_inc(e["zero"].sem, 1)

        def front(s, par):
            act.wait_ge(e["xt_ps"].sem, e["xt_ps"].at(s))
            if begun(s - 2):
                act.wait_ge(e["xk"].sem, e["xk"].at(s - 2))
            if begun(s - 2):
                act.wait_ge(e["xr"].sem, e["xr"].at(s - 2))
            act.copy(w["xTs"][:, par, 1:L + 1], self.banks(par)[0][:, 0:L]).then_inc(e["xt"].sem, 1)

        def first(s, par):
            copy_in(c, e, act, s, par)
            front(s, par)

        def middle(s, par):
            act.wait_ge(e["k_ps"].sem, e["k_ps"].at(s))
            if begun(s - 1):
                act.wait_ge(e["act"].sem, e["act"].at(s - 1))
            act.activation(w["relu"][:], self.banks(par)[1][:, 0:L], ACT.Relu).then_inc(e["relu"].sem, 1)
            act.wait_ge(e["relu"].sem, e["relu"].at(s))
            if begun(s - 2):
                act.wait_ge(e["v_ps"].sem, e["v_ps"].at(s - 2))
            act.activation(w["kact"][:, par], w["relu"][:], ACT.Square).then_inc(e["act"].sem, 1)
            act.wait_ge(e["r_ps"].sem, e["r_ps"].at(s))
            if begun(s - 2):
                act.wait_ge(e["gated"].sem, e["gated"].at(s - 2))
            act.activation(w["tanh"][:, par], self.banks(par)[2][:, 0:L], ACT.Tanh, scale=0.5).then_inc(e["gate"].sem, 1)

        def step(k, par, has_tail, has_front):
            if has_front:
                first(k + 1, 1 - par)
            middle(k, par)

        pipeline(act, first, step, lambda s, par: None)

    def dve(self, dve):
        c, e, w = self.c, self.e, self.w
        dve.wait_ge(e["zero"].sem, e["zero"].at(0))

        def front(s, par):
            dve.wait_ge(e["xt"].sem, e["xt"].at(s))
            if begun(s - 1):
                dve.wait_ge(e["xk"].sem, e["xk"].at(s - 1))
            if begun(s - 1):
                dve.wait_ge(e["xr"].sem, e["xr"].at(s - 1))
            for j in range(2):
                dve.tensor_scalar(w["mixed"][:, j], w["xTs"][:, par, 1:L + 1], w["mu"][:, j:j + 1], None, ALU.mult)\
                   .then_inc(e["mixed"].sem, 1)
            dve.wait_ge(e["mixed"].sem, e["mixed"].at(s, 1))
            if begun(s - 2):
                dve.wait_ge(e["k_ps"].sem, e["k_ps"].at(s - 2))
            dve.scalar_tensor_tensor(w["xk"][:, par], w["xTs"][:, par, 0:L], w["nu"][:, 0:1], w["mixed"][:, 0],
                                     ALU.mult, ALU.add).then_inc(e["xk"].sem, 1)
            dve.wait_ge(e["mixed"].sem, e["mixed"].at(s, 2))
            if begun(s - 2):
                dve.wait_ge(e["r_ps"].sem, e["r_ps"].at(s - 2))
            dve.scalar_tensor_tensor(w["xr"][:, par], w["xTs"][:, par, 0:L], w["nu"][:, 1:2], w["mixed"][:, 1],
                                     ALU.mult, ALU.add).then_inc(e["xr"].sem, 1)

        def tail(s, par):
            dve.wait_ge(e["v_ps"].sem, e["v_ps"].at(s))
            dve.wait_ge(e["gate"].sem, e["gate"].at(s))
            if begun(s - 1):
                dve.wait_ge(e["res"].sem, e["res"].at(s - 1))
            dve.scalar_tensor_tensor(w["gated"][:], w["tanh"][:, par], 1.0, self.banks(par)[3][:, 0:L],
                                     ALU.add, ALU.mult).then_inc(e["gated"].sem, 1)
            dve.wait_ge(e["gated"].sem, e["gated"].at(s))
            dve.wait_ge(e["xres"].sem, e["xres"].at(s))
            if begun(s - 1):
                dve.wait_ge(e["x"].sem, e["x"].at(s - 1))
            dve.scalar_tensor_tensor(c.res[:].rearrange("p t d -> p (t d)"), w["gated"][:], 0.5,
                                     c.xres[:].rearrange("p t d -> p (t d)"), ALU.mult, ALU.add).then_inc(e["res"].sem, 1)
            norm_stats(c, e, dve, s)

        def last_tail(s, par):
            norm_write(c, e, dve, s - 1)
            tail(s, par)
            norm_write(c, e, dve, s)

        def step(k, par, has_tail, has_front):
            if has_front:
                front(k + 1, 1 - par)
            if has_tail and begun(k - 2):
                norm_write(c, e, dve, k - 2)
            if has_tail:
                tail(k - 1, 1 - par)

        pipeline(dve, front, step, last_tail)


class LinearAttention:

    def __init__(self, c, name, w):
        self.c, self.w = c, w
        self.e = c.events(xin=1, xt_ps=1, xt=1, q_ps=1, q=1, kv_ps=1, kv=T, g_ps=1, g=1,
                          o_ps=1, o=1, out_ps=1, xres=1, **LN_EVENTS)

    banks = ChannelMix.banks

    def pool(self, pool):
        c, e, w = self.c, self.e, self.w

        def tail(s, par):
            if begun(s - 1):
                count = held(pool, e["res"].at(s - 1))
                pool.wait_ge(c.made, 1)
                pool.wait_ge(e["res"].sem, count)
            pool.tensor_tensor(c.xres[:], c.X[:, s], w["bo"][:].unsqueeze(1).broadcast_to((P, T, P)), ALU.add).then_inc(e["xres"].sem, 1)
            norm_rstd(c, e, pool, s)

        def step(k, par, has_tail, has_front):
            if has_tail:
                tail(k - 1, 1 - par)

        pipeline(pool, lambda s, par: None, step, tail)

    def pe(self, pe):
        c, e, w = self.c, self.e, self.w

        def front(s, par):
            b = self.banks(par)
            pe.wait_ge(e["xin"].sem, e["xin"].at(s))
            if begun(s - 2):
                pe.wait_ge(e["g"].sem, e["g"].at(s - 2))
            for t in range(T):
                mm = pe.transpose(b[0][:, t * P:(t + 1) * P], c.xin[:, par, t, :], c.ident[:])
            mm.then_inc(e["xt_ps"].sem, 1)

        def middle(s, par):
            b = self.banks(par)
            pe.wait_ge(e["xt"].sem, e["xt"].at(s))
            if begun(s - 2):
                pe.wait_ge(e["o"].sem, e["o"].at(s - 2))
            pe.matmul(b[1][:, 0:L], w["wq"][:], w["xT"][:, par], start=True, stop=True).then_inc(e["q_ps"].sem, 1)
            if begun(s - 2):
                pe.wait_ge(e["res"].sem, e["res"].at(s - 2))
            for t in range(T):
                mm = pe.matmul(b[2 + t][:, 0:2 * P], w["xT"][:, par, t * P:(t + 1) * P], w["wkv"][:], start=True, stop=True)
            mm.then_inc(e["kv_ps"].sem, 1)

        def products(s, par):
            b = self.banks(par)
            pe.wait_ge(e["kv"].sem, e["kv"].at(s))
            for t in range(T):
                mm = pe.matmul(b[0][:, 0:P], w["kv"][:, par, t, 0:P], w["kv"][:, par, t, P:2 * P],
                               start=t == 0, stop=t == T - 1)
            mm.then_inc(e["g_ps"].sem, 1)

        def weighted(s, par):
            b = self.banks(par)
            pe.wait_ge(e["g"].sem, e["g"].at(s))
            pe.wait_ge(e["q"].sem, e["q"].at(s))
            pe.matmul(b[1][:, 0:L], w["g"][:], w["q"][:, par], start=True, stop=True).then_inc(e["o_ps"].sem, 1)

        def output(s, par):
            b = self.banks(par)
            pe.wait_ge(e["o"].sem, e["o"].at(s))
            for t in range(T):
                mm = pe.matmul(b[2][:, t * P:(t + 1) * P], w["oT"][:, t * P:(t + 1) * P], w["wo"][:], start=True, stop=True)
            mm.then_inc(e["out_ps"].sem, 1)

        def step(k, par, has_tail, has_front):
            if has_tail:
                products(k - 1, 1 - par)
            middle(k, par)
            if has_tail:
                weighted(k - 1, 1 - par)
            if has_front:
                front(k + 1, 1 - par)
            if has_tail:
                output(k - 1, 1 - par)

        def tail(s, par):
            products(s, par)
            weighted(s, par)
            output(s, par)

        pipeline(pe, front, step, tail)

    def act(self, act):
        c, e, w = self.c, self.e, self.w

        def front(s, par):
            act.wait_ge(e["xt_ps"].sem, e["xt_ps"].at(s))
            if begun(s - 2):
                act.wait_ge(e["kv_ps"].sem, e["kv_ps"].at(s - 2))
            act.copy(w["xT"][:, par], self.banks(par)[0][:, 0:L]).then_inc(e["xt"].sem, 1)

        def first(s, par):
            copy_in(c, e, act, s, par)
            front(s, par)

        def middle(s, par):
            act.wait_ge(e["q_ps"].sem, e["q_ps"].at(s))
            if begun(s - 2):
                act.wait_ge(e["o_ps"].sem, e["o_ps"].at(s - 2))
            act.activation(w["q"][:, par], self.banks(par)[1][:, 0:L], ACT.Identity, bias=w["bq"][:]).then_inc(e["q"].sem, 1)

        def tail(s, par):
            act.wait_ge(e["o_ps"].sem, e["o_ps"].at(s))
            if begun(s - 1):
                act.wait_ge(e["out_ps"].sem, e["out_ps"].at(s - 1))
            act.copy(w["oT"][:], self.banks(par)[1][:, 0:L]).then_inc(e["o"].sem, 1)

        def step(k, par, has_tail, has_front):
            if has_front:
                copy_in(c, e, act, k + 1, 1 - par)
            middle(k, par)
            if has_tail:
                tail(k - 1, 1 - par)
            if has_front:
                front(k + 1, 1 - par)

        pipeline(act, first, step, tail)

    def dve(self, dve):
        c, e, w = self.c, self.e, self.w

        def middle(s, par):
            dve.wait_ge(e["kv_ps"].sem, e["kv_ps"].at(s))
            if begun(s - 2):
                dve.wait_ge(e["g_ps"].sem, e["g_ps"].at(s - 2))
            for t in range(T):
                dve.tensor_tensor(w["kv"][:, par, t], self.banks(par)[2 + t][:, 0:2 * P], w["bkv"][:], ALU.add)\
                   .then_inc(e["kv"].sem, 1)

        def own_blocks(s, par):
            b = self.banks(par)
            dve.wait_ge(e["g_ps"].sem, e["g_ps"].at(s))
            if begun(s - 1):
                dve.wait_ge(e["o_ps"].sem, e["o_ps"].at(s - 1))
            dve.tensor_tensor(w["g"][:], b[0][:, 0:P], w["blocks"][:], ALU.mult).then_inc(e["g"].sem, 1)

        def residual(s, par):
            b = self.banks(par)
            dve.wait_ge(e["out_ps"].sem, e["out_ps"].at(s))
            dve.wait_ge(e["xres"].sem, e["xres"].at(s))
            if begun(s - 1):
                dve.wait_ge(e["x"].sem, e["x"].at(s - 1))
            dve.tensor_tensor(c.res[:].rearrange("p t d -> p (t d)"), b[2][:, 0:L],
                              c.xres[:].rearrange("p t d -> p (t d)"), ALU.add).then_inc(e["res"].sem, 1)
            norm_stats(c, e, dve, s)

        def last_tail(s, par):
            norm_write(c, e, dve, s - 1)
            own_blocks(s, par)
            residual(s, par)
            norm_write(c, e, dve, s)

        def step(k, par, has_tail, has_front):
            if has_tail:
                own_blocks(k - 1, 1 - par)
            middle(k, par)
            if has_tail and begun(k - 2):
                norm_write(c, e, dve, k - 2)
            if has_tail:
                residual(k - 1, 1 - par)

        pipeline(dve, lambda s, par: None, step, last_tail)


class Mlp:

    def __init__(self, c, name, w, out):
        self.c, self.w, self.out = c, w, out
        self.e = c.events(xin=1, xt_ps=1, xt=1, h_ps=2, ha=2, hd=2, y_ps=1, xres=1, stored=16, **LN_EVENTS)

    banks = ChannelMix.banks

    def pool(self, pool):
        c, e, w = self.c, self.e, self.w

        def tail(s, par):
            if begun(s - 1):
                count = held(pool, e["res"].at(s - 1))
                pool.wait_ge(c.made, 1)
                pool.wait_ge(e["res"].sem, count)
            pool.tensor_tensor(c.xres[:], c.X[:, s], w["b2"][:].unsqueeze(1).broadcast_to((P, T, P)), ALU.add).then_inc(e["xres"].sem, 1)
            norm_rstd(c, e, pool, s)

        def step(k, par, has_tail, has_front):
            if has_tail:
                tail(k - 1, 1 - par)

        pipeline(pool, lambda s, par: None, step, tail)

    def sync(self, sp):
        c, e = self.c, self.e
        with sp.Fori(0, B) as s:
            sp.wait_ge(e["x"].sem, e["x"].at(s))
            sp.dma_start(self.out[s].rearrange("(t p) d -> p t d", t=T), c.X[:, s]).then_inc(e["stored"].sem, 16)
        sp.wait_ge(e["stored"].sem, e["stored"].at(B - 1))

    def pe(self, pe):
        c, e, w = self.c, self.e, self.w

        def front(s, par):
            b = self.banks(par)
            pe.wait_ge(e["xin"].sem, e["xin"].at(s))
            if begun(s - 2):
                pe.wait_ge(e["xt"].sem, e["xt"].at(s - 2))
            for t in range(T):
                mm = pe.transpose(b[0][:, t * P:(t + 1) * P], c.xin[:, par, t, :], c.ident[:])
            mm.then_inc(e["xt_ps"].sem, 1)

        def middle(s, par):
            b = self.banks(par)
            pe.wait_ge(e["xt"].sem, e["xt"].at(s))
            if begun(s - 2):
                pe.wait_ge(e["ha"].sem, e["ha"].at(s - 2))
            if begun(s - 2):
                pe.wait_ge(e["hd"].sem, e["hd"].at(s - 2))
            for j in range(4):
                mm = pe.matmul(b[2 + j // 2][:, (j % 2) * L:(j % 2 + 1) * L], w["w1"][:, j * P:(j + 1) * P], w["xT"][:, par],
                               start=True, stop=True)
                if j % 2:
                    mm.then_inc(e["h_ps"].sem, 1)

        def tail(s, par):
            b = self.banks(par)
            pe.wait_ge(e["ha"].sem, e["ha"].at(s))
            pe.wait_ge(e["hd"].sem, e["hd"].at(s))
            if begun(s - 2):
                pe.wait_ge(e["res"].sem, e["res"].at(s - 2))
            for t in range(T):
                for j in range(4):
                    mm = pe.matmul(b[1][:, t * P:(t + 1) * P], w["h"][:, par, j, t * P:(t + 1) * P], w["w2"][:, j],
                                   start=j == 0, stop=j == 3)
            mm.then_inc(e["y_ps"].sem, 1)

        def step(k, par, has_tail, has_front):
            middle(k, par)
            if has_front:
                front(k + 1, 1 - par)
            if has_tail:
                tail(k - 1, 1 - par)

        pipeline(pe, front, step, tail)

    def act(self, act):
        c, e, w = self.c, self.e, self.w

        def front(s, par):
            act.wait_ge(e["xt_ps"].sem, e["xt_ps"].at(s))
            if begun(s - 2):
                act.wait_ge(e["h_ps"].sem, e["h_ps"].at(s - 2))
            act.copy(w["xT"][:, par], self.banks(par)[0][:, 0:L]).then_inc(e["xt"].sem, 1)

        def first(s, par):
            copy_in(c, e, act, s, par)
            front(s, par)

        def middle(s, par):
            act.wait_ge(e["h_ps"].sem, e["h_ps"].at(s, 1))
            if begun(s - 2):
                act.wait_ge(e["y_ps"].sem, e["y_ps"].at(s - 2))
            for j in range(2):
                act.activation(w["h"][:, par, j], self.banks(par)[2][:, j * L:(j + 1) * L], ACT.Relu,
                               bias=w["b1"][:, j:j + 1]).then_inc(e["ha"].sem, 1)

        def step(k, par, has_tail, has_front):
            if has_front:
                copy_in(c, e, act, k + 1, 1 - par)
            middle(k, par)
            if has_front:
                front(k + 1, 1 - par)

        pipeline(act, first, step, lambda s, par: None)

    def dve(self, dve):
        c, e, w = self.c, self.e, self.w

        def middle(s, par):
            dve.wait_ge(e["h_ps"].sem, e["h_ps"].at(s, 2))
            if begun(s - 2):
                dve.wait_ge(e["y_ps"].sem, e["y_ps"].at(s - 2))
            for j in range(2, 4):
                dve.tensor_scalar(w["h"][:, par, j], self.banks(par)[3][:, (j - 2) * L:(j - 1) * L], w["b1"][:, j:j + 1],
                                  0.0, ALU.add, ALU.max).then_inc(e["hd"].sem, 1)

        def tail(s, par):
            dve.wait_ge(e["y_ps"].sem, e["y_ps"].at(s))
            dve.wait_ge(e["xres"].sem, e["xres"].at(s))
            if begun(s - 1):
                dve.wait_ge(e["x"].sem, e["x"].at(s - 1))
            dve.tensor_tensor(c.res[:].rearrange("p t d -> p (t d)"), self.banks(par)[1][:, 0:L],
                              c.xres[:].rearrange("p t d -> p (t d)"), ALU.add).then_inc(e["res"].sem, 1)
            norm_stats(c, e, dve, s)

        def last_tail(s, par):
            norm_write(c, e, dve, s - 1)
            tail(s, par)
            norm_write(c, e, dve, s)

        def step(k, par, has_tail, has_front):
            middle(k, par)
            if has_tail and begun(k - 2):
                norm_write(c, e, dve, k - 2)
            if has_tail:
                tail(k - 1, 1 - par)

        pipeline(dve, lambda s, par: None, step, last_tail)


class Experts:

    def __init__(self, c, name, layer, w):
        self.c, self.layer, self.w = c, layer, w
        self.NJ = w["hidden"] // P
        self.NA = 2
        self.ND = self.NJ - self.NA
        self.NG = 18 if layer == 0 else 17
        self.e = c.events(xin=1, xt_ps=1, xt=1, lg_ps=1, d=1, ex=1, gate=self.NG, sc=1, z=T, z_ps=1, zT=1,
                          wt_ps=1, wt=1, b_ps=1, acc0=1, zhi=1, zlo=1, h_ps=NE, ha=NE * self.NA, hd=NE * self.ND,
                          y_ps=NE, acc=NE - 1, xres=1, **LN_EVENTS)

        c, hidden = self.c, w["hidden"]
        stacks = [t[:].rearrange("p n g l -> p (n g l)") for t in (c.QS, c.KS)]
        each = 2 * G * L // hidden
        self.w1_hi = [stacks[x // each][:, (x % each) * hidden:(x % each + 1) * hidden] for x in range(NE)]
        self.w1_lo = [w["w1_lo"][:, x * hidden:(x + 1) * hidden] for x in range(NE)]
        self.hi_made, self.lo_made = c.sem(f"w1_hi_{layer}"), c.sem(f"w1_lo_{layer}")

    def split_hi(self, act, attention, loaded, loads):
        act.wait_ge(loaded, loads)
        act.wait_ge(attention["p2"].sem, attention["p2"].at(B - 1))
        if self.layer == 0:
            act.wait_ge(attention["qm"].sem, attention["qm"].at(B - 1))
        for x in range(NE):
            act.copy(self.w1_hi[x], self.w["w1"][:, x, :]).then_inc(self.hi_made, 1)

    def split_lo(self, dve):
        for x in range(NE):
            dve.wait_ge(self.hi_made, x + 1)
            dve.tensor_tensor(self.w1_lo[x], self.w["w1"][:, x, :], self.w1_hi[x].bitcast(F32),
                              ALU.subtract).then_inc(self.lo_made, 1)

    def pool(self, pool):
        c, e = self.c, self.e

        def front(s, par):
            if begun(s - 2):
                count = held(pool, e["xt_ps"].at(s - 2))
                pool.wait_ge(c.made, 1)
                pool.wait_ge(e["xt_ps"].sem, count)
            if self.layer == 0:
                if begun(s - 2):
                    count = held(pool, e["z"].at(s - 2))
                    pool.wait_ge(c.made, 1)
                    pool.wait_ge(e["z"].sem, count)
            pool.tensor_copy(c.xin[:, par], c.X[:, s]).then_inc(e["xin"].sem, 1)

        def keep(s):
            if begun(s - 1):
                count = held(pool, e["acc0"].at(s - 1))
                pool.wait_ge(c.made, 1)
                pool.wait_ge(e["acc0"].sem, count)
            pool.tensor_copy(c.xres[:], c.X[:, s]).then_inc(e["xres"].sem, 1)

        def step(k, par, has_tail, has_front):
            if has_front:
                front(k + 1, 1 - par)
            if has_tail:
                norm_rstd(c, e, pool, k - 1)
            if has_front:
                keep(k + 1)

        def whole_front(s, par):
            front(s, par)
            keep(s)

        pipeline(pool, whole_front, step, lambda s, par: norm_rstd(c, e, pool, s))

    def pe(self, pe):
        c, e, w, NJ = self.c, self.e, self.w, self.NJ

        def front(s, par, n):
            if n == 0:
                pe.wait_ge(e["xin"].sem, e["xin"].at(s))
                if self.layer == 0:
                    if begun(s - 1):
                        pe.wait_ge(e["zT"].sem, e["zT"].at(s - 1))
                for t in range(T):
                    mm = pe.transpose(c.A[:, 0, t * P:(t + 1) * P], c.xin[:, par, t, :], c.ident[:])
                mm.then_inc(e["xt_ps"].sem, 1)
            elif n == 1:
                pe.wait_ge(e["xt"].sem, e["xt"].at(s))
                if begun(s - 1):
                    pe.wait_ge(e["acc0"].sem, e["acc0"].at(s - 1))
                xT = c.xT if self.layer == 0 else w["zT"][:, par]
                for t in range(T):
                    mm = pe.matmul(c.A[:, 1, t * NE:(t + 1) * NE], xT[:, t * P:(t + 1) * P], w["gate"][:],
                                   start=True, stop=True)
                mm.then_inc(e["lg_ps"].sem, 1)
            elif n == 2:
                if self.layer == 0:
                    pe.wait_ge(e["z"].sem, e["z"].at(s))
                    for t in range(T):
                        mm = pe.transpose(c.A[:, 0, t * P:(t + 1) * P], w["z"][:, t, :], c.ident[:])
                    mm.then_inc(e["z_ps"].sem, 1)
                pe.wait_ge(e["sc"].sem, e["sc"].at(s))
                for t in range(T):
                    mm = pe.transpose(c.A[0:NE, 1, t * P:(t + 1) * P], w["sc"][:, par, t, :], c.ident[:])
                mm.then_inc(e["wt_ps"].sem, 1)
            else:
                pe.wait_ge(e["wt"].sem, e["wt"].at(s))
                for t in range(T):
                    mm = pe.matmul(c.A[:, 1, t * P:(t + 1) * P], w["wT"][:, t * P:(t + 1) * P], w["b2"][:], start=True, stop=True)
                mm.then_inc(e["b_ps"].sem, 1)

        def hidden(s, par, x):
            if x == 0:
                pe.wait_ge(e["zhi"].sem, e["zhi"].at(s))
                pe.wait_ge(e["zlo"].sem, e["zlo"].at(s))
            if isinstance(s, int) and s == 0:
                pe.wait_ge(self.lo_made, x + 1)
            if x >= 2:
                pe.wait_ge(e["ha"].sem, e["ha"].at(s, (x - 1) * self.NA))
                if self.ND:
                    pe.wait_ge(e["hd"].sem, e["hd"].at(s, (x - 1) * self.ND))
            else:
                if begun(s - 1):
                    pe.wait_ge(e["ha"].sem, e["ha"].at(s - 1, (NE + x - 1) * self.NA))
                if self.ND and begun(s - 1):
                    pe.wait_ge(e["hd"].sem, e["hd"].at(s - 1, (NE + x - 1) * self.ND))
            for j in range(NJ):
                bank, col = self.place(j)
                out, chunk = c.S[:, x % 2, bank, col:col + L], slice(j * P, (j + 1) * P)
                pe.matmul(out, self.w1_hi[x][:, chunk], c.hi[:, par], start=True, stop=False)
                pe.matmul(out, self.w1_hi[x][:, chunk], c.lo[:, par], start=False, stop=False)
                mm = pe.matmul(out, self.w1_lo[x][:, chunk], c.hi[:, par], start=False, stop=True)
            mm.then_inc(e["h_ps"].sem, 1)

        def output(s, x):
            pe.wait_ge(e["ha"].sem, e["ha"].at(s, (x + 1) * self.NA))
            if self.ND:
                pe.wait_ge(e["hd"].sem, e["hd"].at(s, (x + 1) * self.ND))
            if x >= 2:
                pe.wait_ge(e["acc"].sem, e["acc"].at(s, x - 1))
            else:
                added = e["acc"] if x == 0 else e["res"]
                if begun(s - 1):
                    pe.wait_ge(added.sem, added.at(s - 1))
            for t in range(T):
                for j in range(NJ):
                    mm = pe.matmul(c.O[:, x % 2, t * P:(t + 1) * P], w["h"][:, x % 2, j, t * P:(t + 1) * P],
                                   w["w2"][:, x * NJ + j], start=j == 0, stop=j == NJ - 1)
            mm.then_inc(e["y_ps"].sem, 1)

        def whole_front(s, par):
            for n in range(4):
                front(s, par, n)

        def step(k, par, has_tail, has_front):
            for x in range(NE):
                hidden(k, par, x)
                if x > 0:
                    output(k, x - 1)
                if has_front and x in (0, 1, 7):
                    front(k + 1, 1 - par, (0, 1, 7).index(x))
            output(k, NE - 1)
            if has_front:
                front(k + 1, 1 - par, 3)

        pipeline(pe, whole_front, step, lambda s, par: None)

    def place(self, j):
        return (0, j * L) if j < self.NA else (1, (j - self.NA) * L)

    def act(self, act):
        c, e, w = self.c, self.e, self.w

        def front(s, par, n):
            if n == 0:
                act.wait_ge(e["xt_ps"].sem, e["xt_ps"].at(s))
                if self.layer == 0:
                    if begun(s - 1):
                        act.wait_ge(e["lg_ps"].sem, e["lg_ps"].at(s - 1))
                    act.copy(c.xT[:], c.A[:, 0, 0:L]).then_inc(e["xt"].sem, 1)
                else:
                    if begun(s - 2):
                        act.wait_ge(e["zlo"].sem, e["zlo"].at(s - 2))
                    act.copy(w["zT"][:, par], c.A[:, 0, 0:L]).then_inc(e["xt"].sem, 1)
            elif n == 1:
                act.wait_ge(e["d"].sem, e["d"].at(s))
                act.activation(w["ex"][:], w["d"][:], ACT.Exp).then_inc(e["ex"].sem, 1)
            else:
                if self.layer == 0:
                    act.wait_ge(e["z_ps"].sem, e["z_ps"].at(s))
                    if begun(s - 2):
                        act.wait_ge(e["zlo"].sem, e["zlo"].at(s - 2))
                    act.copy(w["zT"][:, par], c.A[:, 0, 0:L]).then_inc(e["zT"].sem, 1)
                whole = e["zT"] if self.layer == 0 else e["xt"]
                act.wait_ge(whole.sem, whole.at(s))
                if begun(s - 2):
                    act.wait_ge(e["h_ps"].sem, e["h_ps"].at(s - 2))
                act.copy(c.hi[:, par], w["zT"][:, par]).then_inc(e["zhi"].sem, 1)
                act.wait_ge(e["wt_ps"].sem, e["wt_ps"].at(s))
                if begun(s - 1):
                    act.wait_ge(e["b_ps"].sem, e["b_ps"].at(s - 1))
                act.copy(w["wT"][:], c.A[0:NE, 1, 0:L]).then_inc(e["wt"].sem, 1)

        def relu(s, x):
            act.wait_ge(e["h_ps"].sem, e["h_ps"].at(s, x + 1))
            if x >= 2:
                act.wait_ge(e["y_ps"].sem, e["y_ps"].at(s, x - 1))
            else:
                if begun(s - 1):
                    act.wait_ge(e["y_ps"].sem, e["y_ps"].at(s - 1, NE + x - 1))
            for j in range(self.NA):
                bank, col = self.place(j)
                act.activation(w["h"][:, x % 2, j], c.S[:, x % 2, bank, col:col + L], ACT.Relu,
                               bias=w["b1"][:, x * self.NJ + j:x * self.NJ + j + 1]).then_inc(e["ha"].sem, 1)

        def whole_front(s, par):
            for n in range(3):
                front(s, par, n)

        def step(k, par, has_tail, has_front):
            for x in range(NE):
                relu(k, x)
                if has_front and x in (0, 2, 7):
                    front(k + 1, 1 - par, (0, 2, 7).index(x))

        pipeline(act, whole_front, step, lambda s, par: None)

    def dve(self, dve):
        c, e, w, NJ = self.c, self.e, self.w, self.NJ

        def bc(col):
            return col.unsqueeze(2).broadcast_to((P, T, NE))

        def gate(s, par, part):
            n = (0, 2, 5, 9, 13, 17)[part]

            def link(ins):
                nonlocal n
                n += 1
                ins.then_inc(e["gate"].sem, 1)
                count = held(dve, e["gate"].at(s, n))
                dve.wait_ge(c.made, 1)
                dve.wait_ge(e["gate"].sem, count)

            if part == 0:
                dve.wait_ge(e["lg_ps"].sem, e["lg_ps"].at(s))
                lg = c.A[:, 1, 0:T * NE].rearrange("p (t x) -> p t x", x=NE)
                if begun(s - 1):
                    dve.wait_ge(e["ex"].sem, e["ex"].at(s - 1))
                link(dve.tensor_tensor(w["lg"][:], lg, w["bg"][:].unsqueeze(1).broadcast_to((P, T, NE)), ALU.add))
                link(dve.tensor_reduce(w["top"][:], w["lg"][:], AX.X, ALU.max, negate=True))
                dve.tensor_tensor(w["d"][:], w["lg"][:], bc(w["top"][:]), ALU.add).then_inc(e["d"].sem, 1)
            elif part == 1:
                dve.wait_ge(e["ex"].sem, e["ex"].at(s))
                link(dve.tensor_reduce(w["total"][:], w["ex"][:], AX.X, ALU.add))
                link(dve.reciprocal(w["inv"][:], w["total"][:]))
                link(dve.tensor_tensor(w["pr"][:], w["ex"][:], bc(w["inv"][:]), ALU.mult))
            elif part == 2:
                for t in range(T):
                    link(dve.max(w["v8"][:, t, :], w["pr"][:, t, :]))
                for t in range(T):
                    link(dve.max_index(w["i8"][:, t, :], w["v8"][:, t, :], w["pr"][:, t, :]))
            elif self.layer == 0:
                blend_one(s, par, part, link)
            else:
                blend_two(s, par, part, link)

        def picks():
            return w["v8"][:, :, 0], w["v8"][:, :, 1], w["f8"][:, :, 0], w["f8"][:, :, 1]

        def blend_one(s, par, part, link):
            v1, v2, i1, i2 = picks()
            if part == 3:
                link(dve.tensor_copy(w["f8"][:], w["i8"][:]))
                link(dve.tensor_tensor(w["g"][:, 0], i2, i1, ALU.is_gt))
                link(dve.scalar_tensor_tensor(w["g"][:, 1], v2, 0.0, w["g"][:, 0], ALU.is_gt, ALU.mult))
                link(dve.tensor_scalar(w["g"][:, 2], w["g"][:, 1], -1.0, 1.0, ALU.mult, ALU.add))
            elif part == 4:
                link(dve.tensor_tensor(w["g"][:, 3], v1, w["g"][:, 2], ALU.mult))
                link(dve.tensor_tensor(w["g"][:, 4], v2, w["g"][:, 1], ALU.mult))
                link(dve.tensor_tensor(w["g"][:, 5], w["g"][:, 3], w["g"][:, 4], ALU.add))
                link(dve.tensor_tensor(w["g"][:, 6], i2, w["g"][:, 1], ALU.mult))
            else:
                link(dve.tensor_tensor(w["g"][:, 7], w["g"][:, 6], i1, ALU.max))
                sc_free(s)
                dve.tensor_tensor(w["sc"][:, par], w["iota"][:].unsqueeze(1).broadcast_to((P, T, NE)), bc(w["g"][:, 7]),
                                  ALU.is_equal).then_inc(e["sc"].sem, 1)
                if begun(s - 1):
                    dve.wait_ge(e["z_ps"].sem, e["z_ps"].at(s - 1))
                for t in range(T):
                    dve.tensor_scalar(w["z"][:, t, :], c.xin[:, par, t, :], w["g"][:, 5, t:t + 1], None, ALU.mult)\
                       .then_inc(e["z"].sem, 1)

        def blend_two(s, par, part, link):
            v1, v2, i1, i2 = picks()
            iota = w["iota"][:].unsqueeze(1).broadcast_to((P, T, NE))
            if part == 3:
                link(dve.tensor_copy(w["f8"][:], w["i8"][:]))
                link(dve.tensor_tensor(w["g"][:, 0], v1, v2, ALU.add))
                link(dve.reciprocal(w["g"][:, 1], w["g"][:, 0]))
                link(dve.tensor_tensor(w["oh"][:, 0], iota, bc(i1), ALU.is_equal))
            elif part == 4:
                link(dve.tensor_tensor(w["oh"][:, 1], iota, bc(i2), ALU.is_equal))
                link(dve.tensor_tensor(w["oh"][:, 2], w["oh"][:, 0], bc(v1), ALU.mult))
                link(dve.tensor_tensor(w["oh"][:, 3], w["oh"][:, 1], bc(v2), ALU.mult))
                link(dve.tensor_tensor(w["oh"][:, 4], w["oh"][:, 2], w["oh"][:, 3], ALU.add))
            else:
                sc_free(s)
                dve.tensor_tensor(w["sc"][:, par], w["oh"][:, 4], bc(w["g"][:, 1]), ALU.mult).then_inc(e["sc"].sem, 1)

        def sc_free(s):
            if begun(s - 2):
                dve.wait_ge(e["wt_ps"].sem, e["wt_ps"].at(s - 2))
            if begun(s - 2):
                dve.wait_ge(e["res"].sem, e["res"].at(s - 2))

        def start_sum(s):
            dve.wait_ge(e["b_ps"].sem, e["b_ps"].at(s))
            dve.wait_ge(e["xres"].sem, e["xres"].at(s))
            dve.tensor_tensor(w["acc0"][:].rearrange("p t d -> p (t d)"), c.A[:, 1, 0:L],
                              c.xres[:].rearrange("p t d -> p (t d)"), ALU.add).then_inc(e["acc0"].sem, 1)

        def relu(s, x):
            dve.wait_ge(e["h_ps"].sem, e["h_ps"].at(s, x + 1))
            if x >= 2:
                dve.wait_ge(e["y_ps"].sem, e["y_ps"].at(s, x - 1))
            else:
                if begun(s - 1):
                    dve.wait_ge(e["y_ps"].sem, e["y_ps"].at(s - 1, NE + x - 1))
            for j in range(self.NA, NJ):
                bank, col = self.place(j)
                dve.tensor_scalar(w["h"][:, x % 2, j], c.S[:, x % 2, bank, col:col + L], w["b1"][:, x * NJ + j:x * NJ + j + 1],
                                  0.0, ALU.add, ALU.max).then_inc(e["hd"].sem, 1)

        def add(s, par, x):
            dve.wait_ge(e["y_ps"].sem, e["y_ps"].at(s, x + 1))
            if x == 0:
                dve.wait_ge(e["acc0"].sem, e["acc0"].at(s))
                dve.wait_ge(e["sc"].sem, e["sc"].at(s))
            else:
                dve.wait_ge(e["acc"].sem, e["acc"].at(s, x))
            if x == NE - 1:
                if begun(s - 1):
                    dve.wait_ge(e["x"].sem, e["x"].at(s - 1))
            src = w["acc0"] if x == 0 else w["acc"]
            dst = c.res if x == NE - 1 else w["acc"]
            for t in range(T):
                ins = dve.scalar_tensor_tensor(dst[:, t, :], c.O[:, x % 2, t * P:(t + 1) * P], w["sc"][:, par, t, x:x + 1],
                                               src[:, t, :], ALU.mult, ALU.add)
            ins.then_inc((e["res"] if x == NE - 1 else e["acc"]).sem, 1)

        def low(s, par):
            dve.wait_ge(e["zhi"].sem, e["zhi"].at(s))
            if begun(s - 2):
                dve.wait_ge(e["h_ps"].sem, e["h_ps"].at(s - 2))
            dve.tensor_tensor(c.lo[:, par], w["zT"][:, par], c.hi[:, par].bitcast(F32), ALU.subtract)\
               .then_inc(e["zlo"].sem, 1)

        def front(s, par):
            for part in range(6):
                gate(s, par, part)
            low(s, par)
            start_sum(s)

        def step(k, par, has_tail, has_front):
            for x in range(NE):
                if self.ND:
                    relu(k, x)
                if has_front and 2 <= x <= 6:
                    gate(k + 1, 1 - par, x - 2)
                if x > 0:
                    add(k, par, x - 1)
                if has_front and x == 6:
                    gate(k + 1, 1 - par, 5)
                if has_front and x == 7:
                    low(k + 1, 1 - par)
                if x == 1 and has_tail:
                    norm_write(c, e, dve, k - 1)
            add(k, par, NE - 1)
            norm_stats(c, e, dve, k)
            if has_front:
                start_sum(k + 1)

        pipeline(dve, front, step, lambda s, par: norm_write(c, e, dve, s))


def build(nc, x, out, d):
    with ExitStack() as ctx:
        c = Core(nc, ctx)
        sb = c.sb
        loads = {n: [] for n in ("consts", "l0", "x0", "x", "moe0", "l1", "l2", "moe2", "l3")}

        def load(group, dst, src):
            loads[group].append((dst, src))
            return dst

        def row(name):
            return d[name].rearrange("(o n) -> o n", o=1).broadcast_to((P, d[name].shape[0]))

        raw_spread = c.probs[:, 0:2].rearrange("p n b g l -> p (n b g l)")[:, 0:4 * G * P]
        load("consts", c.ident[:], d["ident"])
        load("consts", c.mask_f[:], d["masks"])
        load("consts", raw_spread, d["spread"])
        load("consts", c.one_rows[:], d["one_rows"])
        load("consts", c.trig[:], d["trig"])
        load("x0", c.X[:, 0:2], x[0:2].rearrange("b (t p) d -> p b t d", t=T))
        load("x", c.X[:, 2:B], x[2:B].rearrange("b (t p) d -> p b t d", t=T))

        work = c.probs[:].rearrange("p n b g l -> p (n b g l)")

        def carve(shapes, at=0):
            got = {}
            for name, shape in shapes.items():
                size = int(np.prod(shape))
                axes = " ".join("abc"[:len(shape)])
                view = work[:, at:at + size]
                got[name] = view.rearrange(f"p ({axes}) -> p {axes}", **dict(zip("abc", shape)))
                at += size
            assert at <= 6 * 2 * G * P
            return got

        w0 = dict(wqk_both=sb("wqk0", [P, 2, 2, P]), wv=sb("wv0", [P, P]), wo=sb("wo0", [P, P]),
                             bqk=sb("bqk0", [P, 2, 2]), bv=sb("bv0", [P, P]), bo=sb("bo0", [P, P]))
        w0["wqk"] = [w0["wqk_both"][:, 0], w0["wqk_both"][:, 1]]
        for dst, name in ((w0["wqk_both"], "wqk0"), (w0["wv"], "wv0"), (w0["wo"], "wo0"), (w0["bqk"], "bqk0")):
            load("l0", dst[:], d[name])
        load("l0", w0["bv"][:], row("bv0"))
        load("l0", w0["bo"][:], row("bo0"))
        w1 = dict(wq=sb("wq1", [P, 2, P]), uk=sb("uk1", [LAT, 2, P]), uv=sb("uv1", [LAT, P]),
                             dkv=sb("dkv1", [P, LAT]), wo=sb("wo1", [P, P]), bqk=sb("bqk1", [P, 2, 2]),
                             gamma=sb("gamma1", [P, LAT]), beta=sb("beta1", [P, LAT]),
                             lstats=sb("lstats", [P, T, 6]), lmv=sb("lmv", [P, T, 2]), lve=sb("lve", [P, T]),
                             lrstd=sb("lrstd", [P, T]), lnorm=sb("lnorm", [P, T, LAT]),
                             lscale=sb("lscale", [P, T, LAT]), lat=sb("lat", [P, T, LAT]), latT=sb("latT", [LAT, L]))
        w1["wqk"] = [w1["wq"], w1["uk"]]
        for dst, name in ((w1["wq"], "wq1"), (w1["uk"], "uk1"), (w1["uv"], "uv1"), (w1["dkv"], "dkv1"), (w1["wo"], "wo1")):
            load("l1", dst[:], d[name])
        load("l1", w1["gamma"][:], row("gamma1"))
        load("l1", w1["beta"][:], row("beta1"))
        wm = dict(wr=sb("wr", [P, P]), wk=sb("wk", [P, P]), wv=sb("wvm", [P, P]), mu=sb("mu", [P, 2]),
                             nu=sb("nu", [P, 2]),
                             **carve(dict(xTs=(2, L + 2), mixed=(2, L), xk=(2, L), xr=(2, L), relu=(L,), kact=(2, L),
                                          tanh=(2, L), gated=(L,))))
        for dst, name in ((wm["wr"], "wrm"), (wm["wk"], "wkm"), (wm["wv"], "wvm"), (wm["mu"], "mu")):
            load("l1", dst[:], d[name])
        w2 = dict(raw_qk=sb("raw_qk", [P, 2]), raw_v=sb("raw_v", [P, P]), sqk=sb("sqk", [P, 2]),
                             sv=sb("sv", [P, P]), neg_qk=sb("neg_qk", [P, 2]), neg_v=sb("neg_v", [P, P]))
        load("l2", w2["raw_qk"][:], d["sqk"])
        load("l2", w2["raw_v"][:], row("sv"))
        moe = {}
        for layer, hidden in ((0, d["w1_0"].shape[2]), (2, d["w1_2"].shape[2])):
            nj = hidden // P
            moe[layer] = m = dict(
                hidden=hidden, w1=sb(f"ew1_{layer}", [P, NE, hidden]), w2=sb(f"ew2_{layer}", [P, NE * nj, P]),
                b1=sb(f"eb1_{layer}", [P, NE * nj]), b2=sb(f"eb2_{layer}", [NE, P]), gate=sb(f"eg_{layer}", [P, NE]),
                bg=sb(f"ebg_{layer}", [P, NE]))
            load(f"moe{layer}", m["w1"][:], d[f"w1_{layer}"])
            load(f"moe{layer}", m["w2"][:], d[f"w2_{layer}"])
            load(f"moe{layer}", m["b1"][:], d[f"b1_{layer}"])
            load(f"moe{layer}", m["b2"][:], d[f"b2_{layer}"])
            load(f"moe{layer}", m["gate"][:], d[f"gate_{layer}"])
        load("moe0", moe[0]["bg"][:], row("bg_0"))
        shared = dict(iota=sb("iota", [P, NE]), w1_lo=sb("ew1_lo", [P, NE * d["w1_0"].shape[2]], F32R),
                      **carve(dict(h=(2, 4, L), zT=(2, L), z=(T, P), acc0=(T, P), acc=(T, P))), lg=sb("lg", [P, T, NE]), d=sb("d", [P, T, NE]),
                      ex=sb("ex", [P, T, NE]), pr=sb("pr", [P, T, NE]), v8=sb("v8", [P, T, NE]), f8=sb("f8", [P, T, NE]),
                      i8=sb("i8", [P, T, NE], mybir.dt.uint32), sc=sb("sc", [P, 2, T, NE]), oh=sb("oh", [P, 5, T, NE]),
                      top=sb("top", [P, T]), total=sb("total", [P, T]), inv=sb("inv", [P, T]), g=sb("g", [P, 8, T]),
                      wT=sb("wT", [NE, L]))
        for m in moe.values():
            for k, v in shared.items():
                m[k] = v
        load("consts", shared["iota"][:], row("iota"))
        w3 = dict(wq=sb("wq3", [P, P]), wkv=sb("wkv3", [P, 2 * P]), wo=sb("wo3", [P, P]), bq=sb("bq3", [P, 1]),
                             bkv=sb("bkv3", [P, 2 * P]), bo=sb("bo3", [P, P]), blocks=sb("blocks", [P, P]),
                             **carve(dict(xT=(2, L), q=(2, L), kv=(2, T, 2 * P), g=(P,), oT=(L,)), at=8 * L))
        for dst, name in ((w3["wq"], "wq3"), (w3["wkv"], "wkv3"), (w3["wo"], "wo3"), (w3["bq"], "bq3"), (w3["blocks"], "blocks")):
            load("l3", dst[:], d[name])
        load("l3", w3["bkv"][:], row("bkv3"))
        load("l3", w3["bo"][:], row("bo3"))
        w4 = dict(w1=sb("w1_3", [P, 4 * P]), w2=sb("w2_3", [P, 4, P]), b1=sb("b1_3", [P, 4]), b2=sb("b2_3", [P, P]),
                             xT=w3["xT"], h=shared["h"])
        for dst, name in ((w4["w1"], "w1_3"), (w4["w2"], "w2_3"), (w4["b1"], "b1_3")):
            load("l3", dst[:], d[name])
        load("l3", w4["b2"][:], row("b2_3"))

        loaded = {g: c.sem(f"loaded_{g}") for g in loads}
        made = c.made
        signs = c.sem("signs")
        phases = [("l0", Attention(c, "rope0", "rope", 0, w0)), ("moe0", Experts(c, "moe0", 0, moe[0])),
                  ("l1", Attention(c, "latent1", "latent", 1, w1)), ("l1", ChannelMix(c, "mix1", wm)),
                  ("l2", Attention(c, "sigmoid2", "sigmoid", None, w2)), ("moe2", Experts(c, "moe2", 2, moe[2])),
                  ("l3", LinearAttention(c, "linear3", w3)), ("l3", Mlp(c, "mlp3", w4, out))]
        N_MADE = 13

        phases[0][1].rest = loaded["x"], 16 * len(loads["x"])

        def enter(eng, n, done=B - 1):
            group, phase = phases[n]
            eng.wait_ge(loaded[group], 16 * len(loads[group]))
            if n == 0:
                eng.wait_ge(loaded["x0"], 16 * len(loads["x0"]))
                eng.wait_ge(loaded["consts"], 16 * len(loads["consts"]))
                eng.wait_ge(made, N_MADE)
            else:
                eng.wait_ge(phases[n - 1][1].e["x"].sem, phases[n - 1][1].e["x"].at(done))
            return phase

        block = ctx.enter_context(nc.Block())

        @block.sync
        def _(sp):
            for group in ("consts", "l0", "x0", "x", "moe0", "l1", "l2", "moe2", "l3"):
                for dst, src in loads[group]:
                    sp.dma_start(dst, src).then_inc(loaded[group], 16)
            phases[-1][1].sync(sp)

        @block.gpsimd
        def _(pool):
            for n in range(len(phases)):
                enter(pool, n, B - 2).pool(pool)

        @block.tensor
        def _(pe):
            for n in range(len(phases)):
                enter(pe, n).pe(pe)

        @block.scalar
        def _(act):
            for n in range(len(phases)):
                if n in (1, 5):
                    group, phase = phases[n]
                    phase.split_hi(act, phases[n - 1][1].e, loaded[group], 16 * len(loads[group]))
                enter(act, n, B - 2).act(act)

        @block.vector
        def _(dve):
            dve.memset(c.V[:], 0.0).then_inc(made, 1)
            dve.memset(c.M[:].bitcast(F32), 0.0).then_inc(made, 1)
            dve.memset(c.ones[:], 1.0).then_inc(made, 1)
            dve.memset(c.eps[:], EPS).then_inc(made, 1)
            dve.memset(c.minus_half[:], -0.5).then_inc(made, 1)
            dve.memset(w1["bqk"][:], 0.0).then_inc(made, 1)
            dve.memset(moe[2]["bg"][:], 0.0).then_inc(made, 1)
            dve.wait_ge(made, 1)
            dve.memset(c.V[:, :, :, :, HD:HD + 1].rearrange("p a t h o -> p (a t h) o"), 1.0).then_inc(made, 1)
            dve.wait_ge(loaded["consts"], 16 * len(loads["consts"]))
            dve.tensor_copy(c.ident_r[:], c.ident[:]).then_inc(made, 1)
            dve.tensor_copy(c.ident_b[:], c.ident[:]).then_inc(made, 1)
            dve.tensor_copy(c.mask_q[:], c.mask_f[:, 0]).then_inc(made, 1)
            dve.tensor_copy(c.mask_k[:], c.mask_f[:, 1]).then_inc(made, 1)
            dve.tensor_copy(c.spread[:].rearrange("p a g l -> p (a g l)"), raw_spread).then_inc(made, 1)
            for n in range(len(phases)):
                if n in (1, 5):
                    phases[n][1].split_lo(dve)
                phase = enter(dve, n)
                if n == 2:
                    dve.tensor_scalar(wm["nu"][:], wm["mu"][:], -1.0, 1.0, ALU.mult, ALU.add).then_inc(signs, 1)
                    dve.wait_ge(loaded["l2"], 16 * len(loads["l2"]))
                    dve.tensor_scalar(w2["neg_qk"][:], w2["raw_qk"][:], 0.0, None, ALU.is_lt).then_inc(signs, 1)
                    dve.tensor_scalar(w2["neg_v"][:], w2["raw_v"][:], 0.0, 0.5, ALU.is_lt, ALU.mult).then_inc(signs, 1)
                    dve.tensor_scalar(w2["sv"][:], w2["raw_v"][:], 0.0, 0.5, ALU.is_gt, ALU.mult).then_inc(signs, 1)
                    dve.wait_ge(signs, 4)
                    dve.scalar_tensor_tensor(w2["sqk"][:], w2["raw_qk"][:], 0.0, w2["neg_qk"][:], ALU.is_gt, ALU.subtract)\
                       .then_inc(signs, 1)
                    dve.tensor_tensor(w2["sv"][:], w2["sv"][:], w2["neg_v"][:], ALU.subtract).then_inc(signs, 1)
                    dve.wait_ge(signs, 6)
                phase.dve(dve)



def shape_constants():
    f = np.float32
    rows = np.arange(P)
    masks = np.stack([np.where(rows[None, :] > rows[:, None], MASKED, 0.0),
                      np.where(rows[:, None] > rows[None, :], MASKED, 0.0)], 1).astype(f)
    slots = {0: (0, 1), 1: (2,), 2: (0, 2), 3: (1,)}
    spread = np.zeros((P, 4, G, P), f)
    for kind, ss in slots.items():
        for g in range(G):
            for r in range(G):
                for slot in ss:
                    for i in range(HD):
                        spread[HD * (G * g + r) + i, kind, g, ROWS * r + HD * slot + i] = 1.0
    one_rows = ((rows % ROWS == MAX_HI) | (rows % ROWS == MAX_LO)).astype(f)[:, None]
    half = HD // 2
    pos = np.arange(L).astype(f)
    scale0 = np.power(f(1250), (f(2) * np.arange(half).astype(f) / f(HD))).astype(f)
    freq1 = (f(1.0) / np.power(f(10000.0), np.arange(half).astype(f) / f(half))).astype(f)
    trig = np.zeros((P, 2, 2, L), f)
    for layer, angle in enumerate(((pos[:, None] / scale0[None, :]).astype(f), (pos[:, None] * freq1[None, :]).astype(f))):
        for p in range(P):
            i = p % HD
            a = angle[:, i % half].astype(np.float64)
            trig[p, layer, 0] = np.cos(a)
            trig[p, layer, 1] = np.sin(a) * (-1.0 if i < half else 1.0)
    blocks = (rows[:, None] % 8 == rows[None, :] % 8).astype(f)
    return dict(ident=np.eye(P, dtype=f), masks=masks, spread=spread.reshape(P, -1), one_rows=one_rows, trig=trig,
                blocks=blocks, iota=np.arange(NE).astype(f))


def layout(inputs):
    a = {k: np.asarray(v) for k, v in inputs.items()}

    def halves_swapped(m):
        return m.reshape(*m.shape[:-1], NH, 2, HD // 2)[..., ::-1, :].reshape(m.shape)

    def with_swapped(m):
        return np.stack([m, halves_swapped(m)], -2)

    out = shape_constants()
    wq, wk = with_swapped(a["L0_attn_wq_w"]), with_swapped(a["L0_attn_wk_w"])
    out["wqk0"] = np.stack([wq, wk], 1)
    out["bqk0"] = np.stack([with_swapped(a["L0_attn_wq_b"]), with_swapped(a["L0_attn_wk_b"])], 0).transpose(2, 1, 0)
    out["wv0"], out["bv0"], out["wo0"], out["bo0"] = (a["L0_attn_" + n] for n in ("wv_w", "wv_b", "wo_w", "wo_b"))
    out["wq1"], out["uk1"] = with_swapped(a["L1_attn_W_q"]), with_swapped(a["L1_attn_W_uk"])
    out["uv1"], out["dkv1"], out["wo1"] = a["L1_attn_W_uv"], a["L1_attn_W_dkv"], a["L1_attn_W_o"]
    out["gamma1"], out["beta1"] = a["L1_attn_ln_gamma"], a["L1_attn_ln_beta"]
    for n in "rkv":
        out[f"w{n}m"] = a[f"L1_ffn_W_{n}"].T
    out["mu"] = np.stack([a["L1_ffn_mu_k"], a["L1_ffn_mu_r"]], 1)
    out["sqk"] = np.stack([a["L2_attn_bv_q"].reshape(P), a["L2_attn_bv_k"].reshape(P)], 1)
    out["sv"] = a["L2_attn_bv_v"].reshape(P)
    for layer, pre, names in ((0, "L0_ffn_", ("gate_w", "w1", "b1", "w2", "b2")), (2, "L2_ffn_", ("Wg", "W1", "b1", "W2", "b2"))):
        gate, w1, b1, w2, b2 = (a[pre + n] for n in names)
        out[f"gate_{layer}"], out[f"b2_{layer}"] = gate, b2
        out[f"w1_{layer}"] = w1.transpose(1, 0, 2)
        out[f"b1_{layer}"] = b1.reshape(-1, P).T
        out[f"w2_{layer}"] = w2.reshape(-1, P, P).transpose(1, 0, 2)
    out["bg_0"] = a["L0_ffn_gate_b"]
    wqkv = a["L3_attn_w_qkv"].T
    out["wq3"], out["wkv3"] = wqkv[:, :P], wqkv[:, P:]
    out["bq3"], out["bkv3"] = a["L3_attn_b_qkv"][:P, None], a["L3_attn_b_qkv"][P:]
    out["wo3"] = a["L3_attn_w_o"].T.reshape(8, P // 8, P).transpose(1, 0, 2).reshape(P, P)
    out["bo3"] = a["L3_attn_b_o"]
    out["w1_3"], out["b1_3"] = a["L3_ffn_W1"], a["L3_ffn_b1"].reshape(-1, P).T
    out["w2_3"], out["b2_3"] = a["L3_ffn_W2"].reshape(-1, P, P).transpose(1, 0, 2), a["L3_ffn_b2"]
    return {k: np.ascontiguousarray(v) for k, v in out.items()}


def kernel(**inputs):
    import concourse.bacc as bacc
    from concourse.bass_utils import run_bass_kernel_spmd

    nc = bacc.Bacc("TRN2", target_bir_lowering=False, num_devices=1)
    arrays = {"in_x": np.ascontiguousarray(inputs["L0_attn_x"])}
    arrays.update({"in_" + k: v for k, v in layout(inputs).items()})
    dram = {k[3:]: nc.dram_tensor(k, v.shape, mybir.dt.from_np(v.dtype), kind="ExternalInput").ap()
            for k, v in arrays.items()}
    x = dram.pop("x")
    out = nc.dram_tensor("out", x.shape, F32, kind="ExternalOutput").ap()
    build(nc, x, out, dram)
    return run_bass_kernel_spmd(nc, [arrays], core_ids=[0]).results[0]["out"]
```
